# Optimizing a Trainium2 kernel written in Bass

```python
import numpy as np
import jax
import jax.numpy as jnp

def _softmax(x, axis=-1):
    return jax.nn.softmax(x, axis=axis)

def _gelu(x):
    return jax.nn.gelu(x, approximate=True)

def _silu(x):
    return jax.nn.silu(x)

def _sigmoid(x):
    return jax.nn.sigmoid(x)

def _layernorm(x, axis=-1, eps=1e-05):
    m = jnp.mean(x, axis=axis, keepdims=True)
    v = jnp.var(x, axis=axis, keepdims=True)
    return (x - m) / jnp.sqrt(v + eps)

def _scatter_add(tgt, idx, src, axis=0):
    return tgt.at[idx].add(src)

def _segment_sum(src, seg, n):
    return jax.ops.segment_sum(src, seg, n)
kernel_name = 'mk_sandwich_d1_jaxref_r4_80e32a'

def setup_inputs(seed: int=0):
    np.random.seed(seed)
    _w = jnp.asarray

    def _L0_attn_setup():
        import jax, jax.numpy as jnp
        import numpy as np
        EPS = 1e-06

        def _l2_norm(t):
            inv = 1.0 / jnp.linalg.norm(t, ord=2, axis=-2)
            return t * inv[:, None, :]
        key = jax.random.key(seed)
        ks = jax.random.split(key, 8)
        B, C, D = (16, 512, 256)
        s = 1.0 / np.sqrt(D)
        return {'x': jax.random.normal(ks[0], (B, C, D), dtype=jnp.float32), 'Wq': jax.random.normal(ks[1], (D, D), dtype=jnp.float32) * s, 'bq': jnp.zeros((D,), dtype=jnp.float32), 'Wk': jax.random.normal(ks[2], (D, D), dtype=jnp.float32) * s, 'bk': jnp.zeros((D,), dtype=jnp.float32), 'Wv': jax.random.normal(ks[3], (D, D), dtype=jnp.float32) * s, 'bv': jnp.zeros((D,), dtype=jnp.float32), 'gamma': jax.random.normal(ks[4], (1,), dtype=jnp.float32) * 0.1}
    _L0_attn_in = _L0_attn_setup()

    def _L0_ffn_setup():
        import jax, jax.numpy as jnp
        import numpy as np
        B, S, D, E, H, DO = (4, 512, 256, 8, 1024, 256)
        TOP_K = 2
        LN_EPS = 1e-05
        key = jax.random.key(seed)
        ks = jax.random.split(key, 9)
        s = 0.02
        return {'x': jax.random.normal(ks[0], (B, S, D), dtype=jnp.float32), 'W1': jax.random.normal(ks[1], (E, D, H), dtype=jnp.float32) * s, 'b1': jnp.zeros((E, H), dtype=jnp.float32), 'W2': jax.random.normal(ks[2], (E, H, DO), dtype=jnp.float32) * s, 'b2': jnp.zeros((E, DO), dtype=jnp.float32), 'gate_W': jax.random.normal(ks[3], (D, E), dtype=jnp.float32) * s, 'shared_W': jax.random.normal(ks[4], (D, DO), dtype=jnp.float32) * s, 'shared_b': jnp.zeros((DO,), dtype=jnp.float32), 'gamma': jnp.ones((DO,), dtype=jnp.float32), 'beta': jnp.zeros((DO,), dtype=jnp.float32)}
    _L0_ffn_in = _L0_ffn_setup()
    _d = {'L0_attn_x': _L0_attn_in['x'], 'L0_attn_Wq': _L0_attn_in['Wq'], 'L0_attn_bq': _L0_attn_in['bq'], 'L0_attn_Wk': _L0_attn_in['Wk'], 'L0_attn_bk': _L0_attn_in['bk'], 'L0_attn_Wv': _L0_attn_in['Wv'], 'L0_attn_bv': _L0_attn_in['bv'], 'L0_attn_gamma': _L0_attn_in['gamma'], 'L0_ffn_W1': _L0_ffn_in['W1'], 'L0_ffn_b1': _L0_ffn_in['b1'], 'L0_ffn_W2': _L0_ffn_in['W2'], 'L0_ffn_b2': _L0_ffn_in['b2'], 'L0_ffn_gate_W': _L0_ffn_in['gate_W'], 'L0_ffn_shared_W': _L0_ffn_in['shared_W'], 'L0_ffn_shared_b': _L0_ffn_in['shared_b'], 'L0_ffn_gamma': _L0_ffn_in['gamma'], 'L0_ffn_beta': _L0_ffn_in['beta']}
    _x0 = _d['L0_attn_x']
    _d['L0_attn_x'] = jax.random.normal(jax.random.fold_in(jax.random.key(seed), 1), (8, 512, 256), dtype=_x0.dtype)
    del _x0
    return _d

def reference(L0_attn_x, L0_attn_Wq, L0_attn_bq, L0_attn_Wk, L0_attn_bk, L0_attn_Wv, L0_attn_bv, L0_attn_gamma, L0_ffn_W1, L0_ffn_b1, L0_ffn_W2, L0_ffn_b2, L0_ffn_gate_W, L0_ffn_shared_W, L0_ffn_shared_b, L0_ffn_gamma, L0_ffn_beta):

    def _L0_attn_ref(x, Wq, bq, Wk, bk, Wv, bv, gamma):
        import jax, jax.numpy as jnp
        import numpy as np
        EPS = 1e-06

        def _l2_norm(t):
            inv = 1.0 / jnp.linalg.norm(t, ord=2, axis=-2)
            return t * inv[:, None, :]
        B, C, L = x.shape
        Q = x @ Wq.T + bq
        K = x @ Wk.T + bk
        V = x @ Wv.T + bv
        Q = jnp.transpose(_l2_norm(Q), (0, 2, 1))
        K = _l2_norm(K)
        tailor_sum = 1.0 / (L + jnp.einsum('bnc,bc->bn', Q, jnp.sum(K, axis=-1) + EPS))
        value_sum = jnp.sum(V, axis=-1)[:, :, None]
        matrix = jnp.einsum('bmn,bcn->bmc', K, V)
        matrix_sum = value_sum + jnp.einsum('bnm,bmc->bcn', Q, matrix)
        weight_value = matrix_sum * tailor_sum[:, None, :]
        return x + gamma * weight_value

    def _L0_ffn_ref(x, W1, b1, W2, b2, gate_W, shared_W, shared_b, gamma, beta):
        import jax, jax.numpy as jnp
        import numpy as np
        B, S, D, E, H, DO = (4, 512, 256, 8, 1024, 256)
        TOP_K = 2
        LN_EPS = 1e-05
        d = x.shape[-1]
        flat = x.reshape(-1, d)
        n_exp = gate_W.shape[-1]
        probs = jax.nn.softmax(flat @ gate_W, axis=-1)
        topk_w, topk_idx = jax.lax.top_k(probs, TOP_K)
        topk_w = topk_w / topk_w.sum(axis=-1, keepdims=True)
        combine = (jax.nn.one_hot(topk_idx, n_exp, dtype=flat.dtype) * topk_w[..., None]).sum(axis=1)
        out = 0.5 * jax.nn.gelu(flat @ shared_W + shared_b, approximate=False)
        for e in range(n_exp):
            h = jax.nn.gelu(flat @ W1[e] + b1[e], approximate=False)
            out = out + combine[:, e:e + 1] * (h @ W2[e] + b2[e])
        mean = out.mean(axis=-1, keepdims=True)
        var = ((out - mean) ** 2).mean(axis=-1, keepdims=True)
        out = (out - mean) * jax.lax.rsqrt(var + LN_EPS) * gamma + beta
        return out.reshape(*x.shape[:-1], out.shape[-1])
    x = L0_attn_x
    x = x + _layernorm(_L0_attn_ref(_layernorm(x, axis=-1), L0_attn_Wq, L0_attn_bq, L0_attn_Wk, L0_attn_bk, L0_attn_Wv, L0_attn_bv, L0_attn_gamma), axis=-1)
    x = x + _layernorm(_L0_ffn_ref(_layernorm(x, axis=-1), L0_ffn_W1, L0_ffn_b1, L0_ffn_W2, L0_ffn_b2, L0_ffn_gate_W, L0_ffn_shared_W, L0_ffn_shared_b, L0_ffn_gamma, L0_ffn_beta), axis=-1)
    return x

_drawn_inputs = setup_inputs


def setup_inputs(seed=0):
    import zlib

    import numpy as np

    out = dict(_drawn_inputs(seed))
    spreads = {'L0_attn_bq': (0.0, 2.0),
     'L0_attn_bk': (0.0, 2.0),
     'L0_attn_bv': (0.0, 2.0),
     'L0_ffn_b1': (0.0, 0.1),
     'L0_ffn_b2': (0.0, 0.1),
     'L0_ffn_shared_b': (0.0, 0.1),
     'L0_ffn_gamma': (1.0, 0.2),
     'L0_ffn_beta': (0.0, 0.1)}
    factors = {'L0_attn_Wq': 34.271, 'L0_attn_Wk': 33.859, 'L0_attn_Wv': 36.575}
    for name, (base, spread) in spreads.items():
        noise = np.random.default_rng([zlib.crc32(name.encode()), seed]).standard_normal(out[name].shape)
        drawn = base * np.exp(spread * noise) if base else spread * noise
        out[name] = jnp.asarray(drawn.astype(out[name].dtype))
    for name, factor in factors.items():
        out[name] = (out[name] * factor).astype(out[name].dtype)
    return out
```

```python
from contextlib import ExitStack

import concourse.bass as bass
from concourse import mybir
from concourse.alu_op_type import AluOpType as ALU

ACT = mybir.ActivationFunctionType
AX = mybir.AxisListType
F32 = mybir.dt.float32
F16 = mybir.dt.float16
I32 = mybir.dt.int32
U32 = mybir.dt.uint32

P = 128
EPS_LN = 1e-5
EPS_TAILOR = 1e-6
SX = 2048.0
SG = 16384.0
TOP = 32768.0
EXP_MASK = 0x7F800000
EXP_FLIP = float(0x7F000000)
DCH = 5
SETUP_V = 23
EV1A, EV1, EV2A, EV = 4, 7, 9, 11
BT = 256
HALVES = BT // P


def sandwich(nc, x_in, Wq, bq, Wk, bk, Wv, bv, gam, W1, b1, W2, b2, gate_W, shared_W, shared_b, lng, lnb, out):
    B, C, D = x_in.shape
    E, _, H = W1.shape
    T = C // P
    NF = D // P
    NH = H // P
    TOK = B * C
    NG = TOK // P
    NB = 2 * TOK // BT + E - 1
    PAIRS = 2 * TOK
    SLOTS = NB * BT
    EARLY = 5
    WE = 2 * NF * H + 2 * NH * D

    def dram(name, shape, dt):
        return nc.dram_tensor(name, shape, dt).ap()

    xf_rows = dram("xf_rows", [TOK, 2 * D], F16)
    u_rows = dram("u_rows", [TOK, D], F32)
    table = dram("table", [SLOTS, 4], I32)
    y_rows = dram("y_rows", [PAIRS + SLOTS, D], F32)

    ctx = ExitStack()
    with ctx:
        def sb(name, shape, dt):
            return ctx.enter_context(nc.sbuf_tensor(name, shape, dt))

        def sem(name):
            return ctx.enter_context(nc.semaphore(name))

        W = sb("W", [P, E * WE], F16)
        X = sb("X", [P, NG, D], F32)
        stage = sb("stage", [P, 4096], F32)
        zone = sb("zone", [P, 4096], F32)
        b2b = sb("b2b", [P, E * D], F32)
        lngb = sb("lngb", [P, 2, D], F32)
        sbb = sb("sbb", [P, D], F32)
        ident = sb("ident", [P, P], F16)
        upper = sb("upper", [P, P], F16)
        ones32 = sb("ones32", [P, P], F32)
        row2048 = sb("row2048", [1, P], F16)
        logit = sb("logit", [P, NG, E], F32)
        b1T = sb("b1T", [P, E * NH], F32)
        eps = sb("eps", [P, 3], F32)
        gam_b = sb("gam_b", [P, 1], F32)
        bvc = sb("bvc", [P, NF], F32)
        a1 = sb("a1", [P, NG], F32)
        c2 = sb("c2", [P, NG], F32)
        st = sb("st", [P, 3, T, 6], F32)
        mv = sb("mv", [P, 3, T, 2], F32)
        sd = sb("sd", [P, 3, T], F32)
        cf = sb("cf", [P, 3, T], F32)
        c3 = sb("c3", [P, T], F32)
        kn = sb("kn", [P, 4], F32)
        rk = sb("rk", [P, 4], F32)
        ssq = sb("ssq", [P, 8], F32)
        bnd = sb("bnd", [P, 8], F32)
        scl = sb("scl", [P, 8], F32)
        inv = sb("inv", [P, 8], F32)
        der = sb("der", [P, 16], F32)
        essq = sb("essq", [P, 4], F32)
        etot = sb("etot", [P, 4], F32)
        ebnd = sb("ebnd", [P, 4], F32)
        escl = sb("escl", [P, 4], F32)
        einv = sb("einv", [P, 4], F32)
        tab = sb("tab", [P, 3, E], F32)
        slot_i = sb("slot_i", [P, 2, NG], I32)
        ej_i = sb("ej_i", [P, 48], I32)
        tb = sb("tb", [P, 2, HALVES, 4], I32)
        tsc = sb("tsc", [P, 2, HALVES, 4], I32)

        class Carver:
            def __init__(self, pools):
                self.pools = [list(p) for p in pools]

            def __call__(self, shape, dt):
                n = 1
                for s in shape[1:]:
                    n *= s
                words = (n * (2 if dt == F16 else 4) + 3) // 4
                words = (words + 7) // 8 * 8
                for p in self.pools:
                    if p[1] + words <= p[2]:
                        at = p[1]
                        p[1] += words
                        v = p[0][:, at:at + words]
                        if dt != F32:
                            v = v.bitcast(dt)
                        v = v[0:shape[0], 0:n]
                        if len(shape) == 3:
                            v = v.rearrange("p (a b) -> p a b", b=shape[2])
                        if len(shape) == 4:
                            v = v.rearrange("p (a b c) -> p a b c", b=shape[2], c=shape[3])
                        return v
                raise ValueError("no room")

        ones16 = sb("ones16", [P, P], F16)
        bsq = sb("bsq", [P, NH], F32)
        tinit = W[:, 0:NB * HALVES * 8].bitcast(I32).rearrange("p (g c) -> p g c", c=4)
        late = W[:, EARLY * WE:E * WE].bitcast(F32)
        at_ = Carver([(late, 0, (E - EARLY) * WE // 2), (zone, 0, 4096), (stage, 2048, 4096)])
        xhl = at_([P, T, 2, D], F16)
        xs = at_([P, T, D], F32)
        xT = at_([P, 2 * 2 * NF * C], F16)
        q32 = at_([P, 2, 2 * D], F32)
        qkh = at_([P, T, 2 * D], F16)
        qkl = at_([P, T, 2 * D], F16)
        z = at_([P, T, D], F32)
        xfhl = at_([P, T, 2, D], F16)
        xfT = at_([P, NF, 2, C], F16)
        wqkT = at_([P, NF, 2, 2 * D], F16)
        sqt = at_([P, 2 * D], F32)
        sqa = at_([P, 2 * D], F32)
        gk = at_([P, NF, D], F32)
        ghl = at_([P, 2, NF, D], F16)
        m32 = at_([P, NF, D], F32)
        mhl = at_([P, 2, NF, D], F16)
        wvs = at_([P, NF, 2, D], F16)
        sgs = at_([P, NF, 2, D + E], F16)
        bqk = at_([P, 2 * D], F32)
        u = at_([P, 2, D], F32)
        bvb = at_([P, NF, P], F32)
        rq = at_([P, D], F32)
        den = at_([P, D], F32)
        tg = at_([P, D], F32)
        r32 = at_([1, D], F32)
        rhl = at_([1, 2, D], F16)
        gate_n = at_([P, NF, E], F32)
        vsum = at_([P, NF], F32)
        ident32 = at_([P, P], F32)


        PS = [ctx.enter_context(nc.psum_tensor(f"bank{i}", [P, 512], F32)) for i in range(8)]
        TP = [PS[0], PS[1]]
        QB = [PS[2], PS[3]]
        GB, NB5, SB6, MB = PS[4], PS[5], PS[6], PS[7]

        x_loaded = sem("x_loaded")
        nat_in = sem("nat_in")
        gate_in = sem("gate_in")
        bias_in = sem("bias_in")
        b2_in = sem("b2_in")
        b1_in = sem("b1_in")
        wqk_in = sem("wqk_in")
        wv_in = sem("wv_in")
        sh_in = sem("sh_in")
        bvc_in = sem("bvc_in")
        c_eps = sem("c_eps")
        c_ones = sem("c_ones")
        c_row = sem("c_row")
        c_ident = sem("c_ident")
        c_upper = sem("c_upper")
        ssq_ready = sem("ssq_ready")
        ssq_sum = sem("ssq_sum")
        setup_v = sem("setup_v")
        setup_a = sem("setup_a")
        inv_ready = sem("inv_ready")
        wqk_t = sem("wqk_t")
        wqk_h = sem("wqk_h")
        wqk_l = sem("wqk_l")
        wv_h = sem("wv_h")
        wv_l = sem("wv_l")
        sg_h = sem("sg_h")
        sg_l = sem("sg_l")
        bvb_ready = sem("bvb_ready")
        vs_ps = sem("vs_ps")
        vsum_ready = sem("vsum_ready")
        b1_t = sem("b1_t")
        b1_ready = sem("b1_ready")
        bqk_ready = sem("bqk_ready")
        der_ready = sem("der_ready")
        w1_in = sem("w1_in")
        w2_in = sem("w2_in")
        e_ssq = sem("e_ssq")
        e_tot = sem("e_tot")
        e_v = sem("e_v")
        e_a = sem("e_a")
        e_tab = sem("e_tab")
        w_hi = sem("w_hi")
        w_lo = sem("w_lo")
        st1 = sem("st1")
        mv1 = sem("mv1")
        sd1 = sem("sd1")
        a1_ready = sem("a1_ready")
        c1_ready = sem("c1_ready")
        xs_ready = sem("xs_ready")
        xh_ready = sem("xh_ready")
        xl_ready = sem("xl_ready")
        t1 = sem("t1")
        xT_ready = sem("xT_ready")
        qk_ps = sem("qk_ps")
        q_ev = sem("q_ev")
        q_h = sem("q_h")
        sq_t = sem("sq_t")
        q_l = sem("q_l")
        sq_acc = sem("sq_acc")
        g_ps = sem("g_ps")
        nrm_ps = sem("nrm_ps")
        nsq = sem("nsq")
        rk_ready = sem("rk_ready")
        rq_ready = sem("rq_ready")
        gk_ready = sem("gk_ready")
        g32_ready = sem("g32_ready")
        gh_ready = sem("gh_ready")
        gl_ready = sem("gl_ready")
        sum_ps = sem("sum_ps")
        dchain = sem("dchain")
        tg_ready = sem("tg_ready")
        rh_ready = sem("rh_ready")
        rl_ready = sem("rl_ready")
        m_ps = sem("m_ps")
        m32_ready = sem("m32_ready")
        mh_ready = sem("mh_ready")
        ml_ready = sem("ml_ready")
        z_ps = sem("z_ps")
        z_mul = sem("z_mul")
        z_add = sem("z_add")
        st2 = sem("st2")
        mv2 = sem("mv2")
        sd2 = sem("sd2")
        r2_ready = sem("r2_ready")
        c2_ready = sem("c2_ready")
        x1_ready = sem("x1_ready")
        st3 = sem("st3")
        mv3 = sem("mv3")
        sd3 = sem("sd3")
        a3_ready = sem("a3_ready")
        c3_ready = sem("c3_ready")
        xf_ready = sem("xf_ready")
        xfh_ready = sem("xfh_ready")
        xfl_ready = sem("xfl_ready")
        xf_out = sem("xf_out")
        t3 = sem("t3")
        xfT_ready = sem("xfT_ready")
        sh_ps = sem("sh_ps")
        lg_ready = sem("lg_ready")
        u_ready = sem("u_ready")
        u_out = [sem("u_out0"), sem("u_out1")]
        zone_free = sem("zone_free")
        exp_max = sem("exp_max")
        exp_ready = sem("exp_ready")
        route = sem("route")
        both_ready = sem("both_ready")
        cnt_ps = sem("cnt_ps")
        slots_ready = sem("slots_ready")
        pay_ready = sem("pay_ready")
        table_init = sem("table_init")
        table_set = sem("table_set")
        ej_ready = sem("ej_ready")
        tb_in = [sem("tb_in0"), sem("tb_in1")]
        ts_in = [sem("ts_in0"), sem("ts_in1")]
        xg_in = [sem("xg_in0"), sem("xg_in1")]
        xt_ps = sem("xt_ps")
        xt_ready = sem("xt_ready")
        h_ps = sem("h_ps")
        h_act = sem("h_act")
        h_hi = sem("h_hi")
        h_lo = sem("h_lo")
        y_ps = sem("y_ps")
        y_ev = sem("y_ev")
        y_ready = sem("y_ready")
        y_out = [sem("y_out0"), sem("y_out1")]
        tu_in = sem("tu_in")
        tu_ready = sem("tu_ready")
        ty_in = [sem("ty_in0"), sem("ty_in1")]
        t_sum = sem("t_sum")
        t_o = sem("t_o")
        st4 = sem("st4")
        mv4 = sem("mv4")
        sd4 = sem("sd4")
        r4 = sem("r4")
        c4 = sem("c4")
        t_n = sem("t_n")
        t_g = sem("t_g")
        t_b = sem("t_b")
        st5 = sem("st5")
        mv5 = sem("mv5")
        sd5 = sem("sd5")
        r5 = sem("r5")
        c5 = sem("c5")
        t_f = sem("t_f")
        t_r = sem("t_r")
        t_out = sem("t_out")
        route_consts = sem("route_consts")
        iota_t = sem("iota_t")
        passed = sem("passed")

        def past(count):
            return max(count, 0) if isinstance(count, int) else count

        def settle(eng):
            eng.sem_inc(passed, 1)

        def chain(eng, name, start):
            count = [0]

            def link(ins):
                count[0] += 1
                ins.then_inc(name, 1)
                eng.wait_ge(name, start + count[0])
            link.count = count
            return link

        def at(ap, i):
            return ap[i] if isinstance(i, int) else ap[bass.ds(i, 1)].squeeze(0)

        def run_steps(eng, step):
            for s in range(3):
                step(s)
            with eng.Fori(3, B) as s:
                step(s)
            for s in range(B, B + 2):
                step(s)

        def parts(s):
            if not isinstance(s, int):
                return s, s - 1, s - 2, s - 3
            return tuple(b if 0 <= b < B else None for b in (s, s - 1, s - 2)) + (None,)

        def xTf(b, f):
            n = 2 * C
            return xT[:, bass.ds((b % 2) * (NF * n) + f * n, n)]

        def xTt(b, f, k, t):
            n = 2 * C
            return xT[:, bass.ds((b % 2) * (NF * n) + (f * n + k * C + t * P), P)]

        def Xt(b, t):
            return X[:, bass.ds(b * T + t, 1), :].rearrange("p a d -> p (a d)")

        def w1_part(e, k):
            return W[:, bass.ds(e * WE, 2 * NF * H)].rearrange("p (f k n) -> p f k n", f=NF, k=2)[:, :, k, :]

        def w2_part(e, k):
            return W[:, bass.ds(e * WE + 2 * NF * H, 2 * NH * D)].rearrange("p (j k n) -> p j k n", j=NH, k=2)[:, :, k, :]

        stage1 = stage[:, 0:2048].rearrange("p (f n) -> p f n", f=NF)

        def stage2(e):
            half = int(isinstance(e, int) and e >= EARLY)
            return stage[:, 2048 * half:2048 * half + 2048].rearrange("p (j n) -> p j n", j=NH)

        zr = Carver([(zone, 0, 4096)])
        probs = zr([P, NG, E], F32)
        iota_e = zr([P, NG, E], F32)
        tmp = zr([P, NG, E], F32)
        pick = [zr([P, NG, E], F32) for _ in range(2)]
        both = zr([P, E, NG], F16)
        carry = zr([P, E, NG], F32)
        cum = zr([P, E, NG], F32)
        rank = zr([P, E, NG], F32)
        pay = zr([P, NG, 2, 4], I32)
        jcmp = zr([P, NB, E], F32)
        ejf = zr([P, NB], F32)
        best = [zr([P, NG], F32) for _ in range(2)]
        red = zr([P, NG], F32)
        wsum = zr([P, NG], F32)
        nblk = zr([P, E], F32)
        nblk_i = zr([P, E], I32)
        bend = zr([P, E], F32)
        boff = zr([P, E], F32)
        one8 = zr([P, E], F32)

        zf = Carver([(zone, 0, 4096)])
        xg = zf([P, 2 * HALVES, 2 * D], F16)
        xbT = zf([P, 2 * NF * 2, BT], F16)
        h32 = zf([P, 2, 2 * BT], F32)
        y32 = zf([P, 2 * HALVES, D], F32)
        hhl = stage[:, :].bitcast(F16).rearrange("p (q j k n) -> p q j k n", q=2, j=NH, k=2)

        tail = Carver([(W[:, 0:4 * WE].bitcast(F32), 0, 4 * WE // 2)])
        tu = tail([P, NG, D], F32)
        ty = tail([P, 2 * T, 2, D], F32)
        to = tail([P, 2 * T, D], F32)

        def sync_rest(sp):
            sp.wait_ge(table_set, 16 * 2 * NG)
            sp.wait_ge(xf_out, 16 * B)
            tv = table.rearrange("(j h p) c -> j p h c", p=P, h=HALVES)

            def load_tb(j, q, n):
                sp.wait_ge(xg_in[q], 16 * HALVES * n)
                sp.dma_start(tb[:, q, :, :], at(tv, j)).then_inc(tb_in[q], 16)

            def load_ts(j, q, n):
                sp.wait_ge(y_out[q], 16 * HALVES * n)
                sp.dma_start(tsc[:, q, :, :], at(tv, j)).then_inc(ts_in[q], 16)

            load_tb(0, 0, 0)
            load_tb(1, 1, 0)
            load_ts(0, 0, 0)
            load_ts(1, 1, 0)
            load_tb(2, 0, 1)
            load_tb(3, 1, 1)
            load_ts(2, 0, 1)
            with sp.Fori(1, (NB - 3) // 2) as i:
                load_tb(2 * i + 2, 0, i + 1)
                load_ts(2 * i + 1, 1, i)
                load_tb(2 * i + 3, 1, i + 1)
                load_ts(2 * i + 2, 0, i + 1)
            i = (NB - 3) // 2
            load_tb(2 * i + 2, 0, i + 1)
            load_ts(2 * i + 1, 1, i)
            load_ts(2 * i + 2, 0, i + 1)
            sp.wait_ge(y_ps, NB)
            sp.wait_ge(y_out[0], 16 * HALVES * ((NB + 1) // 2))
            sp.wait_ge(y_out[1], 16 * HALVES * (NB // 2))
            sp.wait_ge(u_out[0], 16 * B * T // 2)
            sp.wait_ge(u_out[1], 16 * B * T // 2)
            ubv = u_rows.rearrange("(b p t) d -> b p (t d)", p=P, t=T)
            for b in range(B):
                sp.dma_start(tu[:, b * T:(b + 1) * T, :].rearrange("p t d -> p (t d)"), ubv[b]).then_inc(tu_in, 16)
            yv = y_rows[0:PAIRS, :].rearrange("(b p t k) d -> b p (t k d)", p=P, t=T, k=2)

            def load_y(b, q, n):
                sp.wait_ge(t_sum, past(b - 1))
                sp.dma_start(ty[:, q * T:(q + 1) * T, :, :].rearrange("p t k d -> p (t k d)"), at(yv, b)).then_inc(ty_in[q], 16)

            def store(b):
                sp.wait_ge(t_r, b + 1)
                sp.dma_start(at(outrows, b), tot_(b)).then_inc(t_out, 16)
            load_y(0, 0, 0)
            load_y(1, 1, 0)
            load_y(2, 0, 1)
            store(0)
            load_y(3, 1, 1)
            store(1)
            with sp.Fori(2, B // 2) as i:
                load_y(2 * i, 0, i)
                store(2 * i - 2)
                load_y(2 * i + 1, 1, i)
                store(2 * i - 1)
            store(B - 2)
            store(B - 1)
            sp.wait_ge(t_out, 16 * B)
            sp.wait_ge(ty_in[0], 16 * B // 2)

        def tot_(b):
            return to[:, bass.ds((b % 2) * T, T), :].rearrange("p t d -> p (t d)")

        def gpsimd_rest(g):
            g.wait_ge(zone_free, 1)
            g.iota(iota_e, [[0, NG], [1, E]], base=0, channel_multiplier=0, allow_small_or_imprecise_dtypes=True).then_inc(route_consts, 1)
            g.memset(carry, 1.0).then_inc(route_consts, 1)
            g.wait_ge(route_consts, 2)
            g.memset(carry[:, :, 0:1], 0.0).then_inc(route_consts, 1)
            g.iota(jcmp, [[1, NB], [0, E]], base=0, channel_multiplier=0, allow_small_or_imprecise_dtypes=True).then_inc(route_consts, 1)
            g.memset(one8, 1.0).then_inc(route_consts, 1)
            pv = pay.rearrange("p (b t) k c -> p b t k c", t=T)
            g.iota(pv[:, :, :, :, 0], [[C, B], [1, T], [0, 2]], base=0, channel_multiplier=T).then_inc(pay_ready, 1)
            g.iota(pv[:, :, :, :, 1], [[2 * C, B], [2, T], [1, 2]], base=0, channel_multiplier=2 * T).then_inc(pay_ready, 1)
            g.iota(pv[:, :, :, :, 3], [[0, B], [0, T], [0, 2]], base=0, channel_multiplier=0).then_inc(pay_ready, 1)
            g.wait_ge(pay_ready, 5)
            g.wait_ge(slots_ready, 1)
            g.wait_ge(table_init, 16)
            for t in range(NG):
                for k in range(2):
                    g.indirect_dma_start(out=table, out_offset=bass.IndirectOffsetOnAxis(ap=slot_i[:, k, t:t + 1], axis=0),
                                         in_=pay[:, t, k, :], in_offset=None).then_inc(table_set, 16)
            g.wait_ge(table_set, 16 * 2 * NG)
            g.wait_ge(xf_out, 16 * B)

            def gather(j, q, n):
                g.wait_ge(tb_in[q], 16 * (n + 1))
                g.wait_ge(xt_ps, past(j - 1))
                settle(g)
                for h in range(HALVES):
                    g.indirect_dma_start(out=xg[:, q * HALVES + h, :], out_offset=None, in_=xf_rows,
                                         in_offset=bass.IndirectOffsetOnAxis(ap=tb[:, q, h, 0:1], axis=0)).then_inc(xg_in[q], 16)

            def scatter(j, q):
                g.wait_ge(y_ready, HALVES * (j + 1))
                settle(g)
                for h in range(HALVES):
                    g.indirect_dma_start(out=y_rows, out_offset=bass.IndirectOffsetOnAxis(ap=tsc[:, q, h, 1:2], axis=0),
                                         in_=y32[:, q * HALVES + h, :], in_offset=None).then_inc(y_out[q], 16)
            gather(0, 0, 0)
            gather(1, 1, 0)
            gather(2, 0, 1)
            gather(3, 1, 1)
            scatter(0, 0)
            gather(4, 0, 2)
            scatter(1, 1)
            with g.Fori(2, (NB - 1) // 2) as i:
                gather(2 * i + 1, 1, i)
                scatter(2 * i - 2, 0)
                gather(2 * i + 2, 0, i + 1)
                scatter(2 * i - 1, 1)
            i = (NB - 1) // 2
            scatter(2 * i - 2, 0)
            scatter(2 * i - 1, 1)
            scatter(2 * i, 0)

            def add_pairs(b, q, n):
                g.wait_ge(ty_in[q], 16 * (n + 1))
                g.wait_ge(t_out, past(16 * (b - 1)))
                yq = ty[:, q * T:(q + 1) * T, :, :]
                g.tensor_tensor(to[:, q * T:(q + 1) * T, :], yq[:, :, 0, :], yq[:, :, 1, :], ALU.add).then_inc(t_sum, 1)

            def add_beta(b, q):
                g.wait_ge(t_g, b + 1)
                o = to[:, q * T:(q + 1) * T, :]
                g.tensor_tensor(o, o, lngb[:, 1, :].unsqueeze(1).broadcast_to([P, T, D]), ALU.add).then_inc(t_b, 1)

            def add_x(b, q):
                g.wait_ge(t_f, T * (b + 1))
                g.tensor_tensor(tot_(q), tot_(q), Xb(b), ALU.add).then_inc(t_r, 1)
            tail_steps(g, lambda b, q, n: add_pairs(b, q, n), lambda b, q, n: add_beta(b, q), lambda b, q, n: add_x(b, q))



        def Xb(b):
            return X[:, bass.ds(b * T, T), :].rearrange("p t d -> p (t d)")

        def tail_steps(eng, first, second, third):
            def one(b, q, n):
                first(b, q, n)
                if not (isinstance(b, int) and b == 0):
                    m = n if q else n - 1
                    second(b - 1, 1 - q, m)
                    third(b - 1, 1 - q, m)
            one(0, 0, 0)
            one(1, 1, 0)
            one(2, 0, 1)
            one(3, 1, 1)
            with eng.Fori(2, B // 2) as i:
                one(2 * i, 0, i)
                one(2 * i + 1, 1, i)
            second(B - 1, 1, B // 2 - 1)
            third(B - 1, 1, B // 2 - 1)

        def tensor_rest(pe):
            pe.wait_ge(both_ready, 1)
            pe.wait_ge(c_upper, 2)
            bm = both.rearrange("p e g -> p (e g)")
            pe.matmul(NB5[:, 0:NG * E], upper[:, :], bm, start=True, stop=True)
            pe.matmul(NB5[:, NG * E:2 * NG * E], ones16[:, :], bm, start=True, stop=True).then_inc(cnt_ps, 1)
            pe.wait_ge(w_lo, 2 * E)
            pe.wait_ge(w_hi, 2 * E)
            pe.wait_ge(ej_ready, 1)

            def turn(j, q, n):
                pe.wait_ge(xg_in[q], 16 * HALVES * (n + 1))
                pe.wait_ge(xt_ready, j)
                for f in range(NF):
                    for k in range(2):
                        for h in range(HALVES):
                            at0 = ((f * 2 + k) * HALVES + h) * P
                            mm = pe.transpose(PS[4][:, :].bitcast(F16)[:, at0:at0 + P],
                                              xg[:, q * HALVES + h, k * D + f * P:k * D + (f + 1) * P], ident[:, :])
                mm.then_inc(xt_ps, 1)

            def up(j, q):
                e = pe.value_load(ej_i[0:1, bass.ds(j, 1)], min_val=0, max_val=E - 1)
                pe.wait_ge(xt_ready, j + 1)
                for m in range(NH // 2):
                    pe.wait_ge(h_act, past(NH * (j - 1) + 2 * m + 2))
                    for r in range(2):
                        for f in range(NF):
                            ws = [W[:, bass.ds(e * WE + (f * 2 + k) * H + (2 * m + r) * P, P)] for k in range(2)]
                            xs_ = [xbT[:, (q * NF + f) * 2 + k, :] for k in range(2)]
                            mm = mm3(pe, PS[m][:, r * BT:(r + 1) * BT], ws[0], ws[1], xs_[0], xs_[1], f == 0, f == NF - 1)
                    mm.then_inc(h_ps, 1)

            def down(j, q):
                e = pe.value_load(ej_i[0:1, bass.ds(j, 1)], min_val=0, max_val=E - 1)
                pe.wait_ge(y_ev, past(j - 1))
                for h in range(HALVES):
                    for m in range(NH):
                        if h == 0 and m % 2 == 0:
                            pe.wait_ge(h_lo, NH // 2 * j + m // 2 + 1)
                        ws = [W[:, bass.ds(e * WE + 2 * NF * H + (m * 2 + k) * D, D)] for k in range(2)]
                        mm = mm3(pe, PS[5 + q][:, h * D:(h + 1) * D], hhl[:, q, m, 0, h * P:(h + 1) * P], hhl[:, q, m, 1, h * P:(h + 1) * P],
                                 ws[0], ws[1], m == 0, m == NH - 1)
                mm.then_inc(y_ps, 1)
            turn(0, 0, 0)
            up(0, 0)
            turn(1, 1, 0)
            up(1, 1)
            turn(2, 0, 1)
            down(0, 0)
            up(2, 0)
            turn(3, 1, 1)
            down(1, 1)
            with pe.Fori(2, (NB - 1) // 2) as i:
                up(2 * i - 1, 1)
                turn(2 * i, 0, i)
                down(2 * i - 2, 0)
                up(2 * i, 0)
                turn(2 * i + 1, 1, i)
                down(2 * i - 1, 1)
            i = (NB - 1) // 2
            up(2 * i - 1, 1)
            turn(2 * i, 0, i)
            down(2 * i - 2, 0)
            up(2 * i, 0)
            down(2 * i - 1, 1)
            down(2 * i, 0)

        def scalar_rest(a):
            a.wait_ge(exp_max, 1)
            a.activation(probs, probs, ACT.Exp).then_inc(exp_ready, 1)
            a.wait_ge(ej_ready, 1)
            a.preload_act_table(ACT.Gelu)

            def gelu(j, q):
                e = a.value_load(ej_i[0:1, bass.ds(j, 1)], min_val=0, max_val=E - 1)
                for m in range(NH // 2):
                    a.wait_ge(h_ps, NH // 2 * j + m + 1)
                    a.wait_ge(h_lo, past(NH // 2 * j + m - 1))
                    for r in range(2):
                        settle(a)
                        a.activation(h32[:, m % 2, r * BT:(r + 1) * BT], PS[m][:, r * BT:(r + 1) * BT], ACT.Gelu,
                                     bias=b1T[:, bass.ds(e * NH + 2 * m + r, 1)], scale=tab[:, 0, bass.ds(e, 1)]).then_inc(h_act, 1)
            gelu(0, 0)
            with a.Fori(1, NB) as j:
                gelu(j, 0)
            a.wait_ge(tu_in, 16 * B)
            for b in range(B):
                a.activation(tu[:, b * T:(b + 1) * T, :], tu[:, b * T:(b + 1) * T, :], ACT.Gelu).then_inc(tu_ready, 1)
            a.preload_act_table(ACT.Sqrt)

            def sd_(which, name, need, b):
                a.wait_ge(need, T * (b + 1))
                settle(a)
                a.activation(sd[:, which, :], mv[:, which, :, 1], ACT.Sqrt, bias=eps[:, 2:3]).then_inc(name, 1)

            def final(b, q):
                a.wait_ge(c5, 2 * (b + 1))
                settle(a)
                for t in range(T):
                    o = to[:, q * T + t, :]
                    a.activation(o, o, ACT.Identity, bias=c3[:, t:t + 1], scale=cf[:, 1, t:t + 1]).then_inc(t_f, 1)
            tail_steps(a, lambda b, q, n: sd_(0, sd4, mv4, b), lambda b, q, n: sd_(1, sd5, mv5, b), lambda b, q, n: final(b, q))

        def vector_rest(v):
            def wide(x):
                return x.unsqueeze(2).broadcast_to([P, NG, E])
            link = chain(v, route, 0)
            link(v.tensor_reduce(red, logit[:, :, :], AX.X, ALU.max))
            v.wait_ge(zone_free, 1)
            v.tensor_tensor(probs, logit[:, :, :], wide(red), ALU.subtract).then_inc(exp_max, 1)
            v.wait_ge(exp_ready, 1)
            link(v.tensor_reduce(red, probs, AX.X, ALU.add))
            link(v.reciprocal(red, red))
            link(v.tensor_tensor(probs, probs, wide(red), ALU.mult))
            v.wait_ge(route_consts, 5)
            for k in range(2):
                link(v.tensor_reduce(best[k], probs, AX.X, ALU.max))
                link(v.tensor_tensor(tmp, probs, wide(best[k]), ALU.is_equal))
                link(v.scalar_tensor_tensor(tmp, tmp, -float(E), iota_e, ALU.mult, ALU.add))
                link(v.tensor_reduce(red, tmp, AX.X, ALU.min))
                link(v.tensor_tensor(pick[k], tmp, wide(red), ALU.is_equal))
                if k == 0:
                    link(v.scalar_tensor_tensor(probs, pick[0], -2.0, probs, ALU.mult, ALU.add))
            link(v.tensor_tensor(both.rearrange("p e g -> p g e"), pick[0], pick[1], ALU.add))
            v.tensor_copy(nblk, one8).then_inc(both_ready, 1)
            link(v.tensor_tensor(wsum, best[0], best[1], ALU.add))
            link(v.reciprocal(wsum, wsum))
            v.wait_ge(pay_ready, 3)
            for k in range(2):
                v.tensor_tensor(pay[:, :, k, 2].bitcast(F32), best[k], wsum, ALU.mult).then_inc(pay_ready, 1)
            v.wait_ge(cnt_ps, 1)
            before = NB5[:, 0:NG * E]
            count = NB5[:, NG * E:2 * NG * E]
            flat = lambda x: x.rearrange("p e g -> p (e g)")
            link(v.tensor_tensor_scan(flat(cum), flat(carry), count, 0.0, ALU.mult, ALU.add))
            link(v.tensor_tensor(flat(rank), flat(cum), count, ALU.subtract))
            link(v.tensor_tensor(flat(rank), flat(rank), before, ALU.add))
            link(v.tensor_scalar(nblk_i, cum[:, :, NG - 1], float(BT - 1), None, ALU.add))
            link(v.tensor_scalar(nblk_i, nblk_i, BT.bit_length() - 1, None, ALU.arith_shift_right))
            link(v.tensor_copy(nblk, nblk_i))
            link(v.tensor_tensor_scan(bend, one8, nblk, 0.0, ALU.mult, ALU.add))
            link(v.tensor_tensor(boff, bend, nblk, ALU.subtract))
            link(v.tensor_scalar(boff, boff, float(BT), None, ALU.mult))
            link(v.tensor_tensor(rank, rank, boff.unsqueeze(2).broadcast_to([P, E, NG]), ALU.add))
            for k in range(2):
                link(v.tensor_tensor(tmp, pick[k], rank.rearrange("p e g -> p g e"), ALU.mult))
                link(v.tensor_reduce(red, tmp, AX.X, ALU.add))
                link(v.tensor_copy(slot_i[:, k, :], red))
            v.wait_ge(route, link.count[0])
            v.tensor_copy(nblk, one8).then_inc(slots_ready, 1)
            link(v.tensor_tensor(jcmp, jcmp, bend.unsqueeze(1).broadcast_to([P, NB, E]), ALU.is_ge))
            link(v.tensor_reduce(ejf, jcmp, AX.X, ALU.add))
            link(v.tensor_scalar(ej_i[:, 0:NB], ejf, float(E - 1), None, ALU.min))
            v.wait_ge(route, link.count[0])
            v.tensor_copy(nblk, one8).then_inc(ej_ready, 1)

            def split(j, q):
                e = v.value_load(ej_i[0:1, bass.ds(j, 1)], min_val=0, max_val=E - 1)
                v.wait_ge(y_ps, past(j - 1))
                for m in range(NH // 2):
                    v.wait_ge(h_act, NH * j + 2 * m + 2)
                    o = [hhl[:, q, 2 * m:2 * m + 2, k, :] for k in range(2)]
                    src = h32[:, m % 2, :].rearrange("p (r n) -> p r n", r=2)
                    v.tensor_scalar(o[0], src, tab[:, 1, bass.ds(e, 1)], None, ALU.mult).then_inc(h_hi, 1)
                    v.wait_ge(h_hi, NH // 2 * j + m + 1)
                    v.scalar_tensor_tensor(o[1], src, tab[:, 1, bass.ds(e, 1)], o[0], ALU.mult, ALU.subtract).then_inc(h_lo, 1)

            def turned_block(j, q):
                v.wait_ge(xt_ps, j + 1)
                v.wait_ge(h_ps, past(NH // 2 * (j - 1)))
                v.tensor_copy(xbT[:, q * NF * 2:(q + 1) * NF * 2, :].rearrange("p a n -> p (a n)"), PS[4][:, :].bitcast(F16)).then_inc(xt_ready, 1)

            def result(j, q, n):
                e = v.value_load(ej_i[0:1, bass.ds(j, 1)], min_val=0, max_val=E - 1)
                v.wait_ge(y_ps, j + 1)
                v.wait_ge(y_out[q], 16 * HALVES * n)
                yq = y32[:, q * HALVES:(q + 1) * HALVES, :]
                v.scalar_tensor_tensor(yq, PS[5 + q][:, :].rearrange("p (h d) -> p h d", h=HALVES), tab[:, 2, bass.ds(e, 1)],
                                       b2b[:, bass.ds(e * D, D)].unsqueeze(1).broadcast_to([P, HALVES, D]), ALU.mult, ALU.add).then_inc(y_ev, 1)
                v.wait_ge(y_ev, j + 1)
                v.wait_ge(ts_in[q], 16 * (n + 1))
                for h in range(HALVES):
                    v.tensor_scalar(y32[:, q * HALVES + h, :], y32[:, q * HALVES + h, :], tsc[:, q, h, 2:3].bitcast(F32), None,
                                    ALU.mult).then_inc(y_ready, 1)
            turned_block(0, 0)
            split(0, 0)
            turned_block(1, 1)
            split(1, 1)
            turned_block(2, 0)
            result(0, 0, 0)
            split(2, 0)
            turned_block(3, 1)
            result(1, 1, 0)
            with v.Fori(2, (NB - 1) // 2) as i:
                split(2 * i - 1, 1)
                turned_block(2 * i, 0)
                result(2 * i - 2, 0, i - 1)
                split(2 * i, 0)
                turned_block(2 * i + 1, 1)
                result(2 * i - 1, 1, i - 1)
            i = (NB - 1) // 2
            split(2 * i - 1, 1)
            turned_block(2 * i, 0)
            result(2 * i - 2, 0, i - 1)
            split(2 * i, 0)
            result(2 * i - 1, 1, i - 1)
            result(2 * i, 0, i)

            def tstats(which, b, q, src_ready, st_name, mv_name):
                for n, c in src_ready:
                    v.wait_ge(n, past(c))
                settle(v)
                for t in range(T):
                    v.bn_stats(st[:, which, t, :], to[:, q * T + t, :]).then_inc(st_name, 1)
                for t in range(T):
                    v.wait_ge(st_name, T * b + t + 1)
                    settle(v)
                    v.bn_aggr(mv[:, which, t, :], st[:, which, t, :]).then_inc(mv_name, 1)

            def first(b, q, n):
                v.wait_ge(tu_ready, B)
                v.wait_ge(t_sum, b + 1)
                o = to[:, q * T:(q + 1) * T, :]
                v.scalar_tensor_tensor(o, tu[:, bass.ds(b * T, T), :], 0.5, o, ALU.mult, ALU.add).then_inc(t_o, 1)
                tstats(0, b, q, [(t_o, b + 1)], st4, mv4)
                v.wait_ge(sd4, b + 1)
                v.reciprocal(cf[:, 0, :], sd[:, 0, :]).then_inc(r4, 1)
                v.wait_ge(r4, b + 1)
                v.scalar_tensor_tensor(cf[:, 2, :], mv[:, 0, :, 0], -1.0, cf[:, 0, :], ALU.mult, ALU.mult).then_inc(c4, 1)
                v.wait_ge(c4, b + 1)
                for t in range(T):
                    v.tensor_scalar(to[:, q * T + t, :], to[:, q * T + t, :], cf[:, 0, t:t + 1], cf[:, 2, t:t + 1], ALU.mult, ALU.add).then_inc(t_n, 1)
                v.wait_ge(t_n, T * (b + 1))
                v.tensor_tensor(o, o, lngb[:, 0, :].unsqueeze(1).broadcast_to([P, T, D]), ALU.mult).then_inc(t_g, 1)

            def second(b, q, n):
                tstats(1, b, q, [(t_b, b + 1)], st5, mv5)
                v.wait_ge(sd5, b + 1)
                v.wait_ge(t_f, T * b)
                v.reciprocal(cf[:, 1, :], sd[:, 1, :]).then_inc(r5, 1)
                v.wait_ge(r5, b + 1)
                v.scalar_tensor_tensor(c3[:, :], mv[:, 1, :, 0], -1.0, cf[:, 1, :], ALU.mult, ALU.mult).then_inc(c5, 1)
                v.wait_ge(c5, 2 * b + 1)
                v.tensor_tensor(c3[:, :], c3[:, :], c2[:, bass.ds(b * T, T)], ALU.add).then_inc(c5, 1)
            tail_steps(v, first, second, lambda b, q, n: None)

        block = ctx.enter_context(nc.Block())
        xrows = x_in.rearrange("b (p t) d -> b p (t d)", t=T)
        outrows = out.rearrange("b (p t) d -> b p (t d)", t=T)
        xfv = xf_rows.rearrange("(b p t) d -> b p (t d)", p=P, t=T)
        uv = u_rows.rearrange("(b p t) d -> b p t d", p=P, t=T)
        wqk_n = z[:, :, :]
        wv_n = m32[:, :, :]
        sh_n = gk[:, :, :]
        b1_n = u[0:E * NH, 0, 0:P]

        def mm3(pe, o, lh, ll, rh, rl, first, last):
            pe.matmul(o, lh, rh, start=first, stop=False)
            pe.matmul(o, lh, rl, start=False, stop=False)
            return pe.matmul(o, ll, rh, start=False, stop=last)

        @block.sync
        def _(sp):
            def load_x(b):
                sp.wait_ge(x_loaded, 16 * b)
                sp.dma_start(X[:, b * T:(b + 1) * T, :].rearrange("p t d -> p (t d)"), xrows[b]).then_inc(x_loaded, 16)

            def load_w1(e):
                sp.wait_ge(w_hi, 2 * e)
                sp.wait_ge(w_lo, 2 * e)
                sp.dma_start(stage[:, 0:2048].rearrange("p (f n) -> p f n", f=NF),
                             at(W1, e).rearrange("(f p) n -> p f n", p=P)).then_inc(w1_in, 16)

            def load_w2(e, half):
                if not half:
                    sp.wait_ge(w_hi, 2 * e + 1)
                    sp.wait_ge(w_lo, 2 * e + 1)
                sp.dma_start(stage[:, 2048 * half:2048 * half + 2048].rearrange("p (j n) -> p j n", j=NH),
                             at(W2, e).rearrange("(j p) n -> p j n", p=P)).then_inc(w2_in, 16)

            def store_u(b, t):
                sp.wait_ge(u_ready, T * b + t + 1)
                sp.dma_start(at(uv, b)[:, t, :], u[:, t % 2, :]).then_inc(u_out[t % 2], 16)

            def store_xf(b):
                sp.wait_ge(xfh_ready, b + 1)
                sp.wait_ge(xfl_ready, b + 1)
                sp.dma_start(at(xfv, b),
                             xfhl.rearrange("p t k d -> p (t k d)")).then_inc(xf_out, 16)

            load_x(0)
            with nc.allow_non_contiguous_dma(reason="512 single words, once"):
                for j in range(NF):
                    sp.dma_start(wqk_n[:, j, :], Wq[j * P:(j + 1) * P, :]).then_inc(wqk_in, 16)
                    sp.dma_start(wqk_n[:, NF + j, :], Wk[j * P:(j + 1) * P, :]).then_inc(wqk_in, 16)
                sp.dma_start(bqk[:, 0:D], bq.partition_broadcast(P)).then_inc(bias_in, 16)
                sp.dma_start(bqk[:, D:2 * D], bk.partition_broadcast(P)).then_inc(bias_in, 16)
                sp.dma_start(wv_n, Wv.rearrange("(j p) i -> p j i", p=P)).then_inc(wv_in, 16)
                sp.dma_start(bvc[:, :], bv.rearrange("(j p) -> p j", p=P)).then_inc(bvc_in, 16)
                sp.dma_start(gam_b[:, :], gam.partition_broadcast(P)).then_inc(bvc_in, 16)
                load_x(1)
                sp.dma_start(sh_n, shared_W.rearrange("(j p) i -> p j i", p=P)).then_inc(sh_in, 16)
                sp.dma_start(gate_n, gate_W.rearrange("(j p) i -> p j i", p=P)).then_inc(sh_in, 16)
                sp.dma_start(b1_n, b1.rearrange("e (j p) -> (e j) p", p=P)).then_inc(b1_in, 16)
                sp.dma_start(sbb[:, :], shared_b.partition_broadcast(P)).then_inc(b2_in, 16)
                sp.dma_start(lngb[:, 0, :], lng.partition_broadcast(P)).then_inc(b2_in, 16)
                sp.dma_start(lngb[:, 1, :], lnb.partition_broadcast(P)).then_inc(b2_in, 16)
                sp.dma_start(b2b[:, :], b2.rearrange("e d -> (e d)").partition_broadcast(P)).then_inc(b2_in, 16)
            for b in range(2, B):
                load_x(b)
            sp.wait_ge(iota_t, 2)
            sp.dma_start(table.rearrange("(g p) c -> p g c", p=P), tinit[:, :, :]).then_inc(table_init, 16)

            def step(s):
                if not isinstance(s, int):
                    load_w1(s - 3)
                if not isinstance(s, int) or 2 <= s:
                    store_xf(s - 2)
                    for t in range(T):
                        store_u(s - 2, t)
                if not isinstance(s, int):
                    load_w2(s - 3, 0)
            run_steps(sp, step)
            sp.wait_ge(zone_free, 1)
            for e in range(EARLY, E):
                load_w1(e)
                load_w2(e, 1)
            sync_rest(sp)

        @block.gpsimd
        def _(g):
            g.memset(eps[:, 0:1], EPS_LN / SX / SX).then_inc(c_eps, 1)
            g.memset(eps[:, 1:2], EPS_LN * SX * SX).then_inc(c_eps, 1)
            g.memset(eps[:, 2:3], EPS_LN).then_inc(c_eps, 1)
            g.memset(ident32, 0.0).then_inc(c_ident, 1)
            g.memset(ident[:, :], 0.0).then_inc(c_ident, 1)
            g.memset(upper[:, :], 1.0).then_inc(c_upper, 1)
            g.memset(ones32[:, :], 1.0).then_inc(c_ones, 1)
            g.memset(ones16[:, :], 1.0).then_inc(c_ones, 1)
            g.memset(row2048[:, :], SX).then_inc(c_row, 1)
            g.wait_ge(c_ident, 2)
            for i in (ident32, ident[:, :]):
                g.affine_select(out=i, in_=i, compare_op=ALU.not_equal, fill=1.0, base=0,
                                pattern=[[-1, P]], channel_multiplier=1).then_inc(c_ident, 1)
            g.wait_ge(c_upper, 1)
            g.affine_select(out=upper[:, :], in_=upper[:, :], compare_op=ALU.is_gt, fill=0.0, base=0,
                            pattern=[[1, P]], channel_multiplier=-1).then_inc(c_upper, 1)
            g.iota(tinit[:, :, 0:4], [[0, NB * HALVES], [0, 4]], base=0, channel_multiplier=0).then_inc(iota_t, 1)
            g.wait_ge(iota_t, 1)
            g.iota(tinit[:, :, 1], [[P, NB * HALVES]], base=PAIRS, channel_multiplier=1).then_inc(iota_t, 1)

            def low(o, x, h, name, o_free, waits):
                for n, v in waits:
                    g.wait_ge(n, past(v))
                g.tensor_tensor(o, x, h, ALU.subtract).then_inc(name, 1)

            def e_reduce(n, lo, hi):
                g.wait_ge(e_ssq, n)
                settle(g)
                g.partition_all_reduce(etot[:, lo:hi], essq[:, lo:hi], P, bass.bass_isa.ReduceOp.add).then_inc(e_tot, 1)

            def attend(b1_, b2_, prep):
                if b1_ is not None:
                    g.wait_ge(xh_ready, b1_ + 1)
                    g.wait_ge(t1, 2 * b1_)
                    g.tensor_tensor(xhl[:, :, 1, :], xs, xhl[:, :, 0, :], ALU.subtract).then_inc(xl_ready, 1)
                if prep is not None:
                    e_reduce(3 * prep + 2, 0, 2)
                if b1_ is not None:
                    for t in range(T):
                        g.wait_ge(q_h, T * b1_ + t + 1)
                        g.wait_ge(nrm_ps, b1_)
                        g.tensor_tensor(qkl[:, t, :], q32[:, t % 2, :], qkh[:, t, :], ALU.subtract).then_inc(q_l, 1)
                        if t:
                            g.wait_ge(sq_t, T * b1_ + t + 1)
                            g.wait_ge(sq_acc, past((T - 1) * b1_ + t - 1))
                            g.tensor_tensor(sqa, sqa, sqt, ALU.add).then_inc(sq_acc, 1)
                if prep is not None:
                    e_reduce(3 * prep + 3, 2, 3)
                if b2_ is not None:
                    g.wait_ge(xfh_ready, b2_ + 1)
                    g.wait_ge(t3, 2 * b2_)
                    g.wait_ge(xf_out, 16 * b2_)
                    g.tensor_tensor(xfhl[:, :, 1, :], z, xfhl[:, :, 0, :], ALU.subtract).then_inc(xfl_ready, 1)

            def step(s):
                b1_, b2_, b3_, e = parts(s)
                attend(b1_, b2_, e)
            run_steps(g, step)
            for e in range(EARLY, E):
                e_reduce(3 * e + 2, 0, 2)
                e_reduce(3 * e + 3, 2, 3)
            gpsimd_rest(g)

        @block.tensor
        def _(pe):
            pe.wait_ge(c_ones, 2)
            pe.wait_ge(ssq_ready, 6)
            pe.matmul(NB5[:, 0:6], ones32[:, :], ssq[:, 0:6], start=True, stop=True)
            pe.wait_ge(bvc_in, 32)
            pe.matmul(NB5[:, 8:8 + NF], ones32[:, :], bvc[:, :], start=True, stop=True).then_inc(ssq_sum, 1)
            pe.wait_ge(c_ident, 4)
            for i in range(NF):
                for j in range(2 * NF):
                    mm = pe.transpose(TP[i][:, j * P:(j + 1) * P], wqk_n[:, j, i * P:(i + 1) * P], ident32)
            mm.then_inc(wqk_t, 1)
            for i in range(NF):
                for l in range(NF):
                    mm = pe.matmul(SB6[:, i:i + 1], wv_n[:, l, i * P:(i + 1) * P], ones32[:, 0:1], start=(l == 0), stop=(l == NF - 1))
            mm.then_inc(vs_ps, 1)
            pe.wait_ge(b1_in, 16)
            pe.transpose(QB[0][:, 0:E * NH], b1_n, ident32[0:E * NH, 0:E * NH]).then_inc(b1_t, 1)

            def transposes(b, src, name, f, extra):
                for t in range(T):
                    for k in range(2):
                        mm = pe.transpose(TP[f][:, :].bitcast(F16)[:, (k * T + t) * P:(k * T + t + 1) * P],
                                          src[:, t, k, f * P:(f + 1) * P], ident[:, :])
                mm.then_inc(name, 1)

            def scores(b):
                pe.wait_ge(q_l, T * (b + 1))
                pe.wait_ge(z_mul, 2 * b)
                for lt in range(NF):
                    cs = slice(D + lt * P, D + (lt + 1) * P)
                    for t in range(T):
                        mm = mm3(pe, GB[:, lt * D:(lt + 1) * D], qkh[:, t, cs], qkl[:, t, cs], qkh[:, t, 0:D], qkl[:, t, 0:D],
                                 t == 0, t == T - 1)
                mm.then_inc(g_ps, 1)
                pe.wait_ge(sq_acc, past((T - 1) * (b + 1)))
                pe.wait_ge(dchain, DCH * b)
                pe.matmul(NB5[:, 0:D], ones32[:, :], sqa[:, 0:D], start=True, stop=True)
                for t in range(T):
                    pe.matmul(NB5[:, D:2 * D], ones16[:, :], qkh[:, t, 0:D], start=(t == 0), stop=False)
                    pe.matmul(NB5[:, D:2 * D], ones16[:, :], qkl[:, t, 0:D], start=False, stop=(t == T - 1))
                for lt in range(NF):
                    mm = pe.matmul(SB6[:, lt:lt + 1], sqa[:, D + lt * P:D + (lt + 1) * P], ones32[:, 0:1], start=True, stop=True)
                mm.then_inc(nrm_ps, 1)

            def shared(b):
                pe.wait_ge(xfh_ready, b + 1)
                pe.wait_ge(xfl_ready, b + 1)
                for f in range(NF):
                    transposes(b, xfhl, t3, f, None)
                pe.wait_ge(xfT_ready, 2 * (b + 1))
                for t in range(T):
                    pe.wait_ge(u_ready, past(T * b + t - 1))
                    pe.wait_ge(lg_ready, past(T * b + t - 1))
                    for f in range(NF):
                        ts = slice(t * P, (t + 1) * P)
                        mm = mm3(pe, TP[t % 2][:, 0:D + E], xfT[:, f, 0, ts], xfT[:, f, 1, ts], sgs[:, f, 0, :], sgs[:, f, 1, :],
                                 f == 0, f == NF - 1)
                    mm.then_inc(sh_ps, 1)

            def turn_x(b):
                pe.wait_ge(xl_ready, b + 1)
                pe.wait_ge(u_ready, past(T * (b - 1)))
                pe.wait_ge(lg_ready, past(T * (b - 1)))
                for f in range(NF):
                    transposes(b, xhl, t1, f, None)

            def sums(b):
                pe.wait_ge(g32_ready, b + 1)
                pe.wait_ge(nsq, 2 * (b + 1))
                for l in range(NF):
                    pe.matmul(SB6[:, 0:D], ones32[:, :], gk[:, l, :], start=(l == 0), stop=(l == NF - 1))
                for l in range(NF):
                    mm = pe.matmul(SB6[:, D:2 * D], bvb[:, l, :], gk[:, l, :], start=(l == 0), stop=(l == NF - 1))
                mm.then_inc(sum_ps, 1)

            def project(b, t):
                if t == 0:
                    pe.wait_ge(xT_ready, 2 * (b + 1))
                pe.wait_ge(q_ev, past(T * b + t - 1))
                for f in range(NF):
                    mm = mm3(pe, QB[t % 2][:, :], xTt(b, f, 0, t), xTt(b, f, 1, t), wqkT[:, f, 0, :], wqkT[:, f, 1, :], f == 0, f == NF - 1)
                mm.then_inc(qk_ps, 1)

            def mix(b):
                pe.wait_ge(gh_ready, b + 1)
                pe.wait_ge(gl_ready, b + 1)
                for i in range(NF):
                    for l in range(NF):
                        mm = mm3(pe, MB[:, i * D:(i + 1) * D], wvs[:, l, 0, i * P:(i + 1) * P], wvs[:, l, 1, i * P:(i + 1) * P],
                                 ghl[:, 0, l, :], ghl[:, 1, l, :], l == 0, l == NF - 1)
                mm.then_inc(m_ps, 1)

            def values(b):
                pe.wait_ge(mh_ready, b + 1)
                pe.wait_ge(ml_ready, b + 1)
                pe.wait_ge(rl_ready, b + 1)
                for t in range(T):
                    o = (GB, MB)[t // 2][:, (t % 2) * D:(t % 2 + 1) * D]
                    for f in range(NF):
                        mm3(pe, o, xTt(b, f, 0, t), xTt(b, f, 1, t), mhl[:, 0, f, :], mhl[:, 1, f, :], f == 0, False)
                    for k in range(2):
                        mm = pe.matmul(o, row2048[:, :], rhl[:, k, :], start=False, stop=(k == 1))
                    if t % 2:
                        mm.then_inc(z_ps, 1)

            def step(s):
                b1_, b2_, b3_, e = parts(s)
                if b2_ is not None:
                    scores(b2_)
                if b3_ is not None:
                    shared(b3_)
                if b1_ is not None:
                    turn_x(b1_)
                if b2_ is not None:
                    sums(b2_)
                if b1_ is not None:
                    project(b1_, 0)
                    project(b1_, 1)
                if b2_ is not None:
                    mix(b2_)
                if b1_ is not None:
                    project(b1_, 2)
                    project(b1_, 3)
                if b2_ is not None:
                    values(b2_)
            pe.wait_ge(wqk_h, NF)
            pe.wait_ge(wqk_l, NF)
            pe.wait_ge(b1_ready, 1)
            pe.wait_ge(wv_l, 1)
            pe.wait_ge(sg_l, 2)
            pe.wait_ge(setup_v, SETUP_V)
            run_steps(pe, step)
            tensor_rest(pe)

        @block.scalar
        def _(a):
            a.wait_ge(c_eps, 3)
            a.preload_act_table(ACT.Sqrt)
            link = chain(a, ssq_ready, 0)
            dump = xfhl.rearrange("p t k d -> p (t k d)")
            a.wait_ge(wqk_in, 64)
            link(a.activation(dump[:, 0:4 * D], wqk_n.rearrange("p j i -> p (j i)"), ACT.Square, accum_out=ssq[:, 0:1]))
            a.wait_ge(bias_in, 32)
            link(a.activation(dump[:, 0:2 * D], bqk, ACT.Square, accum_out=ssq[:, 5:6]))
            a.wait_ge(wv_in, 16)
            link(a.activation(dump[:, 0:2 * D], wv_n.rearrange("p j i -> p (j i)"), ACT.Square, accum_out=ssq[:, 1:2]))
            a.wait_ge(bvc_in, 32)
            link(a.activation(dump[:, 0:NF], bvc[:, :], ACT.Square, accum_out=ssq[:, 4:5]))
            a.wait_ge(sh_in, 32)
            link(a.activation(dump[:, 0:2 * D], sh_n.rearrange("p j i -> p (j i)"), ACT.Square, accum_out=ssq[:, 2:3]))
            link(a.activation(dump[:, 0:NF * E], gate_n.rearrange("p j i -> p (j i)"), ACT.Square, accum_out=ssq[:, 3:4]))
            a.wait_ge(setup_v, 10)
            a.activation(scl[:, 0:6], bnd[:, 0:6], ACT.Sqrt, scale=TOP * TOP).then_inc(setup_a, 1)
            a.wait_ge(setup_v, 11)
            a.wait_ge(wqk_t, 1)
            for i in range(NF):
                a.activation(wqkT[:, i, 0, :], TP[i][:, :], ACT.Copy, scale=scl[:, 0:1]).then_inc(wqk_h, 1)
            a.activation(wvs[:, :, 0, :], wv_n, ACT.Copy, scale=scl[:, 2:3]).then_inc(wv_h, 1)
            a.activation(sgs[:, :, 0, 0:D], sh_n, ACT.Copy, scale=scl[:, 4:5]).then_inc(sg_h, 1)
            a.activation(sgs[:, :, 0, D:D + E], gate_n, ACT.Copy, scale=scl[:, 5:6]).then_inc(sg_h, 1)
            a.wait_ge(b1_t, 1)
            a.activation(b1T[:, :], QB[0][:, 0:E * NH], ACT.Copy).then_inc(b1_ready, 1)
            a.wait_ge(b1_ready, 1)

            def spread(which, name, need, epsc, scale):
                a.wait_ge(need[0], need[1])
                settle(a)
                a.activation(sd[:, which, :], mv[:, which, :, 1], ACT.Sqrt, bias=eps[:, epsc:epsc + 1], scale=scale).then_inc(name, 1)

            def e_squares(e, which):
                if which == 0:
                    a.wait_ge(w1_in, 16 * (e + 1))
                    a.wait_ge(e_tab, 2 * e)
                    settle(a)
                    a.activation(w1_part(e, 0), stage1, ACT.Square, accum_out=essq[:, 0:1]).then_inc(e_ssq, 1)
                    settle(a)
                    a.activation(bsq[:, :], b1T[:, bass.ds(e * NH, NH)], ACT.Square, accum_out=essq[:, 1:2]).then_inc(e_ssq, 1)
                    a.wait_ge(e_ssq, 3 * e + 2)
                else:
                    a.wait_ge(w2_in, 16 * (e + 1))
                    settle(a)
                    a.activation(w2_part(e, 0), stage2(e), ACT.Square, accum_out=essq[:, 2:3]).then_inc(e_ssq, 1)
                    a.wait_ge(e_ssq, 3 * e + 3)

            def e_scales(e, which):
                lo, hi = ((0, 2), (2, 3))[which]
                a.wait_ge(e_v, EV * e + (EV1A, EV2A)[which])
                settle(a)
                a.activation(escl[:, lo:hi], ebnd[:, lo:hi], ACT.Sqrt, scale=TOP * TOP).then_inc(e_a, 1)

            def e_high(e, which):
                a.wait_ge(e_tab, 2 * e + which + 1)
                if which == 0:
                    settle(a)
                    a.activation(w1_part(e, 0), stage1, ACT.Copy, scale=escl[:, 0:1]).then_inc(w_hi, 1)
                else:
                    settle(a)
                    a.activation(w2_part(e, 0), stage2(e), ACT.Copy, scale=escl[:, 2:3]).then_inc(w_hi, 1)

            def norms(b):
                a.wait_ge(nrm_ps, b + 1)
                a.wait_ge(rk_ready, b)
                settle(a)
                a.activation(kn[:, 0:NF], SB6[:, 0:NF], ACT.Sqrt).then_inc(nsq, 1)
                a.wait_ge(dchain, DCH * b)
                settle(a)
                a.activation(rq, NB5[:, 0:D], ACT.Sqrt).then_inc(nsq, 1)

            def turned(b, dst, bank, t_name, name, extra):
                a.wait_ge(t_name, 2 * b + 1)
                for n, v in extra:
                    a.wait_ge(n, past(v))
                settle(a)
                a.activation(dst, TP[0][:, :].bitcast(F16), ACT.Copy).then_inc(name, 1)

            def g_copy(b):
                a.wait_ge(rk_ready, b + 1)
                a.wait_ge(sum_ps, b)
                a.wait_ge(gl_ready, b)
                for l in range(NF):
                    settle(a)
                    a.activation(gk[:, l, :], GB[:, l * D:(l + 1) * D], ACT.Copy, scale=rk[:, l:l + 1]).then_inc(gk_ready, 1)

            def g_high(b):
                a.wait_ge(g32_ready, b + 1)
                a.wait_ge(m_ps, b)
                settle(a)
                a.activation(ghl[:, 0, :, :], gk, ACT.Copy).then_inc(gh_ready, 1)

            def x_high(b):
                a.wait_ge(xs_ready, T * (b + 1))
                a.wait_ge(t1, 2 * b)
                settle(a)
                a.activation(xhl[:, :, 0, :], xs, ACT.Copy).then_inc(xh_ready, 1)

            def q_high(b, t):
                a.wait_ge(q_ev, T * b + t + 1)
                a.wait_ge(nrm_ps, b)
                settle(a)
                a.activation(qkh[:, t, :], q32[:, t % 2, :], ACT.Copy).then_inc(q_h, 1)
                if t:
                    a.wait_ge(sq_acc, past((T - 1) * b + t - 1))
                settle(a)
                a.activation(sqt if t else sqa, q32[:, t % 2, :], ACT.Square).then_inc(sq_t, 1)

            def m_high(b):
                a.wait_ge(m_ps, b + 1)
                a.wait_ge(ml_ready, b)
                for i in range(NF):
                    settle(a)
                    a.activation(m32[:, i, :], MB[:, i * D:(i + 1) * D], ACT.Identity, bias=vsum[:, i:i + 1], scale=der[:, 1:2]).then_inc(m32_ready, 1)
                a.wait_ge(m32_ready, 2 * (b + 1))
                a.wait_ge(z_ps, 2 * b)
                settle(a)
                a.activation(mhl[:, 0, :, :], m32, ACT.Copy).then_inc(mh_ready, 1)

            def xf_high(b):
                a.wait_ge(xf_ready, T * (b + 1))
                a.wait_ge(t3, 2 * b)
                a.wait_ge(xf_out, 16 * b)
                settle(a)
                a.activation(xfhl[:, :, 0, :], z, ACT.Copy).then_inc(xfh_ready, 1)

            def step(s):
                b1_, b2_, b3_, e = parts(s)
                if b2_ is not None:
                    norms(b2_)
                if b3_ is not None:
                    turned(b3_, xfT[:, 0, :, :].rearrange("p k c -> p (k c)"), 0, t3, xfT_ready, [(sh_ps, T * b3_)])
                if b1_ is not None:
                    spread(0, sd1, (mv1, T * (b1_ + 1)), 0, 1.0 / SX / SX)
                if b2_ is not None:
                    g_copy(b2_)
                if b1_ is not None:
                    x_high(b1_)
                if b2_ is not None:
                    g_high(b2_)
                if e is not None:
                    e_squares(e, 0)
                if e is not None:
                    e_scales(e, 0)
                if b1_ is not None:
                    turned(b1_, xTf(b1_, 0), 0, t1, xT_ready, [(z_ps, 2 * (b1_ - 1))])
                if e is not None:
                    e_high(e, 0)
                if b1_ is not None:
                    q_high(b1_, 0)
                    q_high(b1_, 1)
                if b2_ is not None:
                    m_high(b2_)
                if b1_ is not None:
                    q_high(b1_, 2)
                    q_high(b1_, 3)
                if e is not None:
                    e_squares(e, 1)
                    e_scales(e, 1)
                if b2_ is not None:
                    spread(1, sd2, (mv2, T * (b2_ + 1)), 1, 1.0)
                if e is not None:
                    e_high(e, 1)
                if b2_ is not None:
                    spread(2, sd3, (mv3, T * (b2_ + 1)), 0, 1.0 / SX / SX)
                    xf_high(b2_)
            a.wait_ge(table_init, 16)
            run_steps(a, step)
            a.wait_ge(zone_free, 1)
            for e in range(EARLY, E):
                for which in range(2):
                    e_squares(e, which)
                    e_scales(e, which)
                    e_high(e, which)
            scalar_rest(a)

        @block.vector
        def _(v):
            link = chain(v, setup_v, 0)
            v.wait_ge(ssq_ready, 6)
            v.wait_ge(ssq_sum, 1)
            tot = NB5
            link(v.tensor_copy(bnd[:, 0:1], tot[:, 0:1]))
            link(v.scalar_tensor_tensor(bnd[:, 1:2], tot[:, 0:1], float(D), ssq[:, 5:6], ALU.mult, ALU.add))
            link(v.tensor_scalar(bnd[:, 1:2], bnd[:, 1:2], 2.0, None, ALU.mult))
            link(v.tensor_copy(bnd[:, 2:3], tot[:, 1:2]))
            link(v.tensor_copy(bnd[:, 3:4], tot[:, 1:2]))
            link(v.scalar_tensor_tensor(bnd[:, 3:4], tot[:, 4:5], 1.0, bnd[:, 3:4], ALU.mult, ALU.add))
            link(v.tensor_scalar(bnd[:, 3:4], bnd[:, 3:4], 8.0 * D, None, ALU.mult))
            link(v.tensor_copy(bnd[:, 4:6], tot[:, 2:4]))
            link(v.tensor_scalar(bnd[:, 0:6], bnd[:, 0:6], 1e-24, None, ALU.max))
            link(v.reciprocal(bnd[:, 0:6], bnd[:, 0:6]))
            v.wait_ge(setup_a, 1)
            link(v.tensor_scalar(scl[:, 0:6].bitcast(I32), scl[:, 0:6].bitcast(I32), EXP_MASK, None, ALU.bitwise_and))
            link(v.tensor_scalar(inv[:, 0:6].bitcast(I32), scl[:, 0:6].bitcast(I32), -1.0, EXP_FLIP, ALU.mult, ALU.add))
            link(v.scalar_tensor_tensor(der[:, 0:1], scl[:, 1:2], 1.0 / SX, inv[:, 0:1], ALU.mult, ALU.mult))
            link(v.scalar_tensor_tensor(der[:, 1:2], scl[:, 3:4], 1.0 / SG, inv[:, 2:3], ALU.mult, ALU.mult))
            v.wait_ge(bvc_in, 32)
            link(v.tensor_tensor(der[:, 2:3], gam_b[:, :], inv[:, 3:4], ALU.mult))
            link(v.tensor_scalar(der[:, 3:5], inv[:, 4:6], 1.0 / SX, None, ALU.mult))
            link(v.tensor_scalar(der[:, 5:6], scl[:, 3:4], 1.0 / SG, None, ALU.mult))
            link(v.tensor_copy(der[:, 7:8], tot[:, 8:9]))
            link(v.scalar_tensor_tensor(der[:, 6:7], tot[:, 9:10], 1.0, der[:, 7:8], ALU.mult, ALU.add))
            link(v.tensor_tensor(der[:, 6:7], der[:, 6:7], scl[:, 3:4], ALU.mult))
            v.wait_ge(vs_ps, 1)
            link(v.tensor_scalar(vsum, SB6[:, 0:NF], scl[:, 3:4], None, ALU.mult))
            link(v.tensor_scalar(bqk, bqk, scl[:, 1:2], None, ALU.mult))
            link(v.tensor_copy(bvb, bvc[:, :].unsqueeze(2).broadcast_to([P, NF, P])))
            assert link.count[0] == SETUP_V
            for i in range(NF):
                v.wait_ge(wqk_h, i + 1)
                v.scalar_tensor_tensor(wqkT[:, i, 1, :], TP[i][:, :], scl[:, 0:1], wqkT[:, i, 0, :], ALU.mult, ALU.subtract).then_inc(wqk_l, 1)
            v.wait_ge(wv_h, 1)
            v.scalar_tensor_tensor(wvs[:, :, 1, :], wv_n, scl[:, 2:3], wvs[:, :, 0, :], ALU.mult, ALU.subtract).then_inc(wv_l, 1)
            v.wait_ge(sg_h, 2)
            v.scalar_tensor_tensor(sgs[:, :, 1, 0:D], sh_n, scl[:, 4:5], sgs[:, :, 0, 0:D], ALU.mult, ALU.subtract).then_inc(sg_l, 1)
            v.scalar_tensor_tensor(sgs[:, :, 1, D:D + E], gate_n, scl[:, 5:6], sgs[:, :, 0, D:D + E], ALU.mult, ALU.subtract).then_inc(sg_l, 1)
            v.wait_ge(b2_in, 64)

            def bank_tiles(bank):
                return bank[:, :].rearrange("p (t d) -> p t d", d=D)

            def stats(which, b, src, src_ready, st_name, mv_name):
                for t in range(T):
                    for n, c in src_ready(t):
                        v.wait_ge(n, past(c))
                    settle(v)
                    v.bn_stats(st[:, which, t, :], src(t)).then_inc(st_name, 1)
                for t in range(T):
                    v.wait_ge(st_name, T * b + t + 1)
                    settle(v)
                    v.bn_aggr(mv[:, which, t, :], st[:, which, t, :]).then_inc(mv_name, 1)

            def enter(b):
                stats(0, b, lambda t: Xt(b, t), lambda t: [(x_loaded, 16 * (b + 1))], st1, mv1)
                v.wait_ge(sd1, b + 1)
                v.reciprocal(a1[:, bass.ds(b * T, T)], sd[:, 0, :]).then_inc(a1_ready, 1)
                v.wait_ge(a1_ready, b + 1)
                v.scalar_tensor_tensor(cf[:, 0, :], mv[:, 0, :, 0], -1.0, a1[:, bass.ds(b * T, T)], ALU.mult, ALU.mult).then_inc(c1_ready, 1)
                v.wait_ge(c1_ready, b + 1)
                v.wait_ge(xh_ready, b)
                v.wait_ge(xl_ready, b)
                for t in range(T):
                    v.tensor_scalar(xs[:, t, :], Xt(b, t), a1[:, bass.ds(b * T + t, 1)], cf[:, 0, t:t + 1], ALU.mult, ALU.add).then_inc(xs_ready, 1)

            def turned(b, dst, t_name, name, extra):
                v.wait_ge(t_name, 2 * b + 2)
                for n, c in extra:
                    v.wait_ge(n, past(c))
                v.tensor_copy(dst, TP[1][:, :].bitcast(F16)).then_inc(name, 1)

            def norms(b):
                v.wait_ge(nsq, 2 * (b + 1))
                v.wait_ge(gk_ready, 2 * b)
                v.reciprocal(rk[:, 0:NF], kn[:, 0:NF]).then_inc(rk_ready, 1)
                v.reciprocal(rq, rq).then_inc(rq_ready, 1)

            def cosines(b):
                v.wait_ge(gk_ready, 2 * (b + 1))
                v.wait_ge(rq_ready, b + 1)
                v.scalar_tensor_tensor(gk, gk, SG, rq.unsqueeze(1).broadcast_to([P, NF, D]), ALU.mult, ALU.mult).then_inc(g32_ready, 1)
                v.wait_ge(gh_ready, b + 1)
                v.wait_ge(m_ps, b)
                v.tensor_tensor(ghl[:, 1, :, :], gk, ghl[:, 0, :, :], ALU.subtract).then_inc(gl_ready, 1)

            def tailor(b):
                link = chain(v, dchain, DCH * b)
                v.wait_ge(sum_ps, b + 1)
                link(v.scalar_tensor_tensor(den, NB5[:, D:2 * D], EPS_TAILOR, rq, ALU.mult, ALU.mult))
                link(v.scalar_tensor_tensor(den, SB6[:, 0:D], 1.0 / SG, den, ALU.mult, ALU.add))
                link(v.tensor_scalar(r32, SB6[0:1, D:2 * D], der[0:1, 5:6], der[0:1, 6:7], ALU.mult, ALU.add))
                link(v.tensor_scalar(den, den, float(D), None, ALU.add))
                link(v.reciprocal(den, den))
                assert link.count[0] == DCH
                v.tensor_scalar(tg, den, der[:, 2:3], None, ALU.mult).then_inc(tg_ready, 1)
                v.wait_ge(z_ps, 2 * b)
                v.tensor_copy(rhl[:, 0, :], r32).then_inc(rh_ready, 1)
                v.wait_ge(rh_ready, b + 1)
                v.tensor_tensor(rhl[:, 1, :], r32, rhl[:, 0, :], ALU.subtract).then_inc(rl_ready, 1)

            def q_out(b, t):
                v.wait_ge(qk_ps, T * b + t + 1)
                v.wait_ge(q_l, past(T * b + t - 1))
                v.wait_ge(sq_t, past(T * b + t - 1))
                v.scalar_tensor_tensor(q32[:, t % 2, :], QB[t % 2][:, :], der[:, 0:1], bqk, ALU.mult, ALU.add).then_inc(q_ev, 1)

            def m_low(b):
                v.wait_ge(mh_ready, b + 1)
                v.wait_ge(z_ps, 2 * b)
                v.tensor_tensor(mhl[:, 1, :, :], m32, mhl[:, 0, :, :], ALU.subtract).then_inc(ml_ready, 1)

            def leave(b):
                v.wait_ge(xfh_ready, b)
                v.wait_ge(xfl_ready, b)
                v.wait_ge(tg_ready, b + 1)
                for h in range(2):
                    v.wait_ge(z_ps, 2 * b + h + 1)
                    v.tensor_tensor(z[:, 2 * h:2 * h + 2, :], bank_tiles((GB, MB)[h]), tg.unsqueeze(1).broadcast_to([P, 2, D]),
                                    ALU.mult).then_inc(z_mul, 1)
                for t in range(T):
                    v.wait_ge(z_mul, 2 * b + t // 2 + 1)
                    v.scalar_tensor_tensor(z[:, t, :], Xt(b, t), a1[:, bass.ds(b * T + t, 1)], z[:, t, :], ALU.mult, ALU.add).then_inc(z_add, 1)
                stats(1, b, lambda t: z[:, t, :], lambda t: [(z_add, T * b + t + 1)], st2, mv2)
                v.wait_ge(sd2, b + 1)
                v.reciprocal(cf[:, 1, :], sd[:, 1, :]).then_inc(r2_ready, 1)
                v.wait_ge(r2_ready, b + 1)
                v.scalar_tensor_tensor(c2[:, bass.ds(b * T, T)], mv[:, 1, :, 0], -1.0, cf[:, 1, :], ALU.mult, ALU.mult).then_inc(c2_ready, 1)
                for t in range(T):
                    v.scalar_tensor_tensor(Xt(b, t), z[:, t, :], cf[:, 1, t:t + 1], Xt(b, t), ALU.mult, ALU.add).then_inc(x1_ready, 1)
                stats(2, b, lambda t: Xt(b, t), lambda t: [(x1_ready, T * b + t + 1)], st3, mv3)
                v.wait_ge(sd3, b + 1)
                v.reciprocal(cf[:, 2, :], sd[:, 2, :]).then_inc(a3_ready, 1)
                v.wait_ge(a3_ready, b + 1)
                v.scalar_tensor_tensor(c3[:, :], mv[:, 2, :, 0], -1.0, cf[:, 2, :], ALU.mult, ALU.mult).then_inc(c3_ready, 1)
                v.wait_ge(c3_ready, b + 1)
                for t in range(T):
                    v.tensor_scalar(z[:, t, :], Xt(b, t), cf[:, 2, t:t + 1], c3[:, t:t + 1], ALU.mult, ALU.add).then_inc(xf_ready, 1)

            def shared_out(b):
                for t in range(T):
                    v.wait_ge(sh_ps, T * b + t + 1)
                    v.wait_ge(u_out[t % 2], 16 * (2 * b + t // 2))
                    v.scalar_tensor_tensor(u[:, t % 2, :], TP[t % 2][:, 0:D], der[:, 3:4], sbb[:, :], ALU.mult, ALU.add).then_inc(u_ready, 1)
                    v.tensor_scalar(logit[:, bass.ds(b * T + t, 1), :].rearrange("p a e -> p (a e)"), TP[t % 2][:, D:D + E], der[:, 4:5], None,
                                    ALU.mult).then_inc(lg_ready, 1)

            def e_bounds(e, which):
                link = chain(v, e_v, EV * e + (0, EV1A)[which])
                v.wait_ge(e_tot, 2 * e + which + 1)
                if which == 0:
                    link(v.scalar_tensor_tensor(ebnd[:, 1:2], etot[:, 0:1], float(D), etot[:, 1:2], ALU.mult, ALU.add))
                    link(v.tensor_scalar(ebnd[:, 0:1], etot[:, 0:1], 1e-24, None, ALU.max))
                    link(v.tensor_scalar(ebnd[:, 1:2], ebnd[:, 1:2], 2.0, 1e-24, ALU.mult, ALU.max))
                    link(v.reciprocal(ebnd[:, 0:2], ebnd[:, 0:2]))
                else:
                    link = chain(v, e_v, EV * e + EV1)
                    link(v.tensor_scalar(ebnd[:, 2:3], etot[:, 2:3], 1e-24, None, ALU.max))
                    link(v.reciprocal(ebnd[:, 2:3], ebnd[:, 2:3]))

            def e_tables(e, which):
                lo, hi = ((0, 2), (2, 3))[which]
                v.wait_ge(e_a, 2 * e + which + 1)
                v.tensor_scalar(escl[:, lo:hi].bitcast(I32), escl[:, lo:hi].bitcast(I32), EXP_MASK, None, ALU.bitwise_and).then_inc(e_tab, 1)
                v.wait_ge(e_tab, 2 * e + which + 1)
                link = chain(v, e_v, EV * e + (EV1A, EV2A)[which])
                link(v.tensor_scalar(einv[:, lo:hi].bitcast(I32), escl[:, lo:hi].bitcast(I32), -1.0, EXP_FLIP, ALU.mult, ALU.add))
                if which == 0:
                    link(v.tensor_scalar(tab[:, 0, bass.ds(e, 1)], einv[:, 0:1], 1.0 / SX, None, ALU.mult))
                    link(v.tensor_copy(tab[:, 1, bass.ds(e, 1)], escl[:, 1:2]))
                else:
                    link(v.tensor_tensor(tab[:, 2, bass.ds(e, 1)], einv[:, 2:3], einv[:, 1:2], ALU.mult))

            def e_low(e, which):
                v.wait_ge(w_hi, 2 * e + which + 1)
                if which == 0:
                    v.scalar_tensor_tensor(w1_part(e, 1), stage1, escl[:, 0:1], w1_part(e, 0), ALU.mult, ALU.subtract).then_inc(w_lo, 1)
                else:
                    v.scalar_tensor_tensor(w2_part(e, 1), stage2(e), escl[:, 2:3], w2_part(e, 0), ALU.mult, ALU.subtract).then_inc(w_lo, 1)

            def step(s):
                b1_, b2_, b3_, e = parts(s)
                if b2_ is not None:
                    norms(b2_)
                if b1_ is not None:
                    enter(b1_)
                if b3_ is not None:
                    turned(b3_, xfT[:, 1, :, :].rearrange("p k c -> p (k c)"), t3, xfT_ready, [(sh_ps, T * b3_)])
                if b2_ is not None:
                    cosines(b2_)
                if e is not None:
                    e_bounds(e, 0)
                if b3_ is not None:
                    shared_out(b3_)
                if e is not None:
                    e_tables(e, 0)
                if b1_ is not None:
                    turned(b1_, xTf(b1_, 1), t1, xT_ready, [(z_ps, 2 * (b1_ - 1))])
                if b2_ is not None:
                    tailor(b2_)
                if b1_ is not None:
                    q_out(b1_, 0)
                    q_out(b1_, 1)
                if b2_ is not None:
                    m_low(b2_)
                if e is not None:
                    e_low(e, 0)
                if b1_ is not None:
                    q_out(b1_, 2)
                    q_out(b1_, 3)
                if e is not None:
                    e_bounds(e, 1)
                    e_tables(e, 1)
                if b2_ is not None:
                    leave(b2_)
                if e is not None:
                    e_low(e, 1)
            run_steps(v, step)
            v.wait_ge(sh_ps, T * B)
            v.wait_ge(z_ps, 2 * B)
            v.wait_ge(xfh_ready, B)
            v.wait_ge(xfl_ready, B)
            v.wait_ge(xf_out, 16 * B)
            v.wait_ge(u_out[0], 16 * B * T // 2)
            v.wait_ge(u_out[1], 16 * B * T // 2)
            v.wait_ge(lg_ready, T * B)
            v.memset(red, 0.0).then_inc(zone_free, 1)
            for e in range(EARLY, E):
                for which in range(2):
                    e_bounds(e, which)
                    e_tables(e, which)
                    e_low(e, which)
            vector_rest(v)


_OUT = ((8, 512, 256), "float32")
_INS = ["L0_attn_x", "L0_attn_Wq", "L0_attn_bq", "L0_attn_Wk", "L0_attn_bk", "L0_attn_Wv", "L0_attn_bv", "L0_attn_gamma",
        "L0_ffn_W1", "L0_ffn_b1", "L0_ffn_W2", "L0_ffn_b2", "L0_ffn_gate_W", "L0_ffn_shared_W", "L0_ffn_shared_b",
        "L0_ffn_gamma", "L0_ffn_beta"]


def kernel(**inputs):
    import numpy as _np
    import concourse.bacc as _bacc
    from concourse import mybir as _mybir
    from concourse.bass_utils import run_bass_kernel_spmd as _run

    nc = _bacc.Bacc("TRN2", target_bir_lowering=False, num_devices=1)
    arrays, args = {}, []
    for name in _INS:
        a = _np.ascontiguousarray(inputs[name])
        arrays[f"in_{name}"] = a
        args.append(nc.dram_tensor(f"in_{name}", a.shape, _mybir.dt.from_np(a.dtype), kind="ExternalInput").ap())
    args.append(nc.dram_tensor("out_0", _OUT[0], _mybir.dt.from_np(_np.dtype(_OUT[1])), kind="ExternalOutput").ap())
    sandwich(nc, *args)
    r = _run(nc, [arrays], core_ids=[0])
    return r.results[0]["out_0"]
```

```python
from contextlib import ExitStack

import concourse.bass as bass
from concourse import mybir
from concourse.alu_op_type import AluOpType as ALU

ACT = mybir.ActivationFunctionType
AX = mybir.AxisListType
F32 = mybir.dt.float32
F16 = mybir.dt.float16
I32 = mybir.dt.int32
U32 = mybir.dt.uint32

P = 128
EPS_LN = 1e-5
EPS_TAILOR = 1e-6
SX = 2048.0
SG = 16384.0
TOP = 32768.0
DCH = 6
SETUP_V = 23
EV1A, EV1, EV2A, EV = 4, 7, 9, 11
EXP_MASK = 0x7F800000
EXP_FLIP = float(0x7F000000)
BT = 256
HALVES = BT // P


def sandwich(nc, x_in, Wq, bq, Wk, bk, Wv, bv, gam, W1, b1, W2, b2, gate_W, shared_W, shared_b, lng, lnb, out):
    B, C, D = x_in.shape
    E, _, H = W1.shape
    T = C // P
    NF = D // P
    NH = H // P
    TOK = B * C
    NG = TOK // P
    NB = 2 * TOK // BT + E - 1
    PAIRS = 2 * TOK
    SLOTS = NB * BT
    EARLY = 5
    WE = 2 * NF * H + 2 * NH * D

    def dram(name, shape, dt):
        return nc.dram_tensor(name, shape, dt).ap()

    xf_rows = dram("xf_rows", [TOK, 2 * D], F16)
    u_rows = dram("u_rows", [TOK, D], F32)
    table = dram("table", [SLOTS, 4], I32)
    y_rows = dram("y_rows", [PAIRS + SLOTS, D], F32)

    ctx = ExitStack()
    with ctx:
        def sb(name, shape, dt):
            return ctx.enter_context(nc.sbuf_tensor(name, shape, dt))

        def sem(name):
            return ctx.enter_context(nc.semaphore(name))

        W = sb("W", [P, E * WE], F16)
        X = sb("X", [P, NG, D], F32)
        stage = sb("stage", [P, 4096], F32)
        zone = sb("zone", [P, 4096], F32)
        b2b = sb("b2b", [P, E * D], F32)
        lngb = sb("lngb", [P, 2, D], F32)
        sbb = sb("sbb", [P, D], F32)
        ident = sb("ident", [P, P], F16)
        upper = sb("upper", [P, P], F16)
        ones32 = sb("ones32", [P, P], F32)
        row2048 = sb("row2048", [1, P], F16)
        logit = sb("logit", [P, NG, E], F32)
        b1T = sb("b1T", [P, E * NH], F32)
        eps = sb("eps", [P, 3], F32)
        gam_b = sb("gam_b", [P, 1], F32)
        bvc = sb("bvc", [P, NF], F32)
        a1 = sb("a1", [P, NG], F32)
        c2 = sb("c2", [P, NG], F32)
        st = sb("st", [P, 3, T, 6], F32)
        mv = sb("mv", [P, 3, T, 2], F32)
        sd = sb("sd", [P, 3, T], F32)
        cf = sb("cf", [P, 3, T], F32)
        c3 = sb("c3", [P, T], F32)
        kn = sb("kn", [P, 4], F32)
        rk = sb("rk", [P, 4], F32)
        dn = sb("dn", [P, 4], F32)
        ssq = sb("ssq", [P, 8], F32)
        bnd = sb("bnd", [P, 8], F32)
        scl = sb("scl", [P, 8], F32)
        inv = sb("inv", [P, 8], F32)
        der = sb("der", [P, 16], F32)
        essq = sb("essq", [P, 4], F32)
        etot = sb("etot", [P, 4], F32)
        ebnd = sb("ebnd", [P, 4], F32)
        escl = sb("escl", [P, 4], F32)
        einv = sb("einv", [P, 4], F32)
        tab = sb("tab", [P, 3, E], F32)
        slot_i = sb("slot_i", [P, 2, NG], I32)
        ej_i = sb("ej_i", [P, 48], I32)
        tb = sb("tb", [P, 2, HALVES, 4], I32)
        tsc = sb("tsc", [P, 2, HALVES, 4], I32)

        class Carver:
            def __init__(self, pools):
                self.pools = [list(p) for p in pools]

            def __call__(self, shape, dt):
                n = 1
                for s in shape[1:]:
                    n *= s
                words = (n * (2 if dt == F16 else 4) + 3) // 4
                words = (words + 7) // 8 * 8
                for p in self.pools:
                    if p[1] + words <= p[2]:
                        at = p[1]
                        p[1] += words
                        v = p[0][:, at:at + words]
                        if dt != F32:
                            v = v.bitcast(dt)
                        v = v[0:shape[0], 0:n]
                        if len(shape) == 3:
                            v = v.rearrange("p (a b) -> p a b", b=shape[2])
                        if len(shape) == 4:
                            v = v.rearrange("p (a b c) -> p a b c", b=shape[2], c=shape[3])
                        return v
                raise ValueError("no room")

        ones16 = sb("ones16", [P, P], F16)
        bsq = sb("bsq", [P, NH], F32)
        tinit = W[:, 0:NB * HALVES * 8].bitcast(I32).rearrange("p (g c) -> p g c", c=4)
        late = W[:, EARLY * WE:E * WE].bitcast(F32)
        at_ = Carver([(late, 0, (E - EARLY) * WE // 2), (zone, 0, 4096), (stage, 2048, 4096)])
        xhl = at_([P, T, 2, D], F16)
        xs = at_([P, T, D], F32)
        xT = at_([P, 2 * 2 * NF * C], F16)
        q32 = at_([P, 2, 2 * D], F32)
        qkh = at_([P, T, 2 * D], F16)
        qkl = at_([P, T, 2 * D], F16)
        z = at_([P, T, D], F32)
        xfhl = at_([P, T, 2, D], F16)
        xfT = at_([P, NF, 2, C], F16)
        wqkT = at_([P, NF, 2, 2 * D], F16)
        sqt = at_([P, 2 * D], F32)
        sqa = at_([P, 2 * D], F32)
        gk = at_([P, NF, D], F32)
        ghl = at_([P, 2, NF, D], F16)
        m32 = at_([P, NF, D], F32)
        mhl = at_([P, 2, NF, D], F16)
        wvs = at_([P, NF, 2, D], F16)
        sgs = at_([P, NF, 2, D + E], F16)
        bqk = at_([P, 2 * D], F32)
        u = at_([P, 2, D], F32)
        bvb = at_([P, NF, P], F32)
        dgq = at_([P, NF, P], F32)
        dgt = at_([P, NF, P], F32)
        colrow = at_([P, D], F32)
        r32 = at_([1, D], F32)
        rhl = at_([1, 2, D], F16)
        gate_n = at_([P, NF, E], F32)
        vsum = at_([P, NF], F32)
        ident32 = at_([P, P], F32)


        PS = [ctx.enter_context(nc.psum_tensor(f"bank{i}", [P, 512], F32)) for i in range(8)]
        TP = [PS[0], PS[1]]
        QB = [PS[2], PS[3]]
        GB, NB5, SB6, MB = PS[4], PS[5], PS[6], PS[7]

        x_loaded = sem("x_loaded")
        bias_in = sem("bias_in")
        b2_in = sem("b2_in")
        b1_in = sem("b1_in")
        wqk_in = sem("wqk_in")
        wv_in = sem("wv_in")
        sh_in = sem("sh_in")
        bvc_in = sem("bvc_in")
        c_eps = sem("c_eps")
        c_ones = sem("c_ones")
        c_row = sem("c_row")
        c_ident = sem("c_ident")
        c_upper = sem("c_upper")
        ssq_ready = sem("ssq_ready")
        ssq_sum = sem("ssq_sum")
        setup_v = sem("setup_v")
        setup_a = sem("setup_a")
        wqk_t = sem("wqk_t")
        wqk_h = sem("wqk_h")
        wqk_l = sem("wqk_l")
        wv_h = sem("wv_h")
        wv_l = sem("wv_l")
        sg_h = sem("sg_h")
        sg_l = sem("sg_l")
        vs_ps = sem("vs_ps")
        b1_t = sem("b1_t")
        b1_ready = sem("b1_ready")
        w1_in = sem("w1_in")
        w2_in = sem("w2_in")
        e_ssq = sem("e_ssq")
        e_tot = sem("e_tot")
        e_ps = sem("e_ps")
        e_v = sem("e_v")
        e_a = sem("e_a")
        e_tab = sem("e_tab")
        w_hi = sem("w_hi")
        w_lo = sem("w_lo")
        st1 = sem("st1")
        mv1 = sem("mv1")
        sd1 = sem("sd1")
        a1_ready = sem("a1_ready")
        c1_ready = sem("c1_ready")
        xs_ready = sem("xs_ready")
        xh_ready = sem("xh_ready")
        xl_ready = sem("xl_ready")
        t1 = sem("t1")
        xT_ready = sem("xT_ready")
        qk_ps = sem("qk_ps")
        q_ev = sem("q_ev")
        q_h = sem("q_h")
        sq_t = sem("sq_t")
        q_l = sem("q_l")
        sq_acc = sem("sq_acc")
        g_ps = sem("g_ps")
        nrm_ps = sem("nrm_ps")
        nsq = sem("nsq")
        rk_ready = sem("rk_ready")
        rqs_ready = sem("rqs_ready")
        dq_ready = sem("dq_ready")
        rqb_ps = sem("rqb_ps")
        g32_ready = sem("g32_ready")
        gh_ready = sem("gh_ready")
        gl_ready = sem("gl_ready")
        dt_ready = sem("dt_ready")
        tgb_ps = sem("tgb_ps")
        row_set = sem("row_set")
        sum_ps = sem("sum_ps")
        dchain = sem("dchain")
        rh_ready = sem("rh_ready")
        rl_ready = sem("rl_ready")
        m_ps = sem("m_ps")
        m32_ready = sem("m32_ready")
        mh_ready = sem("mh_ready")
        ml_ready = sem("ml_ready")
        z_ps = sem("z_ps")
        z_mul = sem("z_mul")
        z_add = sem("z_add")
        st2 = sem("st2")
        mv2 = sem("mv2")
        sd2 = sem("sd2")
        r2_ready = sem("r2_ready")
        c2_ready = sem("c2_ready")
        x1_ready = sem("x1_ready")
        st3 = sem("st3")
        mv3 = sem("mv3")
        sd3 = sem("sd3")
        a3_ready = sem("a3_ready")
        c3_ready = sem("c3_ready")
        xf_ready = sem("xf_ready")
        xfh_ready = sem("xfh_ready")
        xfl_ready = sem("xfl_ready")
        xf_out = sem("xf_out")
        t3 = sem("t3")
        xfT_ready = sem("xfT_ready")
        sh_ps = sem("sh_ps")
        lg_ready = sem("lg_ready")
        u_ready = sem("u_ready")
        u_out = [sem("u_out0"), sem("u_out1")]
        zone_free = sem("zone_free")
        exp_max = sem("exp_max")
        exp_ready = sem("exp_ready")
        route = sem("route")
        both_ready = sem("both_ready")
        cnt_ps = sem("cnt_ps")
        slots_ready = sem("slots_ready")
        pay_ready = sem("pay_ready")
        table_init = sem("table_init")
        table_set = sem("table_set")
        ej_ready = sem("ej_ready")
        tb_in = [sem("tb_in0"), sem("tb_in1")]
        ts_in = [sem("ts_in0"), sem("ts_in1")]
        xg_in = [sem("xg_in0"), sem("xg_in1")]
        xt_ps = sem("xt_ps")
        xt_ready = sem("xt_ready")
        h_ps = sem("h_ps")
        h_act = sem("h_act")
        h_hi = sem("h_hi")
        h_lo = sem("h_lo")
        y_ps = sem("y_ps")
        y_ev = sem("y_ev")
        y_ready = sem("y_ready")
        y_out = [sem("y_out0"), sem("y_out1")]
        tu_in = sem("tu_in")
        tu_ready = sem("tu_ready")
        ty_in = sem("ty_in")
        t_sum = sem("t_sum")
        t_o = sem("t_o")
        st4 = sem("st4")
        mv4 = sem("mv4")
        sd4 = sem("sd4")
        r4 = sem("r4")
        c4 = sem("c4")
        t_n = sem("t_n")
        t_g = sem("t_g")
        t_b = sem("t_b")
        st5 = sem("st5")
        mv5 = sem("mv5")
        sd5 = sem("sd5")
        r5 = sem("r5")
        c5 = sem("c5")
        t_f = sem("t_f")
        t_r = sem("t_r")
        t_out = sem("t_out")
        route_consts = sem("route_consts")
        iota_t = sem("iota_t")
        passed = sem("passed")

        def past(count):
            return max(count, 0) if isinstance(count, int) else count

        def settle(eng):
            eng.sem_inc(passed, 1)

        def chain(eng, name, start):
            count = [0]

            def link(ins):
                count[0] += 1
                ins.then_inc(name, 1)
                eng.wait_ge(name, start + count[0])
            link.count = count
            return link

        def at(ap, i):
            return ap[i] if isinstance(i, int) else ap[bass.ds(i, 1)].squeeze(0)

        def run_steps(eng, step):
            for s in range(3):
                step(s)
            with eng.Fori(3, B) as s:
                step(s)
            for s in range(B, B + 2):
                step(s)

        def parts(s):
            if not isinstance(s, int):
                return s, s - 1, s - 2, s - 3
            return tuple(b if 0 <= b < B else None for b in (s, s - 1, s - 2)) + (None,)

        def xTf(b, f):
            n = 2 * C
            return xT[:, bass.ds((b % 2) * (NF * n) + f * n, n)]

        def xTt(b, f, k, t):
            n = 2 * C
            return xT[:, bass.ds((b % 2) * (NF * n) + (f * n + k * C + t * P), P)]

        def Xt(b, t):
            return X[:, bass.ds(b * T + t, 1), :].rearrange("p a d -> p (a d)")

        def w1_part(e, k):
            return W[:, bass.ds(e * WE, 2 * NF * H)].rearrange("p (f k n) -> p f k n", f=NF, k=2)[:, :, k, :]

        def w2_part(e, k):
            return W[:, bass.ds(e * WE + 2 * NF * H, 2 * NH * D)].rearrange("p (j k n) -> p j k n", j=NH, k=2)[:, :, k, :]

        stage1 = stage[:, 0:2048].rearrange("p (f n) -> p f n", f=NF)

        def stage2(e):
            half = int(isinstance(e, int) and e >= EARLY)
            return stage[:, 2048 * half:2048 * half + 2048].rearrange("p (j n) -> p j n", j=NH)

        zr = Carver([(zone, 0, 4096)])
        probs = zr([P, NG, E], F32)
        iota_e = zr([P, NG, E], F32)
        tmp = zr([P, NG, E], F32)
        pick = [zr([P, NG, E], F32) for _ in range(2)]
        both = zr([P, E, NG], F16)
        carry = zr([P, E, NG], F32)
        cum = zr([P, E, NG], F32)
        rank = zr([P, E, NG], F32)
        pay = zr([P, NG, 2, 4], I32)
        jcmp = zr([P, NB, E], F32)
        ejf = zr([P, NB], F32)
        best = [zr([P, NG], F32) for _ in range(2)]
        red = zr([P, NG], F32)
        wsum = zr([P, NG], F32)
        nblk = zr([P, E], F32)
        nblk_i = zr([P, E], I32)
        bend = zr([P, E], F32)
        boff = zr([P, E], F32)
        one8 = zr([P, E], F32)

        zf = Carver([(zone, 0, 4096)])
        xg = zf([P, 2 * HALVES, 2 * D], F16)
        xbT = zf([P, 2 * NF * 2, BT], F16)
        h32 = zf([P, 2, 2 * BT], F32)
        y32 = zf([P, 2 * HALVES, D], F32)
        hhl = stage[:, :].bitcast(F16).rearrange("p (q j k n) -> p q j k n", q=2, j=NH, k=2)

        tail = Carver([(W[:, :].bitcast(F32), 0, E * WE // 2)])
        tu = tail([P, NG, D], F32)
        ty = tail([P, NG, 2, D], F32)
        to = tail([P, NG, D], F32)

        def sync_rest(sp):
            sp.wait_ge(table_set, 16 * 2 * NG)
            sp.wait_ge(xf_out, 16 * B)
            tv = table.rearrange("(j h p) c -> j p h c", p=P, h=HALVES)

            def load_tb(j, q, n):
                sp.wait_ge(xg_in[q], 16 * HALVES * n)
                sp.dma_start(tb[:, q, :, :], at(tv, j)).then_inc(tb_in[q], 16)

            def load_ts(j, q, n):
                sp.wait_ge(y_out[q], 16 * HALVES * n)
                sp.dma_start(tsc[:, q, :, :], at(tv, j)).then_inc(ts_in[q], 16)

            load_tb(0, 0, 0)
            load_tb(1, 1, 0)
            load_ts(0, 0, 0)
            load_ts(1, 1, 0)
            load_tb(2, 0, 1)
            load_tb(3, 1, 1)
            load_ts(2, 0, 1)
            with sp.Fori(1, (NB - 3) // 2) as i:
                load_tb(2 * i + 2, 0, i + 1)
                load_ts(2 * i + 1, 1, i)
                load_tb(2 * i + 3, 1, i + 1)
                load_ts(2 * i + 2, 0, i + 1)
            i = (NB - 3) // 2
            load_tb(2 * i + 2, 0, i + 1)
            load_ts(2 * i + 1, 1, i)
            load_ts(2 * i + 2, 0, i + 1)
            sp.wait_ge(y_ps, NB)
            sp.wait_ge(u_out[0], 16 * B * T // 2)
            sp.wait_ge(u_out[1], 16 * B * T // 2)
            ubv = u_rows.rearrange("(b p t) d -> b p (t d)", p=P, t=T)
            for b in range(B):
                sp.dma_start(tu[:, b * T:(b + 1) * T, :].rearrange("p t d -> p (t d)"), ubv[b]).then_inc(tu_in, 16)
            sp.wait_ge(y_out[0], 16 * HALVES * ((NB + 1) // 2))
            sp.wait_ge(y_out[1], 16 * HALVES * (NB // 2))
            yv = y_rows[0:PAIRS, :].rearrange("(b p t k) d -> b p (t k d)", p=P, t=T, k=2)
            for b in range(B):
                sp.wait_ge(ty_in, 16 * b)
                sp.dma_start(ty[:, b * T:(b + 1) * T, :, :].rearrange("p t k d -> p (t k d)"), yv[b]).then_inc(ty_in, 16)
            with sp.Fori(0, B) as b:
                sp.wait_ge(t_r, b + 1)
                sp.dma_start(at(outrows, b), to_(b).rearrange("p t d -> p (t d)")).then_inc(t_out, 16)
            sp.wait_ge(t_out, 16 * B)

        def rows(buf, b):
            return buf[:, bass.ds(b * T, T), :]

        def to_(b):
            return rows(to, b)

        def gpsimd_rest(g):
            g.wait_ge(zone_free, 1)
            g.iota(iota_e, [[0, NG], [1, E]], base=0, channel_multiplier=0, allow_small_or_imprecise_dtypes=True).then_inc(route_consts, 1)
            g.memset(carry, 1.0).then_inc(route_consts, 1)
            g.wait_ge(route_consts, 2)
            g.memset(carry[:, :, 0:1], 0.0).then_inc(route_consts, 1)
            g.iota(jcmp, [[1, NB], [0, E]], base=0, channel_multiplier=0, allow_small_or_imprecise_dtypes=True).then_inc(route_consts, 1)
            g.memset(one8, 1.0).then_inc(route_consts, 1)
            pv = pay.rearrange("p (b t) k c -> p b t k c", t=T)
            g.iota(pv[:, :, :, :, 0], [[C, B], [1, T], [0, 2]], base=0, channel_multiplier=T).then_inc(pay_ready, 1)
            g.iota(pv[:, :, :, :, 1], [[2 * C, B], [2, T], [1, 2]], base=0, channel_multiplier=2 * T).then_inc(pay_ready, 1)
            g.iota(pv[:, :, :, :, 3], [[0, B], [0, T], [0, 2]], base=0, channel_multiplier=0).then_inc(pay_ready, 1)
            g.wait_ge(pay_ready, 5)
            g.wait_ge(slots_ready, 1)
            g.wait_ge(table_init, 16)
            for t in range(NG):
                for k in range(2):
                    g.indirect_dma_start(out=table, out_offset=bass.IndirectOffsetOnAxis(ap=slot_i[:, k, t:t + 1], axis=0),
                                         in_=pay[:, t, k, :], in_offset=None).then_inc(table_set, 16)
            g.wait_ge(table_set, 16 * 2 * NG)
            g.wait_ge(xf_out, 16 * B)

            def gather(j, q, n):
                g.wait_ge(tb_in[q], 16 * (n + 1))
                g.wait_ge(xt_ps, past(j - 1))
                settle(g)
                for h in range(HALVES):
                    g.indirect_dma_start(out=xg[:, q * HALVES + h, :], out_offset=None, in_=xf_rows,
                                         in_offset=bass.IndirectOffsetOnAxis(ap=tb[:, q, h, 0:1], axis=0)).then_inc(xg_in[q], 16)

            def scatter(j, q):
                g.wait_ge(y_ready, HALVES * (j + 1))
                settle(g)
                for h in range(HALVES):
                    g.indirect_dma_start(out=y_rows, out_offset=bass.IndirectOffsetOnAxis(ap=tsc[:, q, h, 1:2], axis=0),
                                         in_=y32[:, q * HALVES + h, :], in_offset=None).then_inc(y_out[q], 16)
            gather(0, 0, 0)
            gather(1, 1, 0)
            gather(2, 0, 1)
            gather(3, 1, 1)
            scatter(0, 0)
            gather(4, 0, 2)
            scatter(1, 1)
            with g.Fori(2, (NB - 1) // 2) as i:
                gather(2 * i + 1, 1, i)
                scatter(2 * i - 2, 0)
                gather(2 * i + 2, 0, i + 1)
                scatter(2 * i - 1, 1)
            i = (NB - 1) // 2
            scatter(2 * i - 2, 0)
            scatter(2 * i - 1, 1)
            scatter(2 * i, 0)

            def add_pairs(b):
                g.wait_ge(ty_in, 16 * (b + 1))
                yb = ty[:, bass.ds(b * T, T), :, :]
                g.tensor_tensor(to_(b), yb[:, :, 0, :], yb[:, :, 1, :], ALU.add).then_inc(t_sum, 1)

            def add_beta(b):
                g.wait_ge(t_g, b + 1)
                g.tensor_tensor(to_(b), to_(b), lngb[:, 1, :].unsqueeze(1).broadcast_to([P, T, D]), ALU.add).then_inc(t_b, 1)

            def add_x(b):
                g.wait_ge(t_f, T * (b + 1))
                g.tensor_tensor(to_(b), to_(b), rows(X, b), ALU.add).then_inc(t_r, 1)

            def tail_step(s, now, last, old, older):
                if not isinstance(s, int) or s + 1 < B:
                    add_pairs(s + 1)
                if older:
                    add_x(s - 3)
                if last:
                    add_beta(s - 1)
            add_pairs(0)
            tail_steps(g, tail_step)

        def tail_steps(eng, step):
            for s in range(3):
                step(s, True, s >= 1, s >= 2, False)
            with eng.Fori(3, B - 1) as s:
                step(s, True, True, True, True)
            for s in range(B - 1, B + 3):
                step(s, s < B, s < B + 1, s < B + 2, True)

        def tensor_rest(pe):
            pe.wait_ge(both_ready, 1)
            pe.wait_ge(c_upper, 2)
            bm = both.rearrange("p e g -> p (e g)")
            pe.matmul(NB5[:, 0:NG * E], upper[:, :], bm, start=True, stop=True)
            pe.matmul(NB5[:, NG * E:2 * NG * E], ones16[:, :], bm, start=True, stop=True).then_inc(cnt_ps, 1)
            for e in range(EARLY, E):
                for which in range(2):
                    lo, hi = ((0, 2), (2, 3))[which]
                    pe.wait_ge(e_ssq, 3 * e + 2 + which)
                    pe.wait_ge(e_tot, 2 * e + which)
                    pe.matmul(MB[:, lo:hi], ones32[:, :], essq[:, lo:hi], start=True, stop=True).then_inc(e_ps, 1)
            pe.wait_ge(w_lo, 2 * E)
            pe.wait_ge(w_hi, 2 * E)
            pe.wait_ge(ej_ready, 1)

            def turn(j, q, n):
                pe.wait_ge(xg_in[q], 16 * HALVES * (n + 1))
                pe.wait_ge(xt_ready, j)
                for f in range(NF):
                    for k in range(2):
                        for h in range(HALVES):
                            at0 = ((f * 2 + k) * HALVES + h) * P
                            mm = pe.transpose(PS[4][:, :].bitcast(F16)[:, at0:at0 + P],
                                              xg[:, q * HALVES + h, k * D + f * P:k * D + (f + 1) * P], ident[:, :])
                mm.then_inc(xt_ps, 1)

            def up(j, q):
                e = pe.value_load(ej_i[0:1, bass.ds(j, 1)], min_val=0, max_val=E - 1)
                pe.wait_ge(xt_ready, j + 1)
                for m in range(NH // 2):
                    pe.wait_ge(h_act, past(NH * (j - 1) + 2 * m + 2))
                    for r in range(2):
                        for f in range(NF):
                            ws = [W[:, bass.ds(e * WE + (f * 2 + k) * H + (2 * m + r) * P, P)] for k in range(2)]
                            xs_ = [xbT[:, (q * NF + f) * 2 + k, :] for k in range(2)]
                            mm = mm3(pe, PS[m][:, r * BT:(r + 1) * BT], ws[0], ws[1], xs_[0], xs_[1], f == 0, f == NF - 1)
                    mm.then_inc(h_ps, 1)

            def down(j, q):
                e = pe.value_load(ej_i[0:1, bass.ds(j, 1)], min_val=0, max_val=E - 1)
                pe.wait_ge(y_ev, past(j - 1))
                for h in range(HALVES):
                    for m in range(NH):
                        if h == 0 and m % 2 == 0:
                            pe.wait_ge(h_lo, NH // 2 * j + m // 2 + 1)
                        ws = [W[:, bass.ds(e * WE + 2 * NF * H + (m * 2 + k) * D, D)] for k in range(2)]
                        mm = mm3(pe, PS[5 + q][:, h * D:(h + 1) * D], hhl[:, q, m, 0, h * P:(h + 1) * P], hhl[:, q, m, 1, h * P:(h + 1) * P],
                                 ws[0], ws[1], m == 0, m == NH - 1)
                mm.then_inc(y_ps, 1)
            turn(0, 0, 0)
            up(0, 0)
            turn(1, 1, 0)
            up(1, 1)
            turn(2, 0, 1)
            down(0, 0)
            up(2, 0)
            turn(3, 1, 1)
            down(1, 1)
            with pe.Fori(2, (NB - 1) // 2) as i:
                up(2 * i - 1, 1)
                turn(2 * i, 0, i)
                down(2 * i - 2, 0)
                up(2 * i, 0)
                turn(2 * i + 1, 1, i)
                down(2 * i - 1, 1)
            i = (NB - 1) // 2
            up(2 * i - 1, 1)
            turn(2 * i, 0, i)
            down(2 * i - 2, 0)
            up(2 * i, 0)
            down(2 * i - 1, 1)
            down(2 * i, 0)

        def scalar_rest(a):
            a.wait_ge(ej_ready, 1)
            a.preload_act_table(ACT.Gelu)

            def gelu(j, q):
                e = a.value_load(ej_i[0:1, bass.ds(j, 1)], min_val=0, max_val=E - 1)
                for m in range(NH // 2):
                    a.wait_ge(h_ps, NH // 2 * j + m + 1)
                    a.wait_ge(h_lo, past(NH // 2 * j + m - 1))
                    for r in range(2):
                        settle(a)
                        a.activation(h32[:, m % 2, r * BT:(r + 1) * BT], PS[m][:, r * BT:(r + 1) * BT], ACT.Gelu,
                                     bias=b1T[:, bass.ds(e * NH + 2 * m + r, 1)], scale=tab[:, 0, bass.ds(e, 1)]).then_inc(h_act, 1)
            gelu(0, 0)
            with a.Fori(1, NB) as j:
                gelu(j, 0)
            a.wait_ge(tu_in, 16 * B)
            for b in range(B):
                a.activation(tu[:, b * T:(b + 1) * T, :], tu[:, b * T:(b + 1) * T, :], ACT.Gelu).then_inc(tu_ready, 1)
            a.preload_act_table(ACT.Sqrt)

            def sd_(which, name, need, b):
                a.wait_ge(need, T * (b + 1))
                settle(a)
                a.activation(sd[:, which, :], mv[:, which, :, 1], ACT.Sqrt, bias=eps[:, 2:3]).then_inc(name, 1)

            def scaled(b, need, value, factor, shift, name):
                a.wait_ge(need, value)
                settle(a)
                for t in range(T):
                    o = to[:, bass.ds(b * T + t, 1), :].rearrange("p a d -> p (a d)")
                    a.activation(o, o, ACT.Identity, bias=shift[:, t:t + 1], scale=factor[:, t:t + 1]).then_inc(name, 1)

            def tail_step(s, now, last, old, older):
                if now:
                    sd_(0, sd4, mv4, s)
                if old:
                    sd_(1, sd5, mv5, s - 2)
                if now:
                    scaled(s, c4, s + 1, cf[:, 0, :], cf[:, 2, :], t_n)
                if old:
                    scaled(s - 2, c5, 2 * (s - 1), cf[:, 1, :], c3, t_f)
            tail_steps(a, tail_step)

        def vector_route(v):
            def wide(x):
                return x.unsqueeze(2).broadcast_to([P, NG, E])
            link = chain(v, route, 0)
            v.wait_ge(zone_free, 1)
            link(v.tensor_reduce(red, logit[:, :, :], AX.X, ALU.max))
            v.tensor_tensor(probs, logit[:, :, :], wide(red), ALU.subtract).then_inc(exp_max, 1)
            v.wait_ge(exp_ready, 1)
            link(v.tensor_reduce(red, probs, AX.X, ALU.add))
            link(v.reciprocal(red, red))
            link(v.tensor_tensor(probs, probs, wide(red), ALU.mult))
            v.wait_ge(route_consts, 5)
            for k in range(2):
                link(v.tensor_reduce(best[k], probs, AX.X, ALU.max))
                link(v.tensor_tensor(tmp, probs, wide(best[k]), ALU.is_equal))
                link(v.scalar_tensor_tensor(tmp, tmp, -float(E), iota_e, ALU.mult, ALU.add))
                link(v.tensor_reduce(red, tmp, AX.X, ALU.min))
                link(v.tensor_tensor(pick[k], tmp, wide(red), ALU.is_equal))
                if k == 0:
                    link(v.scalar_tensor_tensor(probs, pick[0], -2.0, probs, ALU.mult, ALU.add))
            link(v.tensor_tensor(both.rearrange("p e g -> p g e"), pick[0], pick[1], ALU.add))
            v.tensor_copy(nblk, one8).then_inc(both_ready, 1)
            link(v.tensor_tensor(wsum, best[0], best[1], ALU.add))
            link(v.reciprocal(wsum, wsum))
            v.wait_ge(pay_ready, 3)
            for k in range(2):
                v.tensor_tensor(pay[:, :, k, 2].bitcast(F32), best[k], wsum, ALU.mult).then_inc(pay_ready, 1)
            v.wait_ge(cnt_ps, 1)
            before = NB5[:, 0:NG * E]
            count = NB5[:, NG * E:2 * NG * E]
            flat = lambda x: x.rearrange("p e g -> p (e g)")
            link(v.tensor_tensor_scan(flat(cum), flat(carry), count, 0.0, ALU.mult, ALU.add))
            link(v.tensor_tensor(flat(rank), flat(cum), count, ALU.subtract))
            link(v.tensor_tensor(flat(rank), flat(rank), before, ALU.add))
            link(v.tensor_scalar(nblk_i, cum[:, :, NG - 1], float(BT - 1), None, ALU.add))
            link(v.tensor_scalar(nblk_i, nblk_i, BT.bit_length() - 1, None, ALU.arith_shift_right))
            link(v.tensor_copy(nblk, nblk_i))
            link(v.tensor_tensor_scan(bend, one8, nblk, 0.0, ALU.mult, ALU.add))
            link(v.tensor_tensor(boff, bend, nblk, ALU.subtract))
            link(v.tensor_scalar(boff, boff, float(BT), None, ALU.mult))
            link(v.tensor_tensor(rank, rank, boff.unsqueeze(2).broadcast_to([P, E, NG]), ALU.add))
            for k in range(2):
                link(v.tensor_tensor(tmp, pick[k], rank.rearrange("p e g -> p g e"), ALU.mult))
                link(v.tensor_reduce(red, tmp, AX.X, ALU.add))
                link(v.tensor_copy(slot_i[:, k, :], red))
            v.wait_ge(route, link.count[0])
            v.tensor_copy(nblk, one8).then_inc(slots_ready, 1)
            link(v.tensor_tensor(jcmp, jcmp, bend.unsqueeze(1).broadcast_to([P, NB, E]), ALU.is_ge))
            link(v.tensor_reduce(ejf, jcmp, AX.X, ALU.add))
            link(v.tensor_scalar(ej_i[:, 0:NB], ejf, float(E - 1), None, ALU.min))
            v.wait_ge(route, link.count[0])
            v.tensor_copy(nblk, one8).then_inc(ej_ready, 1)

        def vector_rest(v):
            def split(j, q):
                e = v.value_load(ej_i[0:1, bass.ds(j, 1)], min_val=0, max_val=E - 1)
                v.wait_ge(y_ps, past(j - 1))
                for m in range(NH // 2):
                    v.wait_ge(h_act, NH * j + 2 * m + 2)
                    o = [hhl[:, q, 2 * m:2 * m + 2, k, :] for k in range(2)]
                    src = h32[:, m % 2, :].rearrange("p (r n) -> p r n", r=2)
                    v.tensor_scalar(o[0], src, tab[:, 1, bass.ds(e, 1)], None, ALU.mult).then_inc(h_hi, 1)
                    v.wait_ge(h_hi, NH // 2 * j + m + 1)
                    v.scalar_tensor_tensor(o[1], src, tab[:, 1, bass.ds(e, 1)], o[0], ALU.mult, ALU.subtract).then_inc(h_lo, 1)

            def turned_block(j, q):
                v.wait_ge(xt_ps, j + 1)
                v.wait_ge(h_ps, past(NH // 2 * (j - 1)))
                v.tensor_copy(xbT[:, q * NF * 2:(q + 1) * NF * 2, :].rearrange("p a n -> p (a n)"), PS[4][:, :].bitcast(F16)).then_inc(xt_ready, 1)

            def result(j, q, n):
                e = v.value_load(ej_i[0:1, bass.ds(j, 1)], min_val=0, max_val=E - 1)
                v.wait_ge(y_ps, j + 1)
                v.wait_ge(y_out[q], 16 * HALVES * n)
                yq = y32[:, q * HALVES:(q + 1) * HALVES, :]
                v.scalar_tensor_tensor(yq, PS[5 + q][:, :].rearrange("p (h d) -> p h d", h=HALVES), tab[:, 2, bass.ds(e, 1)],
                                       b2b[:, bass.ds(e * D, D)].unsqueeze(1).broadcast_to([P, HALVES, D]), ALU.mult, ALU.add).then_inc(y_ev, 1)
                v.wait_ge(y_ev, j + 1)
                v.wait_ge(ts_in[q], 16 * (n + 1))
                for h in range(HALVES):
                    v.tensor_scalar(y32[:, q * HALVES + h, :], y32[:, q * HALVES + h, :], tsc[:, q, h, 2:3].bitcast(F32), None,
                                    ALU.mult).then_inc(y_ready, 1)
            turned_block(0, 0)
            split(0, 0)
            turned_block(1, 1)
            split(1, 1)
            turned_block(2, 0)
            result(0, 0, 0)
            split(2, 0)
            turned_block(3, 1)
            result(1, 1, 0)
            with v.Fori(2, (NB - 1) // 2) as i:
                split(2 * i - 1, 1)
                turned_block(2 * i, 0)
                result(2 * i - 2, 0, i - 1)
                split(2 * i, 0)
                turned_block(2 * i + 1, 1)
                result(2 * i - 1, 1, i - 1)
            i = (NB - 1) // 2
            split(2 * i - 1, 1)
            turned_block(2 * i, 0)
            result(2 * i - 2, 0, i - 1)
            split(2 * i, 0)
            result(2 * i - 1, 1, i - 1)
            result(2 * i, 0, i)

            def tstats(which, b, need, value, st_name, mv_name):
                v.wait_ge(need, value)
                settle(v)
                for t in range(T):
                    v.bn_stats(st[:, which, t, :], to[:, bass.ds(b * T + t, 1), :].rearrange("p a d -> p (a d)")).then_inc(st_name, 1)
                for t in range(T):
                    v.wait_ge(st_name, T * b + t + 1)
                    settle(v)
                    v.bn_aggr(mv[:, which, t, :], st[:, which, t, :]).then_inc(mv_name, 1)

            def enter_tail(b):
                v.wait_ge(tu_ready, B)
                v.wait_ge(t_sum, b + 1)
                v.scalar_tensor_tensor(to_(b), rows(tu, b), 0.5, to_(b), ALU.mult, ALU.add).then_inc(t_o, 1)
                tstats(0, b, t_o, b + 1, st4, mv4)

            def inner_factors(b):
                v.wait_ge(sd4, b + 1)
                v.reciprocal(cf[:, 0, :], sd[:, 0, :]).then_inc(r4, 1)
                v.wait_ge(r4, b + 1)
                v.scalar_tensor_tensor(cf[:, 2, :], mv[:, 0, :, 0], -1.0, cf[:, 0, :], ALU.mult, ALU.mult).then_inc(c4, 1)

            def times_gamma(b):
                v.wait_ge(t_n, T * (b + 1))
                v.tensor_tensor(to_(b), to_(b), lngb[:, 0, :].unsqueeze(1).broadcast_to([P, T, D]), ALU.mult).then_inc(t_g, 1)

            def outer_factors(b):
                v.wait_ge(sd5, b + 1)
                v.wait_ge(t_f, T * b)
                v.reciprocal(cf[:, 1, :], sd[:, 1, :]).then_inc(r5, 1)
                v.wait_ge(r5, b + 1)
                v.scalar_tensor_tensor(c3[:, :], mv[:, 1, :, 0], -1.0, cf[:, 1, :], ALU.mult, ALU.mult).then_inc(c5, 1)
                v.wait_ge(c5, 2 * b + 1)
                v.tensor_tensor(c3[:, :], c3[:, :], c2[:, bass.ds(b * T, T)], ALU.add).then_inc(c5, 1)

            def tail_step(s, now, last, old, older):
                if last:
                    times_gamma(s - 1)
                if now:
                    enter_tail(s)
                if old:
                    tstats(1, s - 2, t_b, s - 1, st5, mv5)
                if now:
                    inner_factors(s)
                if old:
                    outer_factors(s - 2)
            tail_steps(v, tail_step)

        block = ctx.enter_context(nc.Block())
        xrows = x_in.rearrange("b (p t) d -> b p (t d)", t=T)
        outrows = out.rearrange("b (p t) d -> b p (t d)", t=T)
        xfv = xf_rows.rearrange("(b p t) d -> b p (t d)", p=P, t=T)
        uv = u_rows.rearrange("(b p t) d -> b p t d", p=P, t=T)
        wqk_n = z[:, :, :]
        wv_n = m32[:, :, :]
        sh_n = gk[:, :, :]
        b1_n = u[0:E * NH, 0, 0:P]

        def mm3(pe, o, lh, ll, rh, rl, first, last):
            pe.matmul(o, lh, rh, start=first, stop=False)
            pe.matmul(o, lh, rl, start=False, stop=False)
            return pe.matmul(o, ll, rh, start=False, stop=last)

        @block.sync
        def _(sp):
            def load_x(b):
                sp.wait_ge(x_loaded, 16 * b)
                sp.dma_start(X[:, b * T:(b + 1) * T, :].rearrange("p t d -> p (t d)"), xrows[b]).then_inc(x_loaded, 16)

            def load_w1(e):
                sp.wait_ge(w_hi, 2 * e)
                sp.wait_ge(w_lo, 2 * e)
                sp.dma_start(stage[:, 0:2048].rearrange("p (f n) -> p f n", f=NF),
                             at(W1, e).rearrange("(f p) n -> p f n", p=P)).then_inc(w1_in, 16)

            def load_w2(e, half):
                if not half:
                    sp.wait_ge(w_hi, 2 * e + 1)
                    sp.wait_ge(w_lo, 2 * e + 1)
                sp.dma_start(stage[:, 2048 * half:2048 * half + 2048].rearrange("p (j n) -> p j n", j=NH),
                             at(W2, e).rearrange("(j p) n -> p j n", p=P)).then_inc(w2_in, 16)

            def load_late(e, which):
                if e == EARLY:
                    sp.wait_ge(w_hi, 2 * e)
                    sp.wait_ge(w_lo, 2 * e)
                    if which:
                        sp.wait_ge(zone_free, 1)
                else:
                    sp.wait_ge(w_hi, past(2 * e - 1 + which))
                    sp.wait_ge(w_lo, past(2 * e - 1 + which))
                if which:
                    sp.dma_start(stage2(e), W2[e].rearrange("(j p) n -> p j n", p=P)).then_inc(w2_in, 16)
                else:
                    sp.dma_start(stage1, W1[e].rearrange("(f p) n -> p f n", p=P)).then_inc(w1_in, 16)

            def store_u(b, t):
                sp.wait_ge(u_ready, T * b + t + 1)
                sp.dma_start(at(uv, b)[:, t, :], u[:, t % 2, :]).then_inc(u_out[t % 2], 16)

            def store_xf(b):
                sp.wait_ge(xfh_ready, b + 1)
                sp.wait_ge(xfl_ready, b + 1)
                sp.dma_start(at(xfv, b),
                             xfhl.rearrange("p t k d -> p (t k d)")).then_inc(xf_out, 16)

            load_x(0)
            with nc.allow_non_contiguous_dma(reason="512 single words, once"):
                for j in range(NF):
                    sp.dma_start(wqk_n[:, j, :], Wq[j * P:(j + 1) * P, :]).then_inc(wqk_in, 16)
                    sp.dma_start(wqk_n[:, NF + j, :], Wk[j * P:(j + 1) * P, :]).then_inc(wqk_in, 16)
                sp.dma_start(bqk[:, 0:D], bq.partition_broadcast(P)).then_inc(bias_in, 16)
                sp.dma_start(bqk[:, D:2 * D], bk.partition_broadcast(P)).then_inc(bias_in, 16)
                sp.dma_start(wv_n, Wv.rearrange("(j p) i -> p j i", p=P)).then_inc(wv_in, 16)
                sp.dma_start(bvc[:, :], bv.rearrange("(j p) -> p j", p=P)).then_inc(bvc_in, 16)
                sp.dma_start(gam_b[:, :], gam.partition_broadcast(P)).then_inc(bvc_in, 16)
                load_x(1)
                sp.dma_start(sh_n, shared_W.rearrange("(j p) i -> p j i", p=P)).then_inc(sh_in, 16)
                sp.dma_start(gate_n, gate_W.rearrange("(j p) i -> p j i", p=P)).then_inc(sh_in, 16)
                sp.dma_start(b1_n, b1.rearrange("e (j p) -> (e j) p", p=P)).then_inc(b1_in, 16)
                sp.dma_start(sbb[:, :], shared_b.partition_broadcast(P)).then_inc(b2_in, 16)
                sp.dma_start(lngb[:, 0, :], lng.partition_broadcast(P)).then_inc(b2_in, 16)
                sp.dma_start(lngb[:, 1, :], lnb.partition_broadcast(P)).then_inc(b2_in, 16)
                sp.dma_start(b2b[:, :], b2.rearrange("e d -> (e d)").partition_broadcast(P)).then_inc(b2_in, 16)
            for b in range(2, B):
                load_x(b)
            sp.wait_ge(iota_t, 2)
            sp.dma_start(table.rearrange("(g p) c -> p g c", p=P), tinit[:, :, :]).then_inc(table_init, 16)

            def step(s):
                if not isinstance(s, int):
                    load_w1(s - 3)
                if not isinstance(s, int) or 2 <= s:
                    store_xf(s - 2)
                    for t in range(T):
                        store_u(s - 2, t)
                if not isinstance(s, int):
                    load_w2(s - 3, 0)
            run_steps(sp, step)
            for e in range(EARLY, E):
                load_late(e, 0)
                load_late(e, 1)
            sync_rest(sp)

        @block.gpsimd
        def _(g):
            g.memset(eps[:, 0:1], EPS_LN / SX / SX).then_inc(c_eps, 1)
            g.memset(eps[:, 1:2], EPS_LN * SX * SX).then_inc(c_eps, 1)
            g.memset(eps[:, 2:3], EPS_LN).then_inc(c_eps, 1)
            g.memset(ident32, 0.0).then_inc(c_ident, 1)
            g.memset(ident[:, :], 0.0).then_inc(c_ident, 1)
            g.memset(upper[:, :], 1.0).then_inc(c_upper, 1)
            g.memset(ones32[:, :], 1.0).then_inc(c_ones, 1)
            g.memset(ones16[:, :], 1.0).then_inc(c_ones, 1)
            g.memset(row2048[:, :], SX).then_inc(c_row, 1)
            g.wait_ge(c_ident, 2)
            for i in (ident32, ident[:, :]):
                g.affine_select(out=i, in_=i, compare_op=ALU.not_equal, fill=1.0, base=0,
                                pattern=[[-1, P]], channel_multiplier=1).then_inc(c_ident, 1)
            g.wait_ge(c_upper, 1)
            g.affine_select(out=upper[:, :], in_=upper[:, :], compare_op=ALU.is_gt, fill=0.0, base=0,
                            pattern=[[1, P]], channel_multiplier=-1).then_inc(c_upper, 1)
            g.iota(tinit[:, :, 0:4], [[0, NB * HALVES], [0, 4]], base=0, channel_multiplier=0).then_inc(iota_t, 1)
            g.wait_ge(iota_t, 1)
            g.iota(tinit[:, :, 1], [[P, NB * HALVES]], base=PAIRS, channel_multiplier=1).then_inc(iota_t, 1)

            def low(o, x, h, name, o_free, waits):
                for n, v in waits:
                    g.wait_ge(n, past(v))
                g.tensor_tensor(o, x, h, ALU.subtract).then_inc(name, 1)

            def e_reduce(n, lo, hi):
                g.wait_ge(e_ssq, n)
                settle(g)
                g.partition_all_reduce(etot[:, lo:hi], essq[:, lo:hi], P, bass.bass_isa.ReduceOp.add).then_inc(e_tot, 1)

            def attend(b1_, b2_, prep):
                if b1_ is not None:
                    g.wait_ge(xh_ready, b1_ + 1)
                    g.wait_ge(t1, 2 * b1_)
                    g.tensor_tensor(xhl[:, :, 1, :], xs, xhl[:, :, 0, :], ALU.subtract).then_inc(xl_ready, 1)
                if prep is not None:
                    e_reduce(3 * prep + 2, 0, 2)
                if b1_ is not None:
                    for t in range(T):
                        g.wait_ge(q_h, T * b1_ + t + 1)
                        g.wait_ge(nrm_ps, b1_)
                        g.tensor_tensor(qkl[:, t, :], q32[:, t % 2, :], qkh[:, t, :], ALU.subtract).then_inc(q_l, 1)
                        if t:
                            g.wait_ge(sq_t, T * b1_ + t + 1)
                            g.wait_ge(sq_acc, past((T - 1) * b1_ + t - 1))
                            g.tensor_tensor(sqa, sqa, sqt, ALU.add).then_inc(sq_acc, 1)
                if prep is not None:
                    e_reduce(3 * prep + 3, 2, 3)
                if b2_ is not None:
                    g.wait_ge(xfh_ready, b2_ + 1)
                    g.wait_ge(t3, 2 * b2_)
                    g.wait_ge(xf_out, 16 * b2_)
                    g.tensor_tensor(xfhl[:, :, 1, :], z, xfhl[:, :, 0, :], ALU.subtract).then_inc(xfl_ready, 1)

            def step(s):
                b1_, b2_, b3_, e = parts(s)
                attend(b1_, b2_, e)
            run_steps(g, step)
            gpsimd_rest(g)

        @block.tensor
        def _(pe):
            pe.wait_ge(c_ones, 2)
            pe.wait_ge(ssq_ready, 6)
            pe.matmul(NB5[:, 0:6], ones32[:, :], ssq[:, 0:6], start=True, stop=True)
            pe.wait_ge(bvc_in, 32)
            pe.matmul(NB5[:, 8:8 + NF], ones32[:, :], bvc[:, :], start=True, stop=True).then_inc(ssq_sum, 1)
            pe.wait_ge(c_ident, 4)
            for i in range(NF):
                for j in range(2 * NF):
                    mm = pe.transpose(TP[i][:, j * P:(j + 1) * P], wqk_n[:, j, i * P:(i + 1) * P], ident32)
            mm.then_inc(wqk_t, 1)
            for i in range(NF):
                for l in range(NF):
                    mm = pe.matmul(SB6[:, i:i + 1], wv_n[:, l, i * P:(i + 1) * P], ones32[:, 0:1], start=(l == 0), stop=(l == NF - 1))
            mm.then_inc(vs_ps, 1)
            pe.wait_ge(b1_in, 16)
            pe.transpose(QB[0][:, 0:E * NH], b1_n, ident32[0:E * NH, 0:E * NH]).then_inc(b1_t, 1)

            def transposes(b, src, name, f, bank):
                for t in range(T):
                    for k in range(2):
                        mm = pe.transpose(bank[:, :].bitcast(F16)[:, (k * T + t) * P:(k * T + t + 1) * P],
                                          src[:, t, k, f * P:(f + 1) * P], ident[:, :])
                mm.then_inc(name, 1)

            def scores(b):
                pe.wait_ge(z_mul, 2 * b)
                pe.wait_ge(row_set, 2 * b)
                for t in range(T):
                    pe.wait_ge(q_l, T * b + t + 1)
                    for lt in range(NF):
                        cs = slice(D + lt * P, D + (lt + 1) * P)
                        mm = mm3(pe, (GB[:, 0:D], NB5[:, D:2 * D])[lt], qkh[:, t, cs], qkl[:, t, cs], qkh[:, t, 0:D], qkl[:, t, 0:D],
                                 t == 0, t == T - 1)
                mm.then_inc(g_ps, 1)
                pe.wait_ge(sq_acc, past((T - 1) * (b + 1)))
                for c in range(2 * NF):
                    pe.matmul(SB6[:, c:c + 1], sqa[:, c * P:(c + 1) * P], ones32[:, 0:1], start=True, stop=True)
                for c in range(NF):
                    for t in range(T):
                        pe.matmul(SB6[:, 4 + c:5 + c], qkh[:, t, c * P:(c + 1) * P], ones16[:, 0:1], start=(t == 0), stop=False)
                        mm = pe.matmul(SB6[:, 4 + c:5 + c], qkl[:, t, c * P:(c + 1) * P], ones16[:, 0:1], start=False, stop=(t == T - 1))
                mm.then_inc(nrm_ps, 1)

            def spread_rows(b, src, cols, need, name):
                pe.wait_ge(need[0], need[1])
                for c in range(NF):
                    mm = pe.matmul(NB5[:, cols + c * P:cols + (c + 1) * P], ones32[:, :], src[:, c, :], start=True, stop=True)
                mm.then_inc(name, 1)

            def shared_turn(b):
                pe.wait_ge(u_ready, T * b)
                pe.wait_ge(lg_ready, T * b)
                pe.wait_ge(xfh_ready, b + 1)
                pe.wait_ge(xfl_ready, b + 1)
                for f in range(NF):
                    transposes(b, xfhl, t3, f, TP[f])

            def shared(b, tiles):
                pe.wait_ge(xfT_ready, 2 * (b + 1))
                for t in tiles:
                    pe.wait_ge(u_ready, past(T * b + t - 1))
                    pe.wait_ge(lg_ready, past(T * b + t - 1))
                    for f in range(NF):
                        ts = slice(t * P, (t + 1) * P)
                        mm = mm3(pe, TP[t % 2][:, 0:D + E], xfT[:, f, 0, ts], xfT[:, f, 1, ts], sgs[:, f, 0, :], sgs[:, f, 1, :],
                                 f == 0, f == NF - 1)
                    mm.then_inc(sh_ps, 1)

            def turn_x(b):
                pe.wait_ge(xl_ready, b + 1)
                pe.wait_ge(q_ev, T * b)
                for f in range(NF):
                    transposes(b, xhl, t1, f, QB[f])

            def sums(b):
                pe.wait_ge(g32_ready, NF * (b + 1))
                for c in range(NF):
                    for l in range(NF):
                        pe.matmul(SB6[:, 6 + c:7 + c], gk[:, l, c * P:(c + 1) * P], ones32[:, 0:1], start=(l == 0), stop=(l == NF - 1))
                for l in range(NF):
                    mm = pe.matmul(SB6[:, D:2 * D], bvb[:, l, :], gk[:, l, :], start=(l == 0), stop=(l == NF - 1))
                mm.then_inc(sum_ps, 1)

            def project(b, t):
                if t == 0:
                    pe.wait_ge(xT_ready, 2 * (b + 1))
                pe.wait_ge(q_ev, past(T * b + t - 1))
                for f in range(NF):
                    mm = mm3(pe, QB[t % 2][:, :], xTt(b, f, 0, t), xTt(b, f, 1, t), wqkT[:, f, 0, :], wqkT[:, f, 1, :], f == 0, f == NF - 1)
                mm.then_inc(qk_ps, 1)

            def mix(b):
                pe.wait_ge(gh_ready, b + 1)
                pe.wait_ge(gl_ready, b + 1)
                for i in range(NF):
                    for l in range(NF):
                        mm = mm3(pe, MB[:, i * D:(i + 1) * D], wvs[:, l, 0, i * P:(i + 1) * P], wvs[:, l, 1, i * P:(i + 1) * P],
                                 ghl[:, 0, l, :], ghl[:, 1, l, :], l == 0, l == NF - 1)
                mm.then_inc(m_ps, 1)

            def values(b):
                pe.wait_ge(mh_ready, b + 1)
                pe.wait_ge(ml_ready, b + 1)
                pe.wait_ge(rl_ready, b + 1)
                for t in range(T):
                    o = (GB, MB)[t // 2][:, (t % 2) * D:(t % 2 + 1) * D]
                    for f in range(NF):
                        mm3(pe, o, xTt(b, f, 0, t), xTt(b, f, 1, t), mhl[:, 0, f, :], mhl[:, 1, f, :], f == 0, False)
                    for k in range(2):
                        mm = pe.matmul(o, row2048[:, :], rhl[:, k, :], start=False, stop=(k == 1))
                    if t % 2:
                        mm.then_inc(z_ps, 1)

            def step(s):
                b1_, b2_, b3_, e = parts(s)
                if b2_ is not None:
                    spread_rows(b2_, dgq, 0, (dq_ready, NF * (b2_ + 1)), rqb_ps)
                if b3_ is not None:
                    shared_turn(b3_)
                if b2_ is not None:
                    sums(b2_)
                    mix(b2_)
                if b3_ is not None:
                    shared(b3_, range(0, 2))
                if b1_ is not None:
                    turn_x(b1_)
                if b2_ is not None:
                    spread_rows(b2_, dgt, D, (dt_ready, NF * (b2_ + 1)), tgb_ps)
                if b1_ is not None:
                    project(b1_, 0)
                    project(b1_, 1)
                if b3_ is not None:
                    shared(b3_, range(2, T))
                if b1_ is not None:
                    project(b1_, 2)
                    project(b1_, 3)
                if b2_ is not None:
                    values(b2_)
                if b1_ is not None:
                    scores(b1_)
            pe.wait_ge(wqk_h, NF)
            pe.wait_ge(wqk_l, NF)
            pe.wait_ge(b1_ready, 1)
            pe.wait_ge(wv_l, 1)
            pe.wait_ge(sg_l, 2)
            pe.wait_ge(setup_v, SETUP_V)
            run_steps(pe, step)
            tensor_rest(pe)

        @block.scalar
        def _(a):
            a.wait_ge(c_eps, 3)
            a.preload_act_table(ACT.Sqrt)
            link = chain(a, ssq_ready, 0)
            dump = xfhl.rearrange("p t k d -> p (t k d)")
            a.wait_ge(wqk_in, 64)
            link(a.activation(dump[:, 0:4 * D], wqk_n.rearrange("p j i -> p (j i)"), ACT.Square, accum_out=ssq[:, 0:1]))
            a.wait_ge(bias_in, 32)
            link(a.activation(dump[:, 0:2 * D], bqk, ACT.Square, accum_out=ssq[:, 5:6]))
            a.wait_ge(wv_in, 16)
            link(a.activation(dump[:, 0:2 * D], wv_n.rearrange("p j i -> p (j i)"), ACT.Square, accum_out=ssq[:, 1:2]))
            a.wait_ge(bvc_in, 32)
            link(a.activation(dump[:, 0:NF], bvc[:, :], ACT.Square, accum_out=ssq[:, 4:5]))
            a.wait_ge(sh_in, 32)
            link(a.activation(dump[:, 0:2 * D], sh_n.rearrange("p j i -> p (j i)"), ACT.Square, accum_out=ssq[:, 2:3]))
            link(a.activation(dump[:, 0:NF * E], gate_n.rearrange("p j i -> p (j i)"), ACT.Square, accum_out=ssq[:, 3:4]))
            a.wait_ge(setup_v, 10)
            a.activation(scl[:, 0:6], bnd[:, 0:6], ACT.Sqrt, scale=TOP * TOP).then_inc(setup_a, 1)
            a.wait_ge(setup_v, 11)
            a.wait_ge(wqk_t, 1)
            for i in range(NF):
                a.activation(wqkT[:, i, 0, :], TP[i][:, :], ACT.Copy, scale=scl[:, 0:1]).then_inc(wqk_h, 1)
            a.activation(wvs[:, :, 0, :], wv_n, ACT.Copy, scale=scl[:, 2:3]).then_inc(wv_h, 1)
            a.activation(sgs[:, :, 0, 0:D], sh_n, ACT.Copy, scale=scl[:, 4:5]).then_inc(sg_h, 1)
            a.activation(sgs[:, :, 0, D:D + E], gate_n, ACT.Copy, scale=scl[:, 5:6]).then_inc(sg_h, 1)
            a.wait_ge(b1_t, 1)
            a.activation(b1T[:, :], QB[0][:, 0:E * NH], ACT.Copy).then_inc(b1_ready, 1)
            a.wait_ge(b1_ready, 1)

            def spread(which, name, need, epsc, scale):
                a.wait_ge(need[0], need[1])
                settle(a)
                a.activation(sd[:, which, :], mv[:, which, :, 1], ACT.Sqrt, bias=eps[:, epsc:epsc + 1], scale=scale).then_inc(name, 1)

            def e_squares(e, which):
                if which == 0:
                    a.wait_ge(w1_in, 16 * (e + 1))
                    if not isinstance(e, int):
                        a.wait_ge(e_tab, 2 * e)
                    settle(a)
                    a.activation(w1_part(e, 0), stage1, ACT.Square, accum_out=essq[:, 0:1]).then_inc(e_ssq, 1)
                    settle(a)
                    a.activation(bsq[:, :], b1T[:, bass.ds(e * NH, NH)], ACT.Square, accum_out=essq[:, 1:2]).then_inc(e_ssq, 1)
                    a.wait_ge(e_ssq, 3 * e + 2)
                else:
                    a.wait_ge(w2_in, 16 * (e + 1))
                    settle(a)
                    a.activation(w2_part(e, 0), stage2(e), ACT.Square, accum_out=essq[:, 2:3]).then_inc(e_ssq, 1)
                    a.wait_ge(e_ssq, 3 * e + 3)

            def e_scales(e, which):
                lo, hi = ((0, 2), (2, 3))[which]
                a.wait_ge(e_v, EV * e + (EV1A, EV2A)[which])
                settle(a)
                a.activation(escl[:, lo:hi], ebnd[:, lo:hi], ACT.Sqrt, scale=TOP * TOP).then_inc(e_a, 1)

            def e_high(e, which):
                a.wait_ge(e_tab, 2 * e + which + 1)
                src, part = ((stage1, w1_part(e, 0)), (stage2(e), w2_part(e, 0)))[which]
                settle(a)
                a.activation(part, src, ACT.Copy, scale=escl[:, 2 * which:2 * which + 1]).then_inc(w_hi, 1)

            def norms(b):
                a.wait_ge(nrm_ps, b + 1)
                settle(a)
                a.activation(kn[:, :], SB6[:, 0:4], ACT.Sqrt).then_inc(nsq, 1)

            def row_out(b, cols, need, n, k):
                a.wait_ge(need, b + 1)
                for m, c in n:
                    a.wait_ge(m, past(c))
                settle(a)
                a.activation(colrow, NB5[:, cols:cols + D], ACT.Copy).then_inc(row_set, 1)

            def turned(b, dst, bank, t_name, name, extra):
                a.wait_ge(t_name, 2 * b + 1)
                for n, v in extra:
                    a.wait_ge(n, past(v))
                settle(a)
                a.activation(dst, bank[:, :].bitcast(F16), ACT.Copy).then_inc(name, 1)

            def g_high(b):
                a.wait_ge(g32_ready, NF * (b + 1))
                a.wait_ge(m_ps, b)
                settle(a)
                a.activation(ghl[:, 0, :, :], gk, ACT.Copy).then_inc(gh_ready, 1)

            def x_high(b):
                a.wait_ge(xs_ready, T * (b + 1))
                a.wait_ge(t1, 2 * b)
                settle(a)
                a.activation(xhl[:, :, 0, :], xs, ACT.Copy).then_inc(xh_ready, 1)

            def q_high(b, t):
                a.wait_ge(q_ev, T * b + t + 1)
                a.wait_ge(nrm_ps, b)
                settle(a)
                a.activation(qkh[:, t, :], q32[:, t % 2, :], ACT.Copy).then_inc(q_h, 1)
                if t:
                    a.wait_ge(sq_acc, past((T - 1) * b + t - 1))
                settle(a)
                a.activation(sqt if t else sqa, q32[:, t % 2, :], ACT.Square).then_inc(sq_t, 1)

            def m_high(b):
                a.wait_ge(m_ps, b + 1)
                a.wait_ge(ml_ready, b)
                for i in range(NF):
                    settle(a)
                    a.activation(m32[:, i, :], MB[:, i * D:(i + 1) * D], ACT.Identity, bias=vsum[:, i:i + 1], scale=der[:, 1:2]).then_inc(m32_ready, 1)
                a.wait_ge(m32_ready, 2 * (b + 1))
                a.wait_ge(z_ps, 2 * b)
                settle(a)
                a.activation(mhl[:, 0, :, :], m32, ACT.Copy).then_inc(mh_ready, 1)

            def xf_high(b):
                a.wait_ge(xf_ready, T * (b + 1))
                a.wait_ge(t3, 2 * b)
                a.wait_ge(xf_out, 16 * b)
                settle(a)
                a.activation(xfhl[:, :, 0, :], z, ACT.Copy).then_inc(xfh_ready, 1)

            def step(s):
                b1_, b2_, b3_, e = parts(s)
                if b2_ is not None:
                    row_out(b2_, 0, rqb_ps, [(z_mul, 2 * b2_)], 1)
                if b1_ is not None:
                    spread(0, sd1, (mv1, T * (b1_ + 1)), 0, 1.0 / SX / SX)
                if b2_ is not None:
                    g_high(b2_)
                if b1_ is not None:
                    x_high(b1_)
                if b3_ is not None:
                    turned(b3_, xfT[:, 0, :, :].rearrange("p k c -> p (k c)"), TP[0], t3, xfT_ready, [(sh_ps, T * b3_)])
                if e is not None:
                    e_squares(e, 0)
                if b2_ is not None:
                    m_high(b2_)
                if b1_ is not None:
                    turned(b1_, xTf(b1_, 0), QB[0], t1, xT_ready, [(z_ps, 2 * (b1_ - 1))])
                if b2_ is not None:
                    row_out(b2_, D, tgb_ps, [(g32_ready, NF * (b2_ + 1))], 2)
                if e is not None:
                    e_scales(e, 0)
                if b1_ is not None:
                    q_high(b1_, 0)
                if e is not None:
                    e_high(e, 0)
                if b1_ is not None:
                    for t in range(1, T):
                        q_high(b1_, t)
                if b2_ is not None:
                    spread(1, sd2, (mv2, T * (b2_ + 1)), 1, 1.0)
                if e is not None:
                    e_squares(e, 1)
                    e_scales(e, 1)
                if b2_ is not None:
                    spread(2, sd3, (mv3, T * (b2_ + 1)), 0, 1.0 / SX / SX)
                if e is not None:
                    e_high(e, 1)
                if b2_ is not None:
                    xf_high(b2_)
                if b1_ is not None:
                    norms(b1_)
            a.wait_ge(table_init, 16)
            run_steps(a, step)
            a.wait_ge(zone_free, 1)
            a.wait_ge(exp_max, 1)
            a.activation(probs, probs, ACT.Exp).then_inc(exp_ready, 1)
            a.preload_act_table(ACT.Sqrt)
            pieces = [(e, which) for e in range(EARLY, E) for which in range(2)]
            e_squares(*pieces[0])
            for i in range(len(pieces)):
                if i + 1 < len(pieces):
                    e, which = pieces[i + 1]
                    a.wait_ge(e_tot, past(2 * e - 1 + which))
                    e_squares(e, which)
                e_scales(*pieces[i])
                e_high(*pieces[i])
            scalar_rest(a)

        @block.vector
        def _(v):
            link = chain(v, setup_v, 0)
            v.wait_ge(ssq_ready, 6)
            v.wait_ge(ssq_sum, 1)
            tot = NB5
            link(v.tensor_copy(bnd[:, 0:1], tot[:, 0:1]))
            link(v.scalar_tensor_tensor(bnd[:, 1:2], tot[:, 0:1], float(D), ssq[:, 5:6], ALU.mult, ALU.add))
            link(v.tensor_scalar(bnd[:, 1:2], bnd[:, 1:2], 2.0, None, ALU.mult))
            link(v.tensor_copy(bnd[:, 2:3], tot[:, 1:2]))
            link(v.tensor_copy(bnd[:, 3:4], tot[:, 1:2]))
            link(v.scalar_tensor_tensor(bnd[:, 3:4], tot[:, 4:5], 1.0, bnd[:, 3:4], ALU.mult, ALU.add))
            link(v.tensor_scalar(bnd[:, 3:4], bnd[:, 3:4], 8.0 * D, None, ALU.mult))
            link(v.tensor_copy(bnd[:, 4:6], tot[:, 2:4]))
            link(v.tensor_scalar(bnd[:, 0:6], bnd[:, 0:6], 1e-24, None, ALU.max))
            link(v.reciprocal(bnd[:, 0:6], bnd[:, 0:6]))
            v.wait_ge(setup_a, 1)
            link(v.tensor_scalar(scl[:, 0:6].bitcast(I32), scl[:, 0:6].bitcast(I32), EXP_MASK, None, ALU.bitwise_and))
            link(v.tensor_scalar(inv[:, 0:6].bitcast(I32), scl[:, 0:6].bitcast(I32), -1.0, EXP_FLIP, ALU.mult, ALU.add))
            link(v.scalar_tensor_tensor(der[:, 0:1], scl[:, 1:2], 1.0 / SX, inv[:, 0:1], ALU.mult, ALU.mult))
            link(v.scalar_tensor_tensor(der[:, 1:2], scl[:, 3:4], 1.0 / SG, inv[:, 2:3], ALU.mult, ALU.mult))
            v.wait_ge(bvc_in, 32)
            link(v.tensor_tensor(der[:, 2:3], gam_b[:, :], inv[:, 3:4], ALU.mult))
            link(v.tensor_scalar(der[:, 3:5], inv[:, 4:6], 1.0 / SX, None, ALU.mult))
            link(v.tensor_scalar(der[:, 5:6], scl[:, 3:4], 1.0 / SG, None, ALU.mult))
            link(v.tensor_copy(der[:, 7:8], tot[:, 8:9]))
            link(v.scalar_tensor_tensor(der[:, 6:7], tot[:, 9:10], 1.0, der[:, 7:8], ALU.mult, ALU.add))
            link(v.tensor_tensor(der[:, 6:7], der[:, 6:7], scl[:, 3:4], ALU.mult))
            v.wait_ge(vs_ps, 1)
            link(v.tensor_scalar(vsum, SB6[:, 0:NF], scl[:, 3:4], None, ALU.mult))
            link(v.tensor_scalar(bqk, bqk, scl[:, 1:2], None, ALU.mult))
            link(v.tensor_copy(bvb, bvc[:, :].unsqueeze(2).broadcast_to([P, NF, P])))
            assert link.count[0] == SETUP_V
            for i in range(NF):
                v.wait_ge(wqk_h, i + 1)
                v.scalar_tensor_tensor(wqkT[:, i, 1, :], TP[i][:, :], scl[:, 0:1], wqkT[:, i, 0, :], ALU.mult, ALU.subtract).then_inc(wqk_l, 1)
            v.wait_ge(wv_h, 1)
            v.scalar_tensor_tensor(wvs[:, :, 1, :], wv_n, scl[:, 2:3], wvs[:, :, 0, :], ALU.mult, ALU.subtract).then_inc(wv_l, 1)
            v.wait_ge(sg_h, 2)
            v.scalar_tensor_tensor(sgs[:, :, 1, 0:D], sh_n, scl[:, 4:5], sgs[:, :, 0, 0:D], ALU.mult, ALU.subtract).then_inc(sg_l, 1)
            v.scalar_tensor_tensor(sgs[:, :, 1, D:D + E], gate_n, scl[:, 5:6], sgs[:, :, 0, D:D + E], ALU.mult, ALU.subtract).then_inc(sg_l, 1)
            v.wait_ge(b2_in, 64)

            def bank_tiles(bank):
                return bank[:, :].rearrange("p (t d) -> p t d", d=D)

            def stats(which, b, src, src_ready, st_name, mv_name):
                for t in range(T):
                    for n, c in src_ready(t):
                        v.wait_ge(n, past(c))
                    settle(v)
                    v.bn_stats(st[:, which, t, :], src(t)).then_inc(st_name, 1)
                for t in range(T):
                    v.wait_ge(st_name, T * b + t + 1)
                    settle(v)
                    v.bn_aggr(mv[:, which, t, :], st[:, which, t, :]).then_inc(mv_name, 1)

            def enter_stats(b):
                stats(0, b, lambda t: Xt(b, t), lambda t: [(x_loaded, 16 * (b + 1))], st1, mv1)

            def enter(b):
                v.wait_ge(sd1, b + 1)
                v.reciprocal(a1[:, bass.ds(b * T, T)], sd[:, 0, :]).then_inc(a1_ready, 1)
                v.wait_ge(a1_ready, b + 1)
                v.scalar_tensor_tensor(cf[:, 0, :], mv[:, 0, :, 0], -1.0, a1[:, bass.ds(b * T, T)], ALU.mult, ALU.mult).then_inc(c1_ready, 1)
                v.wait_ge(c1_ready, b + 1)
                v.wait_ge(xh_ready, b)
                v.wait_ge(xl_ready, b)
                for t in range(T):
                    v.tensor_scalar(xs[:, t, :], Xt(b, t), a1[:, bass.ds(b * T + t, 1)], cf[:, 0, t:t + 1], ALU.mult, ALU.add).then_inc(xs_ready, 1)

            def turned(b, dst, bank, t_name, name, extra):
                v.wait_ge(t_name, 2 * b + 2)
                for n, c in extra:
                    v.wait_ge(n, past(c))
                v.tensor_copy(dst, bank[:, :].bitcast(F16)).then_inc(name, 1)

            def norms(b):
                v.wait_ge(nsq, b + 1)
                v.reciprocal(rk[:, :], kn[:, :]).then_inc(rk_ready, 1)
                v.wait_ge(rk_ready, b + 1)
                v.tensor_scalar(dn[:, 2:4], rk[:, 0:2], SG, None, ALU.mult).then_inc(rqs_ready, 1)
                v.wait_ge(rqs_ready, b + 1)
                for c in range(NF):
                    v.tensor_scalar(dgq[:, c, :], ident32, dn[:, 2 + c:3 + c], None, ALU.mult).then_inc(dq_ready, 1)

            def cosines(b):
                v.wait_ge(row_set, 2 * b + 1)
                for l in range(NF):
                    v.scalar_tensor_tensor(gk[:, l, :], (GB[:, 0:D], NB5[:, D:2 * D])[l], rk[:, 2 + l:3 + l], colrow, ALU.mult, ALU.mult).then_inc(g32_ready, 1)

            def cosines_low(b):
                v.wait_ge(gh_ready, b + 1)
                v.wait_ge(g32_ready, NF * (b + 1))
                v.tensor_tensor(ghl[:, 1, :, :], gk, ghl[:, 0, :, :], ALU.subtract).then_inc(gl_ready, 1)

            def tailor(b):
                link = chain(v, dchain, DCH * b)
                v.wait_ge(sum_ps, b + 1)
                link(v.scalar_tensor_tensor(dn[:, 0:2], SB6[:, 4:6], EPS_TAILOR, rk[:, 0:2], ALU.mult, ALU.mult))
                link(v.scalar_tensor_tensor(dn[:, 0:2], SB6[:, 6:8], 1.0 / SG, dn[:, 0:2], ALU.mult, ALU.add))
                link(v.tensor_scalar(dn[:, 0:2], dn[:, 0:2], float(D), None, ALU.add))
                link(v.reciprocal(dn[:, 0:2], dn[:, 0:2]))
                link(v.tensor_scalar(dn[:, 0:2], dn[:, 0:2], der[:, 2:3], None, ALU.mult))
                for c in range(NF):
                    v.tensor_scalar(dgt[:, c, :], ident32, dn[:, c:c + 1], None, ALU.mult).then_inc(dt_ready, 1)
                link(v.tensor_scalar(r32, SB6[0:1, D:2 * D], der[0:1, 5:6], der[0:1, 6:7], ALU.mult, ALU.add))
                assert link.count[0] == DCH
                v.wait_ge(z_ps, 2 * b)
                v.tensor_copy(rhl[:, 0, :], r32).then_inc(rh_ready, 1)
                v.wait_ge(rh_ready, b + 1)
                v.tensor_tensor(rhl[:, 1, :], r32, rhl[:, 0, :], ALU.subtract).then_inc(rl_ready, 1)

            def q_out(b, t):
                v.wait_ge(qk_ps, T * b + t + 1)
                v.wait_ge(q_l, past(T * b + t - 1))
                v.wait_ge(sq_t, past(T * b + t - 1))
                v.scalar_tensor_tensor(q32[:, t % 2, :], QB[t % 2][:, :], der[:, 0:1], bqk, ALU.mult, ALU.add).then_inc(q_ev, 1)

            def m_low(b):
                v.wait_ge(mh_ready, b + 1)
                v.wait_ge(z_ps, 2 * b)
                v.tensor_tensor(mhl[:, 1, :, :], m32, mhl[:, 0, :, :], ALU.subtract).then_inc(ml_ready, 1)

            def attended(b):
                v.wait_ge(xfh_ready, b)
                v.wait_ge(xfl_ready, b)
                v.wait_ge(row_set, 2 * b + 2)
                for h in range(2):
                    v.wait_ge(z_ps, 2 * b + h + 1)
                    v.tensor_tensor(z[:, 2 * h:2 * h + 2, :], bank_tiles((GB, MB)[h]), colrow.unsqueeze(1).broadcast_to([P, 2, D]),
                                    ALU.mult).then_inc(z_mul, 1)
                for t in range(T):
                    v.wait_ge(z_mul, 2 * b + t // 2 + 1)
                    v.scalar_tensor_tensor(z[:, t, :], Xt(b, t), a1[:, bass.ds(b * T + t, 1)], z[:, t, :], ALU.mult, ALU.add).then_inc(z_add, 1)
                stats(1, b, lambda t: z[:, t, :], lambda t: [(z_add, T * b + t + 1)], st2, mv2)

            def residual(b):
                v.wait_ge(sd2, b + 1)
                v.reciprocal(cf[:, 1, :], sd[:, 1, :]).then_inc(r2_ready, 1)
                v.wait_ge(r2_ready, b + 1)
                v.scalar_tensor_tensor(c2[:, bass.ds(b * T, T)], mv[:, 1, :, 0], -1.0, cf[:, 1, :], ALU.mult, ALU.mult).then_inc(c2_ready, 1)
                for t in range(T):
                    v.scalar_tensor_tensor(Xt(b, t), z[:, t, :], cf[:, 1, t:t + 1], Xt(b, t), ALU.mult, ALU.add).then_inc(x1_ready, 1)
                stats(2, b, lambda t: Xt(b, t), lambda t: [(x1_ready, T * b + t + 1)], st3, mv3)

            def leave(b):
                v.wait_ge(sd3, b + 1)
                v.reciprocal(cf[:, 2, :], sd[:, 2, :]).then_inc(a3_ready, 1)
                v.wait_ge(a3_ready, b + 1)
                v.scalar_tensor_tensor(c3[:, :], mv[:, 2, :, 0], -1.0, cf[:, 2, :], ALU.mult, ALU.mult).then_inc(c3_ready, 1)
                v.wait_ge(c3_ready, b + 1)
                for t in range(T):
                    v.tensor_scalar(z[:, t, :], Xt(b, t), cf[:, 2, t:t + 1], c3[:, t:t + 1], ALU.mult, ALU.add).then_inc(xf_ready, 1)

            def shared_out(b, tiles):
                for t in tiles:
                    v.wait_ge(sh_ps, T * b + t + 1)
                    v.wait_ge(u_out[t % 2], 16 * (2 * b + t // 2))
                    v.scalar_tensor_tensor(u[:, t % 2, :], TP[t % 2][:, 0:D], der[:, 3:4], sbb[:, :], ALU.mult, ALU.add).then_inc(u_ready, 1)
                    v.tensor_scalar(logit[:, bass.ds(b * T + t, 1), :].rearrange("p a e -> p (a e)"), TP[t % 2][:, D:D + E], der[:, 4:5], None,
                                    ALU.mult).then_inc(lg_ready, 1)

            def e_bounds(e, which):
                link = chain(v, e_v, EV * e + (0, EV1A)[which])
                v.wait_ge(e_tot, 2 * e + which + 1)
                if which == 0:
                    link(v.scalar_tensor_tensor(ebnd[:, 1:2], etot[:, 0:1], float(D), etot[:, 1:2], ALU.mult, ALU.add))
                    link(v.tensor_scalar(ebnd[:, 0:1], etot[:, 0:1], 1e-24, None, ALU.max))
                    link(v.tensor_scalar(ebnd[:, 1:2], ebnd[:, 1:2], 2.0, 1e-24, ALU.mult, ALU.max))
                    link(v.reciprocal(ebnd[:, 0:2], ebnd[:, 0:2]))
                else:
                    link = chain(v, e_v, EV * e + EV1)
                    link(v.tensor_scalar(ebnd[:, 2:3], etot[:, 2:3], 1e-24, None, ALU.max))
                    link(v.reciprocal(ebnd[:, 2:3], ebnd[:, 2:3]))

            def e_tables(e, which):
                lo, hi = ((0, 2), (2, 3))[which]
                v.wait_ge(e_a, 2 * e + which + 1)
                v.tensor_scalar(escl[:, lo:hi].bitcast(I32), escl[:, lo:hi].bitcast(I32), EXP_MASK, None, ALU.bitwise_and).then_inc(e_tab, 1)
                v.wait_ge(e_tab, 2 * e + which + 1)
                link = chain(v, e_v, EV * e + (EV1A, EV2A)[which])
                link(v.tensor_scalar(einv[:, lo:hi].bitcast(I32), escl[:, lo:hi].bitcast(I32), -1.0, EXP_FLIP, ALU.mult, ALU.add))
                if which == 0:
                    link(v.tensor_scalar(tab[:, 0, bass.ds(e, 1)], einv[:, 0:1], 1.0 / SX, None, ALU.mult))
                    link(v.tensor_copy(tab[:, 1, bass.ds(e, 1)], escl[:, 1:2]))
                else:
                    link(v.tensor_tensor(tab[:, 2, bass.ds(e, 1)], einv[:, 2:3], einv[:, 1:2], ALU.mult))

            def e_low(e, which):
                v.wait_ge(w_hi, 2 * e + which + 1)
                if which == 0:
                    v.scalar_tensor_tensor(w1_part(e, 1), stage1, escl[:, 0:1], w1_part(e, 0), ALU.mult, ALU.subtract).then_inc(w_lo, 1)
                else:
                    v.scalar_tensor_tensor(w2_part(e, 1), stage2(e), escl[:, 2:3], w2_part(e, 0), ALU.mult, ALU.subtract).then_inc(w_lo, 1)

            def step(s):
                b1_, b2_, b3_, e = parts(s)
                if b1_ is not None:
                    enter_stats(b1_)
                if b2_ is not None:
                    cosines(b2_)
                if b1_ is not None:
                    enter(b1_)
                if b3_ is not None:
                    turned(b3_, xfT[:, 1, :, :].rearrange("p k c -> p (k c)"), TP[1], t3, xfT_ready, [(sh_ps, T * b3_)])
                if b2_ is not None:
                    cosines_low(b2_)
                    tailor(b2_)
                if b3_ is not None:
                    shared_out(b3_, range(0, 2))
                if b2_ is not None:
                    m_low(b2_)
                if b1_ is not None:
                    turned(b1_, xTf(b1_, 1), QB[1], t1, xT_ready, [(z_ps, 2 * (b1_ - 1))])
                if e is not None:
                    e_bounds(e, 0)
                    e_tables(e, 0)
                if b1_ is not None:
                    q_out(b1_, 0)
                    q_out(b1_, 1)
                if b3_ is not None:
                    shared_out(b3_, range(2, T))
                if b1_ is not None:
                    q_out(b1_, 2)
                    q_out(b1_, 3)
                if e is not None:
                    e_low(e, 0)
                if b2_ is not None:
                    attended(b2_)
                    residual(b2_)
                if e is not None:
                    e_bounds(e, 1)
                    e_tables(e, 1)
                if b2_ is not None:
                    leave(b2_)
                if b1_ is not None:
                    norms(b1_)
                if e is not None:
                    e_low(e, 1)
            run_steps(v, step)
            v.wait_ge(sh_ps, T * B)
            v.wait_ge(z_ps, 2 * B)
            v.wait_ge(xfh_ready, B)
            v.wait_ge(xfl_ready, B)
            v.wait_ge(xf_out, 16 * B)
            v.wait_ge(u_out[0], 16 * B * T // 2)
            v.wait_ge(u_out[1], 16 * B * T // 2)
            v.wait_ge(lg_ready, T * B)
            v.memset(red, 0.0).then_inc(zone_free, 1)
            vector_route(v)

            def late_bounds(e, which):
                lo, hi = ((0, 2), (2, 3))[which]
                v.wait_ge(e_ps, past(2 * (e - EARLY) + which + 1))
                v.tensor_copy(etot[:, lo:hi], MB[:, lo:hi]).then_inc(e_tot, 1)
                e_bounds(e, which)
            pieces = [(e, which) for e in range(EARLY, E) for which in range(2)]
            for i, (e, which) in enumerate(pieces):
                late_bounds(e, which)
                if i:
                    e_low(*pieces[i - 1])
                e_tables(e, which)
            e_low(*pieces[-1])
            vector_rest(v)


_OUT = ((8, 512, 256), "float32")
_INS = ["L0_attn_x", "L0_attn_Wq", "L0_attn_bq", "L0_attn_Wk", "L0_attn_bk", "L0_attn_Wv", "L0_attn_bv", "L0_attn_gamma",
        "L0_ffn_W1", "L0_ffn_b1", "L0_ffn_W2", "L0_ffn_b2", "L0_ffn_gate_W", "L0_ffn_shared_W", "L0_ffn_shared_b",
        "L0_ffn_gamma", "L0_ffn_beta"]


def kernel(**inputs):
    import numpy as _np
    import concourse.bacc as _bacc
    from concourse import mybir as _mybir
    from concourse.bass_utils import run_bass_kernel_spmd as _run

    nc = _bacc.Bacc("TRN2", target_bir_lowering=False, num_devices=1)
    arrays, args = {}, []
    for name in _INS:
        a = _np.ascontiguousarray(inputs[name])
        arrays[f"in_{name}"] = a
        args.append(nc.dram_tensor(f"in_{name}", a.shape, _mybir.dt.from_np(a.dtype), kind="ExternalInput").ap())
    args.append(nc.dram_tensor("out_0", _OUT[0], _mybir.dt.from_np(_np.dtype(_OUT[1])), kind="ExternalOutput").ap())
    sandwich(nc, *args)
    r = _run(nc, [arrays], core_ids=[0])
    return r.results[0]["out_0"]
```

```python
from contextlib import ExitStack

import concourse.bass as bass
from concourse import mybir
from concourse.alu_op_type import AluOpType as ALU

ACT = mybir.ActivationFunctionType
AX = mybir.AxisListType
F32 = mybir.dt.float32
F16 = mybir.dt.float16
I32 = mybir.dt.int32

P = 128
EPS_LN = 1e-5
EPS_TAILOR = 1e-6
SX = 2048.0
SG = 16384.0
TOP = 32768.0
ROUTE = 312
PICKS, PLACES = 11, 16
TAILOR = 6
SETUP_V = 23
EV1A, EV1, EV2A, EV = 4, 7, 9, 11
EXP_MASK = 0x7F800000
EXP_FLIP = float(0x7F000000)
BT = 256
HALVES = BT // P


def sandwich(nc, x_in, Wq, bq, Wk, bk, Wv, bv, gam, W1, b1, W2, b2, gate_W, shared_W, shared_b, lng, lnb, out):
    B, C, D = x_in.shape
    E, _, H = W1.shape
    T = C // P
    NF = D // P
    NH = H // P
    TOK = B * C
    NG = TOK // P
    NB = 2 * TOK // BT + E - 1
    PAIRS = 2 * TOK
    RB = TOK // BT
    SLOTS = (E * RB + NB - 2 * TOK // BT) * BT
    PAD_COLS = SLOTS // P
    EARLY = 5
    WE = 2 * NF * H + 2 * NH * D

    def dram(name, shape, dt):
        return nc.dram_tensor(name, shape, dt).ap()

    xf_rows = dram("xf_rows", [TOK, 2 * D], F16)
    u_rows = dram("u_rows", [TOK, D], F32)
    table = dram("table", [SLOTS, 4], I32)
    y_rows = dram("y_rows", [PAIRS + SLOTS, D], F32)

    ctx = ExitStack()
    with ctx:
        def sb(name, shape, dt):
            return ctx.enter_context(nc.sbuf_tensor(name, shape, dt))

        def sem(name):
            return ctx.enter_context(nc.semaphore(name))

        W = sb("W", [P, E * WE], F16)
        X = sb("X", [P, NG, D], F32)
        stage = sb("stage", [P, 4096], F32)
        zone = sb("zone", [P, 4096], F32)
        b2b = sb("b2b", [P, E * D], F32)
        lngb = sb("lngb", [P, 2, D], F32)
        sbb = sb("sbb", [P, D], F32)
        ident = sb("ident", [P, P], F16)
        upper = sb("upper", [P, P], F16)
        ones32 = sb("ones32", [P, P], F32)
        row2048 = sb("row2048", [1, P], F16)
        logit = sb("logit", [P, T, E], F32)[:, :, :]
        rank = sb("rank", [P, T, E], F32)[:, :, :]
        pick = [sb(f"pick{k}", [P, T, E], F32)[:, :, :] for k in range(2)]
        below = sb("below", [P, T, E], F32)[:, :, :]
        counts = sb("counts", [P, (T + 1) * E], F32)[:, :]
        block_at = sb("block_at", [P, NB + 1], I32)
        b1T = sb("b1T", [P, E * NH], F32)
        eps = sb("eps", [P, 3], F32)
        gam_b = sb("gam_b", [P, 1], F32)
        bvc = sb("bvc", [P, NF], F32)
        a1 = sb("a1", [P, NG], F32)
        c2 = sb("c2", [P, NG], F32)
        st = sb("st", [P, 3, T, 6], F32)
        mv = sb("mv", [P, 3, T, 2], F32)
        sd = sb("sd", [P, 3, T], F32)
        cf = sb("cf", [P, 3, T], F32)
        c3 = sb("c3", [P, T], F32)
        kn = sb("kn", [P, 4], F32)
        rk = sb("rk", [P, 4], F32)
        dn = sb("dn", [P, 4], F32)
        ssq = sb("ssq", [P, 8], F32)
        bnd = sb("bnd", [P, 8], F32)
        scl = sb("scl", [P, 8], F32)
        inv = sb("inv", [P, 8], F32)
        der = sb("der", [P, 16], F32)
        essq = sb("essq", [P, 4], F32)
        etot = sb("etot", [P, 4], F32)
        ebnd = sb("ebnd", [P, 4], F32)
        escl = sb("escl", [P, 4], F32)
        einv = sb("einv", [P, 4], F32)
        tab = sb("tab", [P, 3, E], F32)
        slot_i = sb("slot_i", [P, 2, T], I32)
        ej_i = sb("ej_i", [P, NB + 1], I32)
        tb = sb("tb", [P, 2, HALVES, 4], I32)
        tsc = sb("tsc", [P, 2, HALVES, 4], I32)

        class Carver:
            def __init__(self, pools):
                self.pools = [list(p) for p in pools]

            def __call__(self, shape, dt):
                n = 1
                for s in shape[1:]:
                    n *= s
                words = (n * (2 if dt == F16 else 4) + 3) // 4
                words = (words + 7) // 8 * 8
                for p in self.pools:
                    if p[1] + words <= p[2]:
                        at = p[1]
                        p[1] += words
                        v = p[0][:, at:at + words]
                        if dt != F32:
                            v = v.bitcast(dt)
                        v = v[0:shape[0], 0:n]
                        if len(shape) == 3:
                            v = v.rearrange("p (a b) -> p a b", b=shape[2])
                        if len(shape) == 4:
                            v = v.rearrange("p (a b c) -> p a b c", b=shape[2], c=shape[3])
                        return v
                raise ValueError("no room")

        ones16 = sb("ones16", [P, P], F16)
        bsq = sb("bsq", [P, NH], F32)
        tinit = W[:, 0:PAD_COLS * 8].bitcast(I32).rearrange("p (g c) -> p g c", c=4)
        late = W[:, EARLY * WE:E * WE].bitcast(F32)
        attention_buf = Carver([(late, 0, (E - EARLY) * WE // 2), (zone, 0, 4096 - ROUTE), (stage, 2048, 4096)])
        routing_buf = Carver([(zone, 4096 - ROUTE, 4096)])
        xhl = attention_buf([P, T, 2, D], F16)
        xs = attention_buf([P, T, D], F32)
        xT = attention_buf([P, 2 * 2 * NF * C], F16)
        q32 = attention_buf([P, 2, 2 * D], F32)
        qkh = attention_buf([P, T, 2 * D], F16)
        qkl = attention_buf([P, T, 2 * D], F16)
        z = attention_buf([P, T, D], F32)
        xfhl = attention_buf([P, T, 2, D], F16)
        xfT = attention_buf([P, NF, 2, C], F16)
        wqkT = attention_buf([P, NF, 2, 2 * D], F16)
        sqt = attention_buf([P, 2 * D], F32)
        sqa = attention_buf([P, 2 * D], F32)
        gk = attention_buf([P, NF, D], F32)
        ghl = attention_buf([P, 2, NF, D], F16)
        m32 = attention_buf([P, NF, D], F32)
        mhl = attention_buf([P, 2, NF, D], F16)
        wvs = attention_buf([P, NF, 2, D], F16)
        sgs = attention_buf([P, NF, 2, D + E], F16)
        bqk = attention_buf([P, 2 * D], F32)
        u = attention_buf([P, 2, D], F32)
        bvb = attention_buf([P, NF, P], F32)
        dgq = attention_buf([P, NF, P], F32)
        dgt = dgq
        colrow = attention_buf([P, D], F32)
        r32 = attention_buf([1, D], F32)
        rhl = attention_buf([1, 2, D], F16)
        gate_n = attention_buf([P, NF, E], F32)
        vsum = attention_buf([P, NF], F32)
        ident32 = attention_buf([P, P], F32)
        match = routing_buf([P, T, E], F32)
        both = routing_buf([P, T, E], F16)
        four = routing_buf([P, T, 4], F32)
        two = routing_buf([P, T, 2], F32)
        best = [routing_buf([P, T], F32) for _ in range(2)]
        red = routing_buf([P, T], F32)
        gap = routing_buf([P, T], F32)
        second = routing_buf([P, T], F32)
        total = routing_buf([P, T], F32)
        share = routing_buf([P, T], F32)
        slot_f = routing_buf([P, T], F32)
        by_expert = routing_buf([P, T, E], F32)
        place_of = routing_buf([P, E], F32)
        number = routing_buf([P, T, 2, 2], F32)
        ahead = routing_buf([P, T, 2, 2], F32)
        pay = routing_buf([P, T, 2, 4], I32)

        PS = [ctx.enter_context(nc.psum_tensor(f"bank{i}", [P, 512], F32)) for i in range(8)]
        TURN_PS = [PS[0], PS[1]]
        QK_PS = [PS[2], PS[3]]
        SCORE_PS, ROWS_PS, SUMS_PS, MIX_PS = PS[4], PS[5], PS[6], PS[7]

        x_loaded = sem("x_loaded")
        qk_bias_in = sem("qk_bias_in")
        row_biases_in = sem("row_biases_in")
        b1_in = sem("b1_in")
        wqk_in = sem("wqk_in")
        wv_in = sem("wv_in")
        shared_in = sem("shared_in")
        bv_in = sem("bv_in")
        eps_set = sem("eps_set")
        ones_set = sem("ones_set")
        row_set_once = sem("row_set_once")
        identity_set = sem("identity_set")
        upper_set = sem("upper_set")
        setup_squares = sem("setup_squares")
        setup_sums = sem("setup_sums")
        setup_steps = sem("setup_steps")
        setup_roots = sem("setup_roots")
        wqk_turned = sem("wqk_turned")
        wqk_high = sem("wqk_high")
        wqk_low = sem("wqk_low")
        wv_high = sem("wv_high")
        wv_low = sem("wv_low")
        shared_high = sem("shared_high")
        shared_low = sem("shared_low")
        wv_sums_ps = sem("wv_sums_ps")
        b1_turned = sem("b1_turned")
        b1_ready = sem("b1_ready")
        w1_in = sem("w1_in")
        w2_in = sem("w2_in")
        expert_squares = sem("expert_squares")
        expert_sums = sem("expert_sums")
        expert_sums_ps = sem("expert_sums_ps")
        expert_steps = sem("expert_steps")
        expert_roots = sem("expert_roots")
        expert_scales = sem("expert_scales")
        w_high = sem("w_high")
        w_low = sem("w_low")
        enter_stats_t = sem("enter_stats_t")
        enter_mean = sem("enter_mean")
        enter_dev = sem("enter_dev")
        enter_factor = sem("enter_factor")
        enter_shift = sem("enter_shift")
        xs_ready = sem("xs_ready")
        x_high_ready = sem("x_high_ready")
        x_low_ready = sem("x_low_ready")
        x_turned = sem("x_turned")
        xT_ready = sem("xT_ready")
        qk_ps = sem("qk_ps")
        qk_out = sem("qk_out")
        qk_high = sem("qk_high")
        qk_squares = sem("qk_squares")
        qk_low = sem("qk_low")
        squares_added = sem("squares_added")
        scores_ps = sem("scores_ps")
        norms_ps = sem("norms_ps")
        norms_ready = sem("norms_ready")
        norm_inverses = sem("norm_inverses")
        q_inverses = sem("q_inverses")
        q_diagonal = sem("q_diagonal")
        q_row_ps = sem("q_row_ps")
        cosines_ready = sem("cosines_ready")
        cosines_high = sem("cosines_high")
        cosines_low_ready = sem("cosines_low_ready")
        tailor_diagonal = sem("tailor_diagonal")
        tailor_row_ps = sem("tailor_row_ps")
        row_out_ready = sem("row_out_ready")
        cosine_sums_ps = sem("cosine_sums_ps")
        tailor_steps = sem("tailor_steps")
        bv_row_high = sem("bv_row_high")
        bv_row_low = sem("bv_row_low")
        mix_ps = sem("mix_ps")
        mix_out = sem("mix_out")
        mix_high = sem("mix_high")
        mix_low = sem("mix_low")
        z_ps = sem("z_ps")
        z_scaled = sem("z_scaled")
        z_ready = sem("z_ready")
        z_stats_t = sem("z_stats_t")
        z_mean = sem("z_mean")
        z_dev = sem("z_dev")
        z_factor = sem("z_factor")
        z_shift = sem("z_shift")
        x1_ready = sem("x1_ready")
        x1_stats_t = sem("x1_stats_t")
        x1_mean = sem("x1_mean")
        x1_dev = sem("x1_dev")
        x1_factor = sem("x1_factor")
        x1_shift = sem("x1_shift")
        xf_ready = sem("xf_ready")
        xf_high_ready = sem("xf_high_ready")
        xf_low_ready = sem("xf_low_ready")
        xf_stored = sem("xf_stored")
        xf_turned = sem("xf_turned")
        xfT_ready = sem("xfT_ready")
        shared_ps = sem("shared_ps")
        logits_ready = sem("logits_ready")
        u_ready = sem("u_ready")
        u_stored = [sem("u_stored0"), sem("u_stored1")]
        attention_left = sem("attention_left")
        block_steps = sem("block_steps")
        picked = sem("picked")
        placed = sem("placed")
        both_ready = sem("both_ready")
        counts_ps = sem("counts_ps")
        counts_ready = sem("counts_ready")
        gap_ready = sem("gap_ready")
        second_ready = sem("second_ready")
        total_ready = sem("total_ready")
        share_ready = sem("share_ready")
        routing_consts = sem("routing_consts")
        table_init = sem("table_init")
        table_set = sem("table_set")
        blocks_ready = sem("blocks_ready")
        rows_wanted_in = [sem("rows_wanted_in0"), sem("rows_wanted_in1")]
        places_in = [sem("places_in0"), sem("places_in1")]
        gathered = [sem("gathered0"), sem("gathered1")]
        xb_turned = sem("xb_turned")
        xb_ready = sem("xb_ready")
        h_ps = sem("h_ps")
        h_act = sem("h_act")
        h_high = sem("h_high")
        h_low = sem("h_low")
        y_ps = sem("y_ps")
        y_biased = sem("y_biased")
        y_ready = sem("y_ready")
        y_stored = [sem("y_stored0"), sem("y_stored1")]
        tail_u_in = [sem("tail_u_in0"), sem("tail_u_in1")]
        tail_gelu = sem("tail_gelu")
        tail_y_in = sem("tail_y_in")
        tail_sum = sem("tail_sum")
        tail_out = sem("tail_out")
        tail_stats_t = sem("tail_stats_t")
        tail_mean = sem("tail_mean")
        tail_dev = sem("tail_dev")
        tail_factor = sem("tail_factor")
        tail_shift = sem("tail_shift")
        tail_normed = sem("tail_normed")
        tail_gamma = sem("tail_gamma")
        tail_beta = sem("tail_beta")
        last_stats_t = sem("last_stats_t")
        last_mean = sem("last_mean")
        last_dev = sem("last_dev")
        last_factor = sem("last_factor")
        last_shift = sem("last_shift")
        last_normed = sem("last_normed")
        tail_done = sem("tail_done")
        stored = sem("stored")
        block_consts = sem("block_consts")
        padding_set = sem("padding_set")
        passed = sem("passed")

        def past(count):
            return max(count, 0) if isinstance(count, int) else count

        def settle(eng):
            eng.sem_inc(passed, 1)

        def chain(eng, name, start):
            count = [0]

            def link(ins):
                count[0] += 1
                ins.then_inc(name, 1)
                eng.wait_ge(name, start + count[0])
            link.count = count
            return link

        def at(ap, i):
            return ap[i] if isinstance(i, int) else ap[bass.ds(i, 1)].squeeze(0)

        def run_steps(eng, step):
            for s in range(4):
                step(s)
            with eng.Fori(4, B) as s:
                step(s)
            for s in range(B, B + 3):
                step(s)

        def parts(s):
            if not isinstance(s, int):
                return s, s - 1, s - 2, s - 3, s - 3
            b = [s - n if 0 <= s - n < B else None for n in range(4)]
            return b[0], b[1], b[2], (b[3] if s < B else None), b[3]

        def xTf(b, f):
            n = 2 * C
            return xT[:, bass.ds((b % 2) * (NF * n) + f * n, n)]

        def xTt(b, f, k, t):
            n = 2 * C
            return xT[:, bass.ds((b % 2) * (NF * n) + (f * n + k * C + t * P), P)]

        def Xt(b, t):
            return X[:, bass.ds(b * T + t, 1), :].rearrange("p a d -> p (a d)")

        def w1_part(e, k):
            return W[:, bass.ds(e * WE, 2 * NF * H)].rearrange("p (f k n) -> p f k n", f=NF, k=2)[:, :, k, :]

        def w2_part(e, k):
            return W[:, bass.ds(e * WE + 2 * NF * H, 2 * NH * D)].rearrange("p (j k n) -> p j k n", j=NH, k=2)[:, :, k, :]

        late_pieces = [(e, which) for e in range(EARLY, E) for which in range(2)]

        def staged(e, which):
            buf = stage[:, 0:2048]
            if isinstance(e, int) and (e, which) in late_pieces:
                buf = (stage[:, 0:2048], stage[:, 2048:4096], zone[:, 1024:3072])[late_pieces.index((e, which)) % 3]
            return buf.rearrange("p (j n) -> p j n", j=NH if which else NF)

        zr = Carver([(zone, 0, 4096 - ROUTE)])
        block_no = zr([P, NB, E], F32)
        passed_by = zr([P, NB, E], F32)
        over = zr([P, NB], F32)
        first_slot = zr([P, E], F32)
        nblk = zr([P, E], F32)
        nblk_i = zr([P, E], I32)
        bend = zr([P, E], F32)
        one8 = zr([P, E], F32)

        zf = Carver([(zone, 0, 4096)])
        xg = zf([P, 2 * HALVES, 2 * D], F16)
        xbT = zf([P, 2 * NF * 2, BT], F16)
        h32 = zf([P, 2, 2 * BT], F32)
        y32 = zf([P, 2 * HALVES, D], F32)
        hhl = stage[:, :].bitcast(F16).rearrange("p (q j k n) -> p q j k n", q=2, j=NH, k=2)

        tail = Carver([(W[:, :].bitcast(F32), 0, E * WE // 2)])
        tu = tail([P, NG, D], F32)
        ty = tail([P, NG, 2, D], F32)
        to = tail([P, NG, D], F32)

        def sync_rest(sp):
            sp.wait_ge(blocks_ready, 1)
            sp.wait_ge(table_set, 16 * 2 * NG)
            sp.wait_ge(xf_stored, 16 * B)
            tv = table.rearrange("(j h p) c -> j p h c", p=P, h=HALVES)

            def block_in_table(j):
                return sp.value_load(block_at[0:1, bass.ds(j, 1)], min_val=0, max_val=SLOTS // BT - 1)

            def load_tb(j, q, n):
                block = block_in_table(j)
                sp.wait_ge(gathered[q], 16 * HALVES * n)
                sp.dma_start(tb[:, q, :, :], at(tv, block)).then_inc(rows_wanted_in[q], 16)

            def load_ts(j, q, n):
                block = block_in_table(j)
                sp.wait_ge(y_stored[q], 16 * HALVES * n)
                sp.dma_start(tsc[:, q, :, :], at(tv, block)).then_inc(places_in[q], 16)

            load_tb(0, 0, 0)
            load_tb(1, 1, 0)
            load_ts(0, 0, 0)
            load_ts(1, 1, 0)
            load_tb(2, 0, 1)
            load_tb(3, 1, 1)
            load_ts(2, 0, 1)
            with sp.Fori(1, (NB - 3) // 2) as i:
                load_tb(2 * i + 2, 0, i + 1)
                load_ts(2 * i + 1, 1, i)
                load_tb(2 * i + 3, 1, i + 1)
                load_ts(2 * i + 2, 0, i + 1)
            i = (NB - 3) // 2
            load_tb(2 * i + 2, 0, i + 1)
            load_ts(2 * i + 1, 1, i)
            load_ts(2 * i + 2, 0, i + 1)
            sp.wait_ge(y_ps, NB)
            sp.wait_ge(u_stored[0], 16 * B * T // 2)
            sp.wait_ge(u_stored[1], 16 * B * T // 2)
            ubv = u_rows.rearrange("(b p t) d -> b p (t d)", p=P, t=T)
            def load_u(n):
                for b in range(n * B // 2, (n + 1) * B // 2):
                    sp.dma_start(tu[:, b * T:(b + 1) * T, :].rearrange("p t d -> p (t d)"), ubv[b]).then_inc(tail_u_in[n], 16)
            yv = y_rows[0:PAIRS, :].rearrange("(b p t k) d -> b p (t k d)", p=P, t=T, k=2)

            def load_y(b):
                sp.wait_ge(tail_y_in, 16 * b)
                sp.dma_start(ty[:, b * T:(b + 1) * T, :, :].rearrange("p t k d -> p (t k d)"), yv[b]).then_inc(tail_y_in, 16)
            load_u(0)
            sp.wait_ge(y_stored[0], 16 * HALVES * ((NB + 1) // 2))
            sp.wait_ge(y_stored[1], 16 * HALVES * (NB // 2))
            load_y(0)
            load_y(1)
            load_u(1)
            for b in range(2, B):
                load_y(b)
            with sp.Fori(0, B) as b:
                sp.wait_ge(tail_done, b + 1)
                sp.dma_start(at(outrows, b), to_(b).rearrange("p t d -> p (t d)")).then_inc(stored, 16)
            sp.wait_ge(stored, 16 * B)

        def rows(buf, b):
            return buf[:, bass.ds(b * T, T), :]

        def to_(b):
            return rows(to, b)

        def gpsimd_rest(g):
            g.wait_ge(attention_left, 1)
            g.iota(block_no, [[1, NB], [0, E]], base=0, channel_multiplier=0, allow_small_or_imprecise_dtypes=True).then_inc(block_consts, 1)
            g.iota(first_slot, [[TOK, E]], base=0, channel_multiplier=0, allow_small_or_imprecise_dtypes=True).then_inc(block_consts, 1)
            g.memset(one8, 1.0).then_inc(block_consts, 1)
            g.wait_ge(table_set, 16 * 2 * NG)
            g.wait_ge(xf_stored, 16 * B)

            def gather(j, q, n):
                g.wait_ge(rows_wanted_in[q], 16 * (n + 1))
                g.wait_ge(xb_turned, past(j - 1))
                settle(g)
                for h in range(HALVES):
                    g.indirect_dma_start(out=xg[:, q * HALVES + h, :], out_offset=None, in_=xf_rows,
                                         in_offset=bass.IndirectOffsetOnAxis(ap=tb[:, q, h, 0:1], axis=0)).then_inc(gathered[q], 16)

            def scatter(j, q):
                g.wait_ge(y_ready, HALVES * (j + 1))
                settle(g)
                for h in range(HALVES):
                    g.indirect_dma_start(out=y_rows, out_offset=bass.IndirectOffsetOnAxis(ap=tsc[:, q, h, 1:2], axis=0),
                                         in_=y32[:, q * HALVES + h, :], in_offset=None).then_inc(y_stored[q], 16)
            gather(0, 0, 0)
            gather(1, 1, 0)
            gather(2, 0, 1)
            gather(3, 1, 1)
            scatter(0, 0)
            gather(4, 0, 2)
            scatter(1, 1)
            with g.Fori(2, (NB - 1) // 2) as i:
                gather(2 * i + 1, 1, i)
                scatter(2 * i - 2, 0)
                gather(2 * i + 2, 0, i + 1)
                scatter(2 * i - 1, 1)
            i = (NB - 1) // 2
            scatter(2 * i - 2, 0)
            scatter(2 * i - 1, 1)
            scatter(2 * i, 0)

            def add_pairs(b):
                g.wait_ge(tail_y_in, 16 * (b + 1))
                yb = ty[:, bass.ds(b * T, T), :, :]
                g.tensor_tensor(to_(b), yb[:, :, 0, :], yb[:, :, 1, :], ALU.add).then_inc(tail_sum, 1)

            def add_beta(b):
                g.wait_ge(tail_gamma, b + 1)
                g.tensor_tensor(to_(b), to_(b), lngb[:, 1, :].unsqueeze(1).broadcast_to([P, T, D]), ALU.add).then_inc(tail_beta, 1)

            def add_x(b):
                g.wait_ge(last_normed, T * (b + 1))
                g.tensor_tensor(to_(b), to_(b), rows(X, b), ALU.add).then_inc(tail_done, 1)

            def tail_step(s, now, last, old, older):
                if not isinstance(s, int) or s + 1 < B:
                    add_pairs(s + 1)
                if older:
                    add_x(s - 3)
                if last:
                    add_beta(s - 1)
            add_pairs(0)
            tail_steps(g, tail_step)

        def tail_steps(eng, step):
            for s in range(3):
                step(s, True, s >= 1, s >= 2, False)
            with eng.Fori(3, B - 1) as s:
                step(s, True, True, True, True)
            for s in range(B - 1, B + 3):
                step(s, s < B, s < B + 1, s < B + 2, True)

        def tensor_rest(pe):
            pe.wait_ge(attention_left, 1)
            for e in range(EARLY, E):
                for which in range(2):
                    lo, hi = ((0, 2), (2, 3))[which]
                    pe.wait_ge(expert_squares, 3 * e + 2 + which)
                    pe.wait_ge(expert_sums, 2 * e + which)
                    pe.matmul(MIX_PS[:, lo:hi], ones32[:, :], essq[:, lo:hi], start=True, stop=True).then_inc(expert_sums_ps, 1)
            pe.wait_ge(w_low, 2 * E)
            pe.wait_ge(w_high, 2 * E)
            pe.wait_ge(blocks_ready, 1)

            def turn(j, q, n):
                pe.wait_ge(gathered[q], 16 * HALVES * (n + 1))
                pe.wait_ge(xb_ready, j)
                for f in range(NF):
                    for k in range(2):
                        for h in range(HALVES):
                            at0 = ((f * 2 + k) * HALVES + h) * P
                            mm = pe.transpose(PS[4][:, :].bitcast(F16)[:, at0:at0 + P],
                                              xg[:, q * HALVES + h, k * D + f * P:k * D + (f + 1) * P], ident[:, :])
                mm.then_inc(xb_turned, 1)

            def up(j, q):
                e = pe.value_load(ej_i[0:1, bass.ds(j, 1)], min_val=0, max_val=E - 1)
                pe.wait_ge(xb_ready, j + 1)
                for m in range(NH // 2):
                    pe.wait_ge(h_act, past(NH * (j - 1) + 2 * m + 2))
                    for r in range(2):
                        for f in range(NF):
                            ws = [W[:, bass.ds(e * WE + (f * 2 + k) * H + (2 * m + r) * P, P)] for k in range(2)]
                            xs_ = [xbT[:, (q * NF + f) * 2 + k, :] for k in range(2)]
                            mm = mm3(pe, PS[m][:, r * BT:(r + 1) * BT], ws[0], ws[1], xs_[0], xs_[1], f == 0, f == NF - 1)
                    mm.then_inc(h_ps, 1)

            def down(j, q):
                e = pe.value_load(ej_i[0:1, bass.ds(j, 1)], min_val=0, max_val=E - 1)
                pe.wait_ge(y_biased, past(j - 1))
                for h in range(HALVES):
                    for m in range(NH):
                        if h == 0 and m % 2 == 0:
                            pe.wait_ge(h_low, NH // 2 * j + m // 2 + 1)
                        ws = [W[:, bass.ds(e * WE + 2 * NF * H + (m * 2 + k) * D, D)] for k in range(2)]
                        mm = mm3(pe, PS[5 + q][:, h * D:(h + 1) * D], hhl[:, q, m, 0, h * P:(h + 1) * P], hhl[:, q, m, 1, h * P:(h + 1) * P],
                                 ws[0], ws[1], m == 0, m == NH - 1)
                mm.then_inc(y_ps, 1)
            turn(0, 0, 0)
            up(0, 0)
            turn(1, 1, 0)
            up(1, 1)
            turn(2, 0, 1)
            down(0, 0)
            up(2, 0)
            turn(3, 1, 1)
            down(1, 1)
            with pe.Fori(2, (NB - 1) // 2) as i:
                up(2 * i - 1, 1)
                turn(2 * i, 0, i)
                down(2 * i - 2, 0)
                up(2 * i, 0)
                turn(2 * i + 1, 1, i)
                down(2 * i - 1, 1)
            i = (NB - 1) // 2
            up(2 * i - 1, 1)
            turn(2 * i, 0, i)
            down(2 * i - 2, 0)
            up(2 * i, 0)
            down(2 * i - 1, 1)
            down(2 * i, 0)

        def scalar_rest(a):
            a.wait_ge(blocks_ready, 1)
            a.preload_act_table(ACT.Gelu)

            def gelu(j, q):
                e = a.value_load(ej_i[0:1, bass.ds(j, 1)], min_val=0, max_val=E - 1)
                for m in range(NH // 2):
                    a.wait_ge(h_ps, NH // 2 * j + m + 1)
                    a.wait_ge(h_low, past(NH // 2 * j + m - 1))
                    for r in range(2):
                        settle(a)
                        a.activation(h32[:, m % 2, r * BT:(r + 1) * BT], PS[m][:, r * BT:(r + 1) * BT], ACT.Gelu,
                                     bias=b1T[:, bass.ds(e * NH + 2 * m + r, 1)], scale=tab[:, 0, bass.ds(e, 1)]).then_inc(h_act, 1)
            gelu(0, 0)
            with a.Fori(1, NB) as j:
                gelu(j, 0)
            def gelu_shared(n):
                a.wait_ge(tail_u_in[n], 16 * B // 2)
                for b in range(n * B // 2, (n + 1) * B // 2):
                    a.activation(tu[:, b * T:(b + 1) * T, :], tu[:, b * T:(b + 1) * T, :], ACT.Gelu).then_inc(tail_gelu, 1)
                a.preload_act_table(ACT.Sqrt)
            gelu_shared(0)

            def sd_(which, name, need, b):
                a.wait_ge(need, T * (b + 1))
                settle(a)
                a.activation(sd[:, which, :], mv[:, which, :, 1], ACT.Sqrt, bias=eps[:, 2:3]).then_inc(name, 1)

            def scaled(b, need, value, factor, shift, name):
                a.wait_ge(need, value)
                settle(a)
                for t in range(T):
                    o = to[:, bass.ds(b * T + t, 1), :].rearrange("p a d -> p (a d)")
                    a.activation(o, o, ACT.Identity, bias=shift[:, t:t + 1], scale=factor[:, t:t + 1]).then_inc(name, 1)

            def tail_step(s, now, last, old, older):
                if now:
                    sd_(0, tail_dev, tail_mean, s)
                if old:
                    sd_(1, last_dev, last_mean, s - 2)
                if now:
                    scaled(s, tail_shift, s + 1, cf[:, 0, :], cf[:, 2, :], tail_normed)
                if old:
                    scaled(s - 2, last_shift, 2 * (s - 1), cf[:, 1, :], c3, last_normed)
                if isinstance(s, int) and s == 1:
                    a.preload_act_table(ACT.Gelu)
                    gelu_shared(1)
            tail_steps(a, tail_step)

        def vector_blocks(v):
            link = chain(v, block_steps, 0)
            v.wait_ge(placed, PLACES * B)
            v.wait_ge(block_consts, 3)
            link(v.tensor_tensor(nblk, place_of, first_slot, ALU.subtract))
            link(v.tensor_scalar(nblk_i, nblk, float(BT - 1), None, ALU.add))
            link(v.tensor_scalar(nblk_i, nblk_i, BT.bit_length() - 1, None, ALU.arith_shift_right))
            link(v.tensor_copy(nblk, nblk_i))
            link(v.tensor_tensor_scan(bend, one8, nblk, 0.0, ALU.mult, ALU.add))
            link(v.tensor_tensor(passed_by, block_no, bend.unsqueeze(1).broadcast_to([P, NB, E]), ALU.is_ge))
            link(v.tensor_reduce(over, passed_by, AX.X, ALU.add))
            link(v.tensor_scalar(ej_i[:, 0:NB], over, float(E - 1), None, ALU.min))
            link(v.tensor_scalar(nblk, nblk, -1.0, float(RB), ALU.mult, ALU.add))
            link(v.tensor_tensor(passed_by, passed_by, nblk.unsqueeze(1).broadcast_to([P, NB, E]), ALU.mult))
            link(v.tensor_reduce(over, passed_by, AX.X, ALU.add))
            link(v.tensor_tensor(block_at[:, 0:NB], over, block_no[:, :, 0], ALU.add))
            v.tensor_copy(nblk, one8).then_inc(blocks_ready, 1)

        def vector_rest(v):
            def split(j, q):
                e = v.value_load(ej_i[0:1, bass.ds(j, 1)], min_val=0, max_val=E - 1)
                v.wait_ge(y_ps, past(j - 1))
                for m in range(NH // 2):
                    v.wait_ge(h_act, NH * j + 2 * m + 2)
                    o = [hhl[:, q, 2 * m:2 * m + 2, k, :] for k in range(2)]
                    src = h32[:, m % 2, :].rearrange("p (r n) -> p r n", r=2)
                    v.tensor_scalar(o[0], src, tab[:, 1, bass.ds(e, 1)], None, ALU.mult).then_inc(h_high, 1)
                    v.wait_ge(h_high, NH // 2 * j + m + 1)
                    v.scalar_tensor_tensor(o[1], src, tab[:, 1, bass.ds(e, 1)], o[0], ALU.mult, ALU.subtract).then_inc(h_low, 1)

            def turned_block(j, q):
                v.wait_ge(xb_turned, j + 1)
                v.wait_ge(h_ps, past(NH // 2 * (j - 1)))
                v.tensor_copy(xbT[:, q * NF * 2:(q + 1) * NF * 2, :].rearrange("p a n -> p (a n)"), PS[4][:, :].bitcast(F16)).then_inc(xb_ready, 1)

            def result(j, q, n):
                e = v.value_load(ej_i[0:1, bass.ds(j, 1)], min_val=0, max_val=E - 1)
                v.wait_ge(y_ps, j + 1)
                v.wait_ge(y_stored[q], 16 * HALVES * n)
                yq = y32[:, q * HALVES:(q + 1) * HALVES, :]
                v.scalar_tensor_tensor(yq, PS[5 + q][:, :].rearrange("p (h d) -> p h d", h=HALVES), tab[:, 2, bass.ds(e, 1)],
                                       b2b[:, bass.ds(e * D, D)].unsqueeze(1).broadcast_to([P, HALVES, D]), ALU.mult, ALU.add).then_inc(y_biased, 1)
                v.wait_ge(y_biased, j + 1)
                v.wait_ge(places_in[q], 16 * (n + 1))
                for h in range(HALVES):
                    v.tensor_scalar(y32[:, q * HALVES + h, :], y32[:, q * HALVES + h, :], tsc[:, q, h, 2:3].bitcast(F32), None,
                                    ALU.mult).then_inc(y_ready, 1)
            turned_block(0, 0)
            split(0, 0)
            turned_block(1, 1)
            split(1, 1)
            turned_block(2, 0)
            result(0, 0, 0)
            split(2, 0)
            turned_block(3, 1)
            result(1, 1, 0)
            with v.Fori(2, (NB - 1) // 2) as i:
                split(2 * i - 1, 1)
                turned_block(2 * i, 0)
                result(2 * i - 2, 0, i - 1)
                split(2 * i, 0)
                turned_block(2 * i + 1, 1)
                result(2 * i - 1, 1, i - 1)
            i = (NB - 1) // 2
            split(2 * i - 1, 1)
            turned_block(2 * i, 0)
            result(2 * i - 2, 0, i - 1)
            split(2 * i, 0)
            result(2 * i - 1, 1, i - 1)
            result(2 * i, 0, i)

            def tstats(which, b, need, value, st_name, mv_name):
                v.wait_ge(need, value)
                settle(v)
                for t in range(T):
                    v.bn_stats(st[:, which, t, :], to[:, bass.ds(b * T + t, 1), :].rearrange("p a d -> p (a d)")).then_inc(st_name, 1)
                for t in range(T):
                    v.wait_ge(st_name, T * b + t + 1)
                    settle(v)
                    v.bn_aggr(mv[:, which, t, :], st[:, which, t, :]).then_inc(mv_name, 1)

            def enter_tail(b):
                v.wait_ge(tail_gelu, B // 2 if isinstance(b, int) and b < B // 2 else B)
                v.wait_ge(tail_sum, b + 1)
                v.scalar_tensor_tensor(to_(b), rows(tu, b), 0.5, to_(b), ALU.mult, ALU.add).then_inc(tail_out, 1)
                tstats(0, b, tail_out, b + 1, tail_stats_t, tail_mean)

            def inner_factors(b):
                v.wait_ge(tail_dev, b + 1)
                v.reciprocal(cf[:, 0, :], sd[:, 0, :]).then_inc(tail_factor, 1)
                v.wait_ge(tail_factor, b + 1)
                v.scalar_tensor_tensor(cf[:, 2, :], mv[:, 0, :, 0], -1.0, cf[:, 0, :], ALU.mult, ALU.mult).then_inc(tail_shift, 1)

            def times_gamma(b):
                v.wait_ge(tail_normed, T * (b + 1))
                v.tensor_tensor(to_(b), to_(b), lngb[:, 0, :].unsqueeze(1).broadcast_to([P, T, D]), ALU.mult).then_inc(tail_gamma, 1)

            def outer_factors(b):
                v.wait_ge(last_dev, b + 1)
                v.wait_ge(last_normed, T * b)
                v.reciprocal(cf[:, 1, :], sd[:, 1, :]).then_inc(last_factor, 1)
                v.wait_ge(last_factor, b + 1)
                v.scalar_tensor_tensor(c3[:, :], mv[:, 1, :, 0], -1.0, cf[:, 1, :], ALU.mult, ALU.mult).then_inc(last_shift, 1)
                v.wait_ge(last_shift, 2 * b + 1)
                v.tensor_tensor(c3[:, :], c3[:, :], c2[:, bass.ds(b * T, T)], ALU.add).then_inc(last_shift, 1)

            def tail_step(s, now, last, old, older):
                if now:
                    enter_tail(s)
                if last:
                    times_gamma(s - 1)
                if old:
                    tstats(1, s - 2, tail_beta, s - 1, last_stats_t, last_mean)
                if now:
                    inner_factors(s)
                if old:
                    outer_factors(s - 2)
            tail_steps(v, tail_step)

        block = ctx.enter_context(nc.Block())
        xrows = x_in.rearrange("b (p t) d -> b p (t d)", t=T)
        outrows = out.rearrange("b (p t) d -> b p (t d)", t=T)
        xfv = xf_rows.rearrange("(b p t) d -> b p (t d)", p=P, t=T)
        uv = u_rows.rearrange("(b p t) d -> b p t d", p=P, t=T)
        wqk_n = z[:, :, :]
        wv_n = m32[:, :, :]
        sh_n = gk[:, :, :]
        b1_n = u[0:E * NH, 0, 0:P]

        def mm3(pe, o, lh, ll, rh, rl, first, last):
            pe.matmul(o, lh, rh, start=first, stop=False)
            pe.matmul(o, lh, rl, start=False, stop=False)
            return pe.matmul(o, ll, rh, start=False, stop=last)

        @block.sync
        def _(sp):
            def load_x(b):
                sp.wait_ge(x_loaded, 16 * b)
                sp.dma_start(X[:, b * T:(b + 1) * T, :].rearrange("p t d -> p (t d)"), xrows[b]).then_inc(x_loaded, 16)

            def load_w1(e):
                sp.wait_ge(w_high, 2 * e)
                sp.wait_ge(w_low, 2 * e)
                sp.dma_start(staged(e, 0),
                             at(W1, e).rearrange("(f p) n -> p f n", p=P)).then_inc(w1_in, 16)

            def load_w2(e):
                sp.wait_ge(w_high, 2 * e + 1)
                sp.wait_ge(w_low, 2 * e + 1)
                sp.dma_start(staged(e, 1),
                             at(W2, e).rearrange("(j p) n -> p j n", p=P)).then_inc(w2_in, 16)

            def load_late(i):
                e, which = late_pieces[i]
                if i < 3:
                    sp.wait_ge(w_high, 2 * EARLY)
                    sp.wait_ge(w_low, 2 * EARLY)
                    if i:
                        sp.wait_ge(attention_left, 1)
                else:
                    sp.wait_ge(w_high, past(2 * EARLY + i - 2))
                    sp.wait_ge(w_low, past(2 * EARLY + i - 2))
                if which:
                    sp.wait_ge(w2_in, 16 * e)
                    sp.dma_start(staged(e, 1), W2[e].rearrange("(j p) n -> p j n", p=P)).then_inc(w2_in, 16)
                else:
                    sp.wait_ge(w1_in, 16 * e)
                    sp.dma_start(staged(e, 0), W1[e].rearrange("(f p) n -> p f n", p=P)).then_inc(w1_in, 16)

            def store_u(b, t):
                sp.wait_ge(u_ready, T * b + t + 1)
                sp.dma_start(at(uv, b)[:, t, :], u[:, t % 2, :]).then_inc(u_stored[t % 2], 16)

            def store_xf(b):
                sp.wait_ge(xf_high_ready, b + 1)
                sp.wait_ge(xf_low_ready, b + 1)
                sp.dma_start(at(xfv, b),
                             xfhl.rearrange("p t k d -> p (t k d)")).then_inc(xf_stored, 16)

            load_x(0)
            with nc.allow_non_contiguous_dma(reason="512 single words, once"):
                for j in range(NF):
                    sp.dma_start(wqk_n[:, j, :], Wq[j * P:(j + 1) * P, :]).then_inc(wqk_in, 16)
                    sp.dma_start(wqk_n[:, NF + j, :], Wk[j * P:(j + 1) * P, :]).then_inc(wqk_in, 16)
                sp.dma_start(bqk[:, 0:D], bq.partition_broadcast(P)).then_inc(qk_bias_in, 16)
                sp.dma_start(bqk[:, D:2 * D], bk.partition_broadcast(P)).then_inc(qk_bias_in, 16)
                sp.dma_start(wv_n, Wv.rearrange("(j p) i -> p j i", p=P)).then_inc(wv_in, 16)
                sp.dma_start(bvc[:, :], bv.rearrange("(j p) -> p j", p=P)).then_inc(bv_in, 16)
                sp.dma_start(gam_b[:, :], gam.partition_broadcast(P)).then_inc(bv_in, 16)
                load_x(1)
                sp.dma_start(sh_n, shared_W.rearrange("(j p) i -> p j i", p=P)).then_inc(shared_in, 16)
                sp.dma_start(gate_n, gate_W.rearrange("(j p) i -> p j i", p=P)).then_inc(shared_in, 16)
                sp.dma_start(b1_n, b1.rearrange("e (j p) -> (e j) p", p=P)).then_inc(b1_in, 16)
                sp.dma_start(sbb[:, :], shared_b.partition_broadcast(P)).then_inc(row_biases_in, 16)
                sp.dma_start(lngb[:, 0, :], lng.partition_broadcast(P)).then_inc(row_biases_in, 16)
                sp.dma_start(lngb[:, 1, :], lnb.partition_broadcast(P)).then_inc(row_biases_in, 16)
                sp.dma_start(b2b[:, :], b2.rearrange("e d -> (e d)").partition_broadcast(P)).then_inc(row_biases_in, 16)
            for b in range(2, B):
                load_x(b)
            sp.wait_ge(padding_set, 2)
            sp.dma_start(table.rearrange("(p g) c -> p (g c)", p=P), tinit.rearrange("p g c -> p (g c)")).then_inc(table_init, 16)

            def step(s):
                entering, mixing, leaving, e, placing = parts(s)
                if e is not None:
                    load_w1(e)
                if leaving is not None:
                    store_xf(leaving)
                    for t in range(T):
                        store_u(leaving, t)
                if e is not None:
                    load_w2(e)
            run_steps(sp, step)
            for i in range(len(late_pieces)):
                load_late(i)
            sync_rest(sp)

        @block.gpsimd
        def _(g):
            g.memset(eps[:, 0:1], EPS_LN / SX / SX).then_inc(eps_set, 1)
            g.memset(eps[:, 1:2], EPS_LN * SX * SX).then_inc(eps_set, 1)
            g.memset(eps[:, 2:3], EPS_LN).then_inc(eps_set, 1)
            g.memset(ident32, 0.0).then_inc(identity_set, 1)
            g.memset(ident[:, :], 0.0).then_inc(identity_set, 1)
            g.memset(upper[:, :], 1.0).then_inc(upper_set, 1)
            g.memset(ones32[:, :], 1.0).then_inc(ones_set, 1)
            g.memset(ones16[:, :], 1.0).then_inc(ones_set, 1)
            g.memset(row2048[:, :], SX).then_inc(row_set_once, 1)
            g.wait_ge(identity_set, 2)
            for i in (ident32, ident[:, :]):
                g.affine_select(out=i, in_=i, compare_op=ALU.not_equal, fill=1.0, base=0,
                                pattern=[[-1, P]], channel_multiplier=1).then_inc(identity_set, 1)
            g.wait_ge(upper_set, 1)
            g.affine_select(out=upper[:, :], in_=upper[:, :], compare_op=ALU.is_gt, fill=0.0, base=0,
                            pattern=[[1, P]], channel_multiplier=-1).then_inc(upper_set, 1)
            g.iota(tinit[:, :, 0:4], [[0, PAD_COLS], [0, 4]], base=0, channel_multiplier=0).then_inc(padding_set, 1)
            g.wait_ge(padding_set, 1)
            g.iota(tinit[:, :, 1], [[1, PAD_COLS]], base=PAIRS, channel_multiplier=PAD_COLS).then_inc(padding_set, 1)
            g.iota(below, [[0, T], [1, E]], base=-E, channel_multiplier=0, allow_small_or_imprecise_dtypes=True).then_inc(routing_consts, 1)
            g.iota(place_of, [[TOK, E]], base=0, channel_multiplier=0, allow_small_or_imprecise_dtypes=True).then_inc(routing_consts, 1)
            g.iota(number[:, :, :, 0], [[1, T], [0, 2]], base=0, channel_multiplier=T, allow_small_or_imprecise_dtypes=True).then_inc(routing_consts, 1)
            g.iota(number[:, :, :, 1], [[2, T], [1, 2]], base=0, channel_multiplier=2 * T, allow_small_or_imprecise_dtypes=True).then_inc(routing_consts, 1)
            g.memset(ahead[:, :, :, 0], float(C)).then_inc(routing_consts, 1)
            g.memset(ahead[:, :, :, 1], float(2 * C)).then_inc(routing_consts, 1)
            g.iota(pay, [[0, T], [0, 2], [0, 4]], base=0, channel_multiplier=0).then_inc(routing_consts, 1)

            def low(o, x, h, name, o_free, waits):
                for n, v in waits:
                    g.wait_ge(n, past(v))
                g.tensor_tensor(o, x, h, ALU.subtract).then_inc(name, 1)

            def e_reduce(n, lo, hi):
                g.wait_ge(expert_squares, n)
                settle(g)
                g.partition_all_reduce(etot[:, lo:hi], essq[:, lo:hi], P, bass.bass_isa.ReduceOp.add).then_inc(expert_sums, 1)

            def over_experts(link, out, src, op):
                link(g.tensor_tensor(four, src[:, :, 0:4], src[:, :, 4:8], op))
                link(g.tensor_tensor(two, four[:, :, 0:2], four[:, :, 2:4], op))
                link(g.tensor_tensor(out, two[:, :, 0], two[:, :, 1], op))

            def place(b):
                g.wait_ge(counts_ready, b + 1)
                g.wait_ge(share_ready, b + 1)
                g.wait_ge(table_set, 16 * 2 * T * b)
                settle(g)
                link = chain(g, placed, PLACES * b)
                link(g.tensor_tensor(rank, counts[:, 0:T * E].rearrange("p (t e) -> p t e", e=E), place_of.unsqueeze(1).broadcast_to([P, T, E]), ALU.add))
                link(g.tensor_tensor(place_of, place_of, counts[:, T * E:(T + 1) * E], ALU.add))
                for k in range(2):
                    link(g.tensor_tensor(by_expert, pick[k], rank, ALU.mult))
                    over_experts(link, slot_f, by_expert, ALU.add)
                    settle(g)
                    link(g.tensor_copy(slot_i[:, k, :], slot_f))
                settle(g)
                link(g.tensor_copy(pay[:, :, :, 0:2], number))
                link(g.tensor_tensor(number, number, ahead, ALU.add))
                settle(g)
                link(g.tensor_copy(pay[:, :, 0, 2].bitcast(F32), share))
                link(g.tensor_tensor(pay[:, :, 1, 2].bitcast(F32), second, share, ALU.mult))
                assert link.count[0] == PLACES

            def write_slots(b):
                g.wait_ge(table_init, 16)
                g.wait_ge(placed, PLACES * (b + 1))
                settle(g)
                for t in range(T):
                    for k in range(2):
                        g.indirect_dma_start(out=table, out_offset=bass.IndirectOffsetOnAxis(ap=slot_i[:, k, t:t + 1], axis=0),
                                             in_=pay[:, t, k, :], in_offset=None).then_inc(table_set, 16)

            def step(s):
                entering, mixing, leaving, e, placing = parts(s)
                if entering is not None:
                    g.wait_ge(x_high_ready, entering + 1)
                    g.wait_ge(x_turned, 2 * entering)
                    g.tensor_tensor(xhl[:, :, 1, :], xs, xhl[:, :, 0, :], ALU.subtract).then_inc(x_low_ready, 1)
                if e is not None:
                    e_reduce(3 * e + 2, 0, 2)
                if placing is not None:
                    write_slots(placing)
                if entering is not None:
                    for t in range(T):
                        g.wait_ge(qk_high, T * entering + t + 1)
                        g.wait_ge(norms_ps, entering)
                        g.tensor_tensor(qkl[:, t, :], q32[:, t % 2, :], qkh[:, t, :], ALU.subtract).then_inc(qk_low, 1)
                        if t:
                            g.wait_ge(qk_squares, T * entering + t + 1)
                            g.wait_ge(squares_added, past((T - 1) * entering + t - 1))
                            g.tensor_tensor(sqa, sqa, sqt, ALU.add).then_inc(squares_added, 1)
                if e is not None:
                    e_reduce(3 * e + 3, 2, 3)
                if leaving is not None:
                    place(leaving)
                if mixing is not None:
                    g.wait_ge(xf_high_ready, mixing + 1)
                    g.wait_ge(xf_turned, 2 * mixing)
                    g.wait_ge(xf_stored, 16 * mixing)
                    g.tensor_tensor(xfhl[:, :, 1, :], z, xfhl[:, :, 0, :], ALU.subtract).then_inc(xf_low_ready, 1)
            run_steps(g, step)
            gpsimd_rest(g)

        @block.tensor
        def _(pe):
            pe.wait_ge(ones_set, 2)
            pe.wait_ge(setup_squares, 6)
            pe.matmul(ROWS_PS[:, 0:6], ones32[:, :], ssq[:, 0:6], start=True, stop=True)
            pe.wait_ge(bv_in, 32)
            pe.matmul(ROWS_PS[:, 8:8 + NF], ones32[:, :], bvc[:, :], start=True, stop=True).then_inc(setup_sums, 1)
            pe.wait_ge(identity_set, 4)
            for i in range(NF):
                for j in range(2 * NF):
                    mm = pe.transpose(TURN_PS[i][:, j * P:(j + 1) * P], wqk_n[:, j, i * P:(i + 1) * P], ident32)
            mm.then_inc(wqk_turned, 1)
            for i in range(NF):
                for l in range(NF):
                    mm = pe.matmul(SUMS_PS[:, i:i + 1], wv_n[:, l, i * P:(i + 1) * P], ones32[:, 0:1], start=(l == 0), stop=(l == NF - 1))
            mm.then_inc(wv_sums_ps, 1)
            pe.wait_ge(b1_in, 16)
            pe.transpose(QK_PS[0][:, 0:E * NH], b1_n, ident32[0:E * NH, 0:E * NH]).then_inc(b1_turned, 1)

            def transposes(b, src, name, f, bank):
                for t in range(T):
                    for k in range(2):
                        mm = pe.transpose(bank[:, :].bitcast(F16)[:, (k * T + t) * P:(k * T + t + 1) * P],
                                          src[:, t, k, f * P:(f + 1) * P], ident[:, :])
                mm.then_inc(name, 1)

            def scores(b):
                pe.wait_ge(z_scaled, 2 * b)
                pe.wait_ge(row_out_ready, 2 * b)
                for t in range(T):
                    pe.wait_ge(qk_low, T * b + t + 1)
                    for lt in range(NF):
                        cs = slice(D + lt * P, D + (lt + 1) * P)
                        mm = mm3(pe, (SCORE_PS[:, 0:D], ROWS_PS[:, D:2 * D])[lt], qkh[:, t, cs], qkl[:, t, cs], qkh[:, t, 0:D], qkl[:, t, 0:D],
                                 t == 0, t == T - 1)
                mm.then_inc(scores_ps, 1)

            def column_norms(b):
                pe.wait_ge(squares_added, past((T - 1) * (b + 1)))
                for c in range(2 * NF):
                    pe.matmul(SUMS_PS[:, c:c + 1], sqa[:, c * P:(c + 1) * P], ones32[:, 0:1], start=True, stop=True)
                for c in range(NF):
                    for t in range(T):
                        pe.matmul(SUMS_PS[:, 4 + c:5 + c], qkh[:, t, c * P:(c + 1) * P], ones16[:, 0:1], start=(t == 0), stop=False)
                        mm = pe.matmul(SUMS_PS[:, 4 + c:5 + c], qkl[:, t, c * P:(c + 1) * P], ones16[:, 0:1], start=False, stop=(t == T - 1))
                mm.then_inc(norms_ps, 1)

            def count(b):
                pe.wait_ge(both_ready, b + 1)
                pe.wait_ge(counts_ready, b)
                pe.wait_ge(upper_set, 2)
                for t in range(T):
                    o = SUMS_PS[:, 8 + t * E:8 + (t + 1) * E]
                    for n in range(t):
                        pe.matmul(o, ones16[:, :], both[:, n, :], start=(n == 0), stop=False)
                    pe.matmul(o, upper[:, :], both[:, t, :], start=(t == 0), stop=True)
                o = SUMS_PS[:, 8 + T * E:8 + (T + 1) * E]
                for n in range(T):
                    mm = pe.matmul(o, ones16[:, :], both[:, n, :], start=(n == 0), stop=(n == T - 1))
                mm.then_inc(counts_ps, 1)

            def spread_rows(b, src, cols, need, name):
                pe.wait_ge(need[0], need[1])
                for c in range(NF):
                    mm = pe.matmul(ROWS_PS[:, cols + c * P:cols + (c + 1) * P], ones32[:, :], src[:, c, :], start=True, stop=True)
                mm.then_inc(name, 1)

            def shared_turn(b):
                pe.wait_ge(u_ready, T * b)
                pe.wait_ge(logits_ready, T * b)
                pe.wait_ge(xf_high_ready, b + 1)
                pe.wait_ge(xf_low_ready, b + 1)
                for f in range(NF):
                    transposes(b, xfhl, xf_turned, f, TURN_PS[f])

            def shared(b, tiles):
                pe.wait_ge(xfT_ready, 2 * (b + 1))
                for t in tiles:
                    pe.wait_ge(u_ready, past(T * b + t - 1))
                    pe.wait_ge(logits_ready, past(T * b + t - 1))
                    for f in range(NF):
                        ts = slice(t * P, (t + 1) * P)
                        mm = mm3(pe, TURN_PS[t % 2][:, 0:D + E], xfT[:, f, 0, ts], xfT[:, f, 1, ts], sgs[:, f, 0, :], sgs[:, f, 1, :],
                                 f == 0, f == NF - 1)
                    mm.then_inc(shared_ps, 1)

            def turn_x(b):
                pe.wait_ge(x_low_ready, b + 1)
                pe.wait_ge(qk_out, T * b)
                for f in range(NF):
                    transposes(b, xhl, x_turned, f, QK_PS[f])

            def sums(b):
                pe.wait_ge(cosines_ready, NF * (b + 1))
                pe.wait_ge(counts_ready, past(b - 1))
                for c in range(NF):
                    for l in range(NF):
                        pe.matmul(SUMS_PS[:, 6 + c:7 + c], gk[:, l, c * P:(c + 1) * P], ones32[:, 0:1], start=(l == 0), stop=(l == NF - 1))
                for l in range(NF):
                    mm = pe.matmul(SUMS_PS[:, D:2 * D], bvb[:, l, :], gk[:, l, :], start=(l == 0), stop=(l == NF - 1))
                mm.then_inc(cosine_sums_ps, 1)

            def project(b, t):
                if t == 0:
                    pe.wait_ge(xT_ready, 2 * (b + 1))
                pe.wait_ge(qk_out, past(T * b + t - 1))
                for f in range(NF):
                    mm = mm3(pe, QK_PS[t % 2][:, :], xTt(b, f, 0, t), xTt(b, f, 1, t), wqkT[:, f, 0, :], wqkT[:, f, 1, :], f == 0, f == NF - 1)
                mm.then_inc(qk_ps, 1)

            def mix(b):
                pe.wait_ge(cosines_high, b + 1)
                pe.wait_ge(cosines_low_ready, b + 1)
                for i in range(NF):
                    for l in range(NF):
                        mm = mm3(pe, MIX_PS[:, i * D:(i + 1) * D], wvs[:, l, 0, i * P:(i + 1) * P], wvs[:, l, 1, i * P:(i + 1) * P],
                                 ghl[:, 0, l, :], ghl[:, 1, l, :], l == 0, l == NF - 1)
                mm.then_inc(mix_ps, 1)

            def values(b):
                pe.wait_ge(mix_high, b + 1)
                pe.wait_ge(mix_low, b + 1)
                pe.wait_ge(bv_row_low, b + 1)
                for t in range(T):
                    o = (SCORE_PS, MIX_PS)[t // 2][:, (t % 2) * D:(t % 2 + 1) * D]
                    for f in range(NF):
                        mm3(pe, o, xTt(b, f, 0, t), xTt(b, f, 1, t), mhl[:, 0, f, :], mhl[:, 1, f, :], f == 0, False)
                    for k in range(2):
                        mm = pe.matmul(o, row2048[:, :], rhl[:, k, :], start=False, stop=(k == 1))
                    if t % 2:
                        mm.then_inc(z_ps, 1)

            def step(s):
                entering, mixing, leaving, e, placing = parts(s)
                if mixing is not None:
                    spread_rows(mixing, dgq, 0, (q_diagonal, NF * (mixing + 1)), q_row_ps)
                if leaving is not None:
                    shared_turn(leaving)
                if mixing is not None:
                    sums(mixing)
                    mix(mixing)
                if leaving is not None:
                    shared(leaving, range(0, 2))
                if entering is not None:
                    turn_x(entering)
                if mixing is not None:
                    spread_rows(mixing, dgt, D, (tailor_diagonal, NF * (mixing + 1)), tailor_row_ps)
                if entering is not None:
                    project(entering, 0)
                    project(entering, 1)
                if leaving is not None:
                    shared(leaving, range(2, T))
                if entering is not None:
                    project(entering, 2)
                    project(entering, 3)
                if mixing is not None:
                    values(mixing)
                if entering is not None:
                    scores(entering)
                if leaving is not None:
                    count(leaving)
                if entering is not None:
                    column_norms(entering)
            pe.wait_ge(wqk_high, NF)
            pe.wait_ge(wqk_low, NF)
            pe.wait_ge(b1_ready, 1)
            pe.wait_ge(wv_low, 1)
            pe.wait_ge(shared_low, 2)
            pe.wait_ge(setup_steps, SETUP_V)
            run_steps(pe, step)
            tensor_rest(pe)

        @block.scalar
        def _(a):
            a.wait_ge(eps_set, 3)
            a.preload_act_table(ACT.Sqrt)
            link = chain(a, setup_squares, 0)
            dump = xfhl.rearrange("p t k d -> p (t k d)")
            a.wait_ge(wqk_in, 64)
            link(a.activation(dump[:, 0:4 * D], wqk_n.rearrange("p j i -> p (j i)"), ACT.Square, accum_out=ssq[:, 0:1]))
            a.wait_ge(qk_bias_in, 32)
            link(a.activation(dump[:, 0:2 * D], bqk, ACT.Square, accum_out=ssq[:, 5:6]))
            a.wait_ge(wv_in, 16)
            link(a.activation(dump[:, 0:2 * D], wv_n.rearrange("p j i -> p (j i)"), ACT.Square, accum_out=ssq[:, 1:2]))
            a.wait_ge(bv_in, 32)
            link(a.activation(dump[:, 0:NF], bvc[:, :], ACT.Square, accum_out=ssq[:, 4:5]))
            a.wait_ge(shared_in, 32)
            link(a.activation(dump[:, 0:2 * D], sh_n.rearrange("p j i -> p (j i)"), ACT.Square, accum_out=ssq[:, 2:3]))
            link(a.activation(dump[:, 0:NF * E], gate_n.rearrange("p j i -> p (j i)"), ACT.Square, accum_out=ssq[:, 3:4]))
            a.wait_ge(setup_steps, 10)
            a.activation(scl[:, 0:6], bnd[:, 0:6], ACT.Sqrt, scale=TOP * TOP).then_inc(setup_roots, 1)
            a.wait_ge(setup_steps, 11)
            a.wait_ge(wqk_turned, 1)
            for i in range(NF):
                a.activation(wqkT[:, i, 0, :], TURN_PS[i][:, :], ACT.Copy, scale=scl[:, 0:1]).then_inc(wqk_high, 1)
            a.activation(wvs[:, :, 0, :], wv_n, ACT.Copy, scale=scl[:, 2:3]).then_inc(wv_high, 1)
            a.activation(sgs[:, :, 0, 0:D], sh_n, ACT.Copy, scale=scl[:, 4:5]).then_inc(shared_high, 1)
            a.activation(sgs[:, :, 0, D:D + E], gate_n, ACT.Copy, scale=scl[:, 5:6]).then_inc(shared_high, 1)
            a.wait_ge(b1_turned, 1)
            a.activation(b1T[:, :], QK_PS[0][:, 0:E * NH], ACT.Copy).then_inc(b1_ready, 1)
            a.wait_ge(b1_ready, 1)

            def spread(which, name, need, epsc, scale):
                a.wait_ge(need[0], need[1])
                settle(a)
                a.activation(sd[:, which, :], mv[:, which, :, 1], ACT.Sqrt, bias=eps[:, epsc:epsc + 1], scale=scale).then_inc(name, 1)

            def e_squares(e, which):
                if which == 0:
                    a.wait_ge(w1_in, 16 * (e + 1))
                    if not (isinstance(e, int) and e >= EARLY):
                        a.wait_ge(expert_scales, 2 * e)
                    settle(a)
                    a.activation(w1_part(e, 0), staged(e, 0), ACT.Square, accum_out=essq[:, 0:1]).then_inc(expert_squares, 1)
                    settle(a)
                    a.activation(bsq[:, :], b1T[:, bass.ds(e * NH, NH)], ACT.Square, accum_out=essq[:, 1:2]).then_inc(expert_squares, 1)
                    a.wait_ge(expert_squares, 3 * e + 2)
                else:
                    a.wait_ge(w2_in, 16 * (e + 1))
                    settle(a)
                    a.activation(w2_part(e, 0), staged(e, 1), ACT.Square, accum_out=essq[:, 2:3]).then_inc(expert_squares, 1)
                    a.wait_ge(expert_squares, 3 * e + 3)

            def e_scales(e, which):
                lo, hi = ((0, 2), (2, 3))[which]
                a.wait_ge(expert_steps, EV * e + (EV1A, EV2A)[which])
                settle(a)
                a.activation(escl[:, lo:hi], ebnd[:, lo:hi], ACT.Sqrt, scale=TOP * TOP).then_inc(expert_roots, 1)

            def e_high(e, which):
                a.wait_ge(expert_scales, 2 * e + which + 1)
                src, part = ((staged(e, 0), w1_part(e, 0)), (staged(e, 1), w2_part(e, 0)))[which]
                settle(a)
                a.activation(part, src, ACT.Copy, scale=escl[:, 2 * which:2 * which + 1]).then_inc(w_high, 1)

            def norms(b):
                a.wait_ge(norms_ps, b + 1)
                settle(a)
                a.activation(kn[:, :], SUMS_PS[:, 0:4], ACT.Sqrt).then_inc(norms_ready, 1)

            def counts_out(b):
                a.wait_ge(counts_ps, b + 1)
                a.wait_ge(placed, PLACES * b)
                settle(a)
                a.activation(counts, SUMS_PS[:, 8:8 + (T + 1) * E], ACT.Copy).then_inc(counts_ready, 1)

            def second_weight(b):
                a.wait_ge(gap_ready, b + 1)
                a.wait_ge(placed, PLACES * b)
                settle(a)
                a.preload_act_table(ACT.Exp)
                a.activation(second, gap, ACT.Exp).then_inc(second_ready, 1)
                a.preload_act_table(ACT.Sqrt)

            def row_out(b, cols, need, n, k):
                a.wait_ge(need, b + 1)
                for m, c in n:
                    a.wait_ge(m, past(c))
                settle(a)
                a.activation(colrow, ROWS_PS[:, cols:cols + D], ACT.Copy).then_inc(row_out_ready, 1)

            def turned(b, dst, bank, t_name, name, extra):
                a.wait_ge(t_name, 2 * b + 1)
                for n, v in extra:
                    a.wait_ge(n, past(v))
                settle(a)
                a.activation(dst, bank[:, :].bitcast(F16), ACT.Copy).then_inc(name, 1)

            def g_high(b):
                a.wait_ge(cosines_ready, NF * (b + 1))
                a.wait_ge(mix_ps, b)
                settle(a)
                a.activation(ghl[:, 0, :, :], gk, ACT.Copy).then_inc(cosines_high, 1)

            def x_high(b):
                a.wait_ge(xs_ready, T * (b + 1))
                a.wait_ge(x_turned, 2 * b)
                settle(a)
                a.activation(xhl[:, :, 0, :], xs, ACT.Copy).then_inc(x_high_ready, 1)

            def q_high(b, t):
                a.wait_ge(qk_out, T * b + t + 1)
                a.wait_ge(norms_ps, b)
                settle(a)
                a.activation(qkh[:, t, :], q32[:, t % 2, :], ACT.Copy).then_inc(qk_high, 1)
                if t:
                    a.wait_ge(squares_added, past((T - 1) * b + t - 1))
                settle(a)
                a.activation(sqt if t else sqa, q32[:, t % 2, :], ACT.Square).then_inc(qk_squares, 1)

            def m_high(b):
                a.wait_ge(mix_ps, b + 1)
                a.wait_ge(mix_low, b)
                for i in range(NF):
                    settle(a)
                    a.activation(m32[:, i, :], MIX_PS[:, i * D:(i + 1) * D], ACT.Identity, bias=vsum[:, i:i + 1], scale=der[:, 1:2]).then_inc(mix_out, 1)
                a.wait_ge(mix_out, 2 * (b + 1))
                a.wait_ge(z_ps, 2 * b)
                settle(a)
                a.activation(mhl[:, 0, :, :], m32, ACT.Copy).then_inc(mix_high, 1)

            def xf_high(b):
                a.wait_ge(xf_ready, T * (b + 1))
                a.wait_ge(xf_turned, 2 * b)
                a.wait_ge(xf_stored, 16 * b)
                settle(a)
                a.activation(xfhl[:, :, 0, :], z, ACT.Copy).then_inc(xf_high_ready, 1)

            def step(s):
                entering, mixing, leaving, e, placing = parts(s)
                if isinstance(s, int) and s == 2:
                    a.wait_ge(table_init, 16)
                if mixing is not None:
                    row_out(mixing, 0, q_row_ps, [(z_scaled, 2 * mixing)], 1)
                if entering is not None:
                    spread(0, enter_dev, (enter_mean, T * (entering + 1)), 0, 1.0 / SX / SX)
                if mixing is not None:
                    g_high(mixing)
                if entering is not None:
                    x_high(entering)
                if leaving is not None:
                    turned(leaving, xfT[:, 0, :, :].rearrange("p k c -> p (k c)"), TURN_PS[0], xf_turned, xfT_ready, [(shared_ps, T * leaving)])
                if e is not None:
                    e_squares(e, 0)
                if mixing is not None:
                    m_high(mixing)
                if entering is not None:
                    turned(entering, xTf(entering, 0), QK_PS[0], x_turned, xT_ready, [(z_ps, 2 * (entering - 1))])
                if mixing is not None:
                    row_out(mixing, D, tailor_row_ps, [(cosines_ready, NF * (mixing + 1))], 2)
                if e is not None:
                    e_scales(e, 0)
                if entering is not None:
                    q_high(entering, 0)
                if e is not None:
                    e_high(e, 0)
                if entering is not None:
                    for t in range(1, T):
                        q_high(entering, t)
                if leaving is not None:
                    second_weight(leaving)
                if mixing is not None:
                    spread(1, z_dev, (z_mean, T * (mixing + 1)), 1, 1.0)
                if e is not None:
                    e_squares(e, 1)
                if entering is not None:
                    norms(entering)
                if leaving is not None:
                    counts_out(leaving)
                if e is not None:
                    e_scales(e, 1)
                if mixing is not None:
                    spread(2, x1_dev, (x1_mean, T * (mixing + 1)), 0, 1.0 / SX / SX)
                if e is not None:
                    e_high(e, 1)
                if mixing is not None:
                    xf_high(mixing)
            run_steps(a, step)
            for e, which in late_pieces:
                a.wait_ge(expert_sums, past(2 * e - 1 + which))
                e_squares(e, which)
                e_scales(e, which)
                e_high(e, which)
            scalar_rest(a)

        @block.vector
        def _(v):
            link = chain(v, setup_steps, 0)
            v.wait_ge(setup_squares, 6)
            v.wait_ge(setup_sums, 1)
            tot = ROWS_PS
            link(v.tensor_copy(bnd[:, 0:1], tot[:, 0:1]))
            link(v.scalar_tensor_tensor(bnd[:, 1:2], tot[:, 0:1], float(D), ssq[:, 5:6], ALU.mult, ALU.add))
            link(v.tensor_scalar(bnd[:, 1:2], bnd[:, 1:2], 2.0, None, ALU.mult))
            link(v.tensor_copy(bnd[:, 2:3], tot[:, 1:2]))
            link(v.tensor_copy(bnd[:, 3:4], tot[:, 1:2]))
            link(v.scalar_tensor_tensor(bnd[:, 3:4], tot[:, 4:5], 1.0, bnd[:, 3:4], ALU.mult, ALU.add))
            link(v.tensor_scalar(bnd[:, 3:4], bnd[:, 3:4], 8.0 * D, None, ALU.mult))
            link(v.tensor_copy(bnd[:, 4:6], tot[:, 2:4]))
            link(v.tensor_scalar(bnd[:, 0:6], bnd[:, 0:6], 1e-24, None, ALU.max))
            link(v.reciprocal(bnd[:, 0:6], bnd[:, 0:6]))
            v.wait_ge(setup_roots, 1)
            link(v.tensor_scalar(scl[:, 0:6].bitcast(I32), scl[:, 0:6].bitcast(I32), EXP_MASK, None, ALU.bitwise_and))
            link(v.tensor_scalar(inv[:, 0:6].bitcast(I32), scl[:, 0:6].bitcast(I32), -1.0, EXP_FLIP, ALU.mult, ALU.add))
            link(v.scalar_tensor_tensor(der[:, 0:1], scl[:, 1:2], 1.0 / SX, inv[:, 0:1], ALU.mult, ALU.mult))
            link(v.scalar_tensor_tensor(der[:, 1:2], scl[:, 3:4], 1.0 / SG, inv[:, 2:3], ALU.mult, ALU.mult))
            v.wait_ge(bv_in, 32)
            link(v.tensor_tensor(der[:, 2:3], gam_b[:, :], inv[:, 3:4], ALU.mult))
            link(v.tensor_scalar(der[:, 3:5], inv[:, 4:6], 1.0 / SX, None, ALU.mult))
            link(v.tensor_scalar(der[:, 5:6], scl[:, 3:4], 1.0 / SG, None, ALU.mult))
            link(v.tensor_copy(der[:, 7:8], tot[:, 8:9]))
            link(v.scalar_tensor_tensor(der[:, 6:7], tot[:, 9:10], 1.0, der[:, 7:8], ALU.mult, ALU.add))
            link(v.tensor_tensor(der[:, 6:7], der[:, 6:7], scl[:, 3:4], ALU.mult))
            v.wait_ge(wv_sums_ps, 1)
            link(v.tensor_scalar(vsum, SUMS_PS[:, 0:NF], scl[:, 3:4], None, ALU.mult))
            link(v.tensor_scalar(bqk, bqk, scl[:, 1:2], None, ALU.mult))
            link(v.tensor_copy(bvb, bvc[:, :].unsqueeze(2).broadcast_to([P, NF, P])))
            assert link.count[0] == SETUP_V
            for i in range(NF):
                v.wait_ge(wqk_high, i + 1)
                v.scalar_tensor_tensor(wqkT[:, i, 1, :], TURN_PS[i][:, :], scl[:, 0:1], wqkT[:, i, 0, :], ALU.mult, ALU.subtract).then_inc(wqk_low, 1)
            v.wait_ge(wv_high, 1)
            v.scalar_tensor_tensor(wvs[:, :, 1, :], wv_n, scl[:, 2:3], wvs[:, :, 0, :], ALU.mult, ALU.subtract).then_inc(wv_low, 1)
            v.wait_ge(shared_high, 2)
            v.scalar_tensor_tensor(sgs[:, :, 1, 0:D], sh_n, scl[:, 4:5], sgs[:, :, 0, 0:D], ALU.mult, ALU.subtract).then_inc(shared_low, 1)
            v.scalar_tensor_tensor(sgs[:, :, 1, D:D + E], gate_n, scl[:, 5:6], sgs[:, :, 0, D:D + E], ALU.mult, ALU.subtract).then_inc(shared_low, 1)
            v.wait_ge(row_biases_in, 64)

            def bank_tiles(bank):
                return bank[:, :].rearrange("p (t d) -> p t d", d=D)

            def stats(which, b, src, src_ready, st_name, mv_name):
                for t in range(T):
                    for n, c in src_ready(t):
                        v.wait_ge(n, past(c))
                    settle(v)
                    v.bn_stats(st[:, which, t, :], src(t)).then_inc(st_name, 1)
                for t in range(T):
                    v.wait_ge(st_name, T * b + t + 1)
                    settle(v)
                    v.bn_aggr(mv[:, which, t, :], st[:, which, t, :]).then_inc(mv_name, 1)

            def enter_stats(b):
                stats(0, b, lambda t: Xt(b, t), lambda t: [(x_loaded, 16 * (b + 1))], enter_stats_t, enter_mean)

            def enter(b):
                v.wait_ge(enter_dev, b + 1)
                v.reciprocal(a1[:, bass.ds(b * T, T)], sd[:, 0, :]).then_inc(enter_factor, 1)
                v.wait_ge(enter_factor, b + 1)
                v.scalar_tensor_tensor(cf[:, 0, :], mv[:, 0, :, 0], -1.0, a1[:, bass.ds(b * T, T)], ALU.mult, ALU.mult).then_inc(enter_shift, 1)
                v.wait_ge(enter_shift, b + 1)
                v.wait_ge(x_high_ready, b)
                v.wait_ge(x_low_ready, b)
                for t in range(T):
                    v.tensor_scalar(xs[:, t, :], Xt(b, t), a1[:, bass.ds(b * T + t, 1)], cf[:, 0, t:t + 1], ALU.mult, ALU.add).then_inc(xs_ready, 1)

            def turned(b, dst, bank, t_name, name, extra):
                v.wait_ge(t_name, 2 * b + 2)
                for n, c in extra:
                    v.wait_ge(n, past(c))
                v.tensor_copy(dst, bank[:, :].bitcast(F16)).then_inc(name, 1)

            def norms(b):
                v.wait_ge(norms_ready, b + 1)
                v.reciprocal(rk[:, :], kn[:, :]).then_inc(norm_inverses, 1)
                v.wait_ge(norm_inverses, b + 1)
                v.tensor_scalar(dn[:, 2:4], rk[:, 0:2], SG, None, ALU.mult).then_inc(q_inverses, 1)
                v.wait_ge(q_inverses, b + 1)
                for c in range(NF):
                    v.tensor_scalar(dgq[:, c, :], ident32, dn[:, 2 + c:3 + c], None, ALU.mult).then_inc(q_diagonal, 1)

            def cosines(b):
                v.wait_ge(row_out_ready, 2 * b + 1)
                for l in range(NF):
                    v.scalar_tensor_tensor(gk[:, l, :], (SCORE_PS[:, 0:D], ROWS_PS[:, D:2 * D])[l], rk[:, 2 + l:3 + l], colrow, ALU.mult, ALU.mult).then_inc(cosines_ready, 1)

            def cosines_low(b):
                v.wait_ge(cosines_high, b + 1)
                v.wait_ge(cosines_ready, NF * (b + 1))
                v.tensor_tensor(ghl[:, 1, :, :], gk, ghl[:, 0, :, :], ALU.subtract).then_inc(cosines_low_ready, 1)

            def tailor(b):
                link = chain(v, tailor_steps, TAILOR * b)
                v.wait_ge(cosine_sums_ps, b + 1)
                link(v.scalar_tensor_tensor(dn[:, 0:2], SUMS_PS[:, 4:6], EPS_TAILOR, rk[:, 0:2], ALU.mult, ALU.mult))
                link(v.scalar_tensor_tensor(dn[:, 0:2], SUMS_PS[:, 6:8], 1.0 / SG, dn[:, 0:2], ALU.mult, ALU.add))
                link(v.tensor_scalar(dn[:, 0:2], dn[:, 0:2], float(D), None, ALU.add))
                link(v.reciprocal(dn[:, 0:2], dn[:, 0:2]))
                link(v.tensor_scalar(dn[:, 0:2], dn[:, 0:2], der[:, 2:3], None, ALU.mult))
                for c in range(NF):
                    v.tensor_scalar(dgt[:, c, :], ident32, dn[:, c:c + 1], None, ALU.mult).then_inc(tailor_diagonal, 1)
                link(v.tensor_scalar(r32, SUMS_PS[0:1, D:2 * D], der[0:1, 5:6], der[0:1, 6:7], ALU.mult, ALU.add))
                assert link.count[0] == TAILOR
                v.wait_ge(z_ps, 2 * b)
                v.tensor_copy(rhl[:, 0, :], r32).then_inc(bv_row_high, 1)
                v.wait_ge(bv_row_high, b + 1)
                v.tensor_tensor(rhl[:, 1, :], r32, rhl[:, 0, :], ALU.subtract).then_inc(bv_row_low, 1)

            def q_out(b, t):
                v.wait_ge(qk_ps, T * b + t + 1)
                v.wait_ge(qk_low, past(T * b + t - 1))
                v.wait_ge(qk_squares, past(T * b + t - 1))
                v.scalar_tensor_tensor(q32[:, t % 2, :], QK_PS[t % 2][:, :], der[:, 0:1], bqk, ALU.mult, ALU.add).then_inc(qk_out, 1)

            def m_low(b):
                v.wait_ge(mix_high, b + 1)
                v.wait_ge(z_ps, 2 * b)
                v.tensor_tensor(mhl[:, 1, :, :], m32, mhl[:, 0, :, :], ALU.subtract).then_inc(mix_low, 1)

            def attended(b):
                v.wait_ge(xf_high_ready, b)
                v.wait_ge(xf_low_ready, b)
                v.wait_ge(row_out_ready, 2 * b + 2)
                for h in range(2):
                    v.wait_ge(z_ps, 2 * b + h + 1)
                    v.tensor_tensor(z[:, 2 * h:2 * h + 2, :], bank_tiles((SCORE_PS, MIX_PS)[h]), colrow.unsqueeze(1).broadcast_to([P, 2, D]),
                                    ALU.mult).then_inc(z_scaled, 1)
                for t in range(T):
                    v.wait_ge(z_scaled, 2 * b + t // 2 + 1)
                    v.scalar_tensor_tensor(z[:, t, :], Xt(b, t), a1[:, bass.ds(b * T + t, 1)], z[:, t, :], ALU.mult, ALU.add).then_inc(z_ready, 1)
                stats(1, b, lambda t: z[:, t, :], lambda t: [(z_ready, T * b + t + 1)], z_stats_t, z_mean)

            def residual(b):
                v.wait_ge(z_dev, b + 1)
                v.reciprocal(cf[:, 1, :], sd[:, 1, :]).then_inc(z_factor, 1)
                v.wait_ge(z_factor, b + 1)
                v.scalar_tensor_tensor(c2[:, bass.ds(b * T, T)], mv[:, 1, :, 0], -1.0, cf[:, 1, :], ALU.mult, ALU.mult).then_inc(z_shift, 1)
                for t in range(T):
                    v.scalar_tensor_tensor(Xt(b, t), z[:, t, :], cf[:, 1, t:t + 1], Xt(b, t), ALU.mult, ALU.add).then_inc(x1_ready, 1)
                stats(2, b, lambda t: Xt(b, t), lambda t: [(x1_ready, T * b + t + 1)], x1_stats_t, x1_mean)

            def leave(b):
                v.wait_ge(x1_dev, b + 1)
                v.reciprocal(cf[:, 2, :], sd[:, 2, :]).then_inc(x1_factor, 1)
                v.wait_ge(x1_factor, b + 1)
                v.scalar_tensor_tensor(c3[:, :], mv[:, 2, :, 0], -1.0, cf[:, 2, :], ALU.mult, ALU.mult).then_inc(x1_shift, 1)
                v.wait_ge(x1_shift, b + 1)
                for t in range(T):
                    v.tensor_scalar(z[:, t, :], Xt(b, t), cf[:, 2, t:t + 1], c3[:, t:t + 1], ALU.mult, ALU.add).then_inc(xf_ready, 1)

            def wide(x):
                return x.unsqueeze(2).broadcast_to([P, T, E])

            def pick_experts(b, between):
                v.wait_ge(logits_ready, T * (b + 1))
                v.wait_ge(routing_consts, 7)
                v.wait_ge(counts_ps, b)
                v.wait_ge(placed, PLACES * b)
                link = chain(v, picked, PICKS * b)
                for k in range(2):
                    if k and between:
                        between()
                    link(v.tensor_reduce(best[k], logit, AX.X, ALU.max))
                    link(v.tensor_tensor(match, logit, wide(best[k]), ALU.is_equal))
                    link(v.tensor_tensor(match, match, below, ALU.mult))
                    link(v.tensor_reduce(red, match, AX.X, ALU.min))
                    link(v.tensor_tensor(pick[k], match, wide(red), ALU.is_equal))
                    if k == 0:
                        link(v.scalar_tensor_tensor(logit, pick[0], -3e38, logit, ALU.mult, ALU.add))
                assert link.count[0] == PICKS
                v.tensor_tensor(both, pick[0], pick[1], ALU.add).then_inc(both_ready, 1)
                v.tensor_tensor(gap, best[1], best[0], ALU.subtract).then_inc(gap_ready, 1)

            def shares(b):
                v.wait_ge(second_ready, b + 1)
                v.wait_ge(placed, PLACES * b)
                v.tensor_scalar(total, second, 1.0, None, ALU.add).then_inc(total_ready, 1)
                v.wait_ge(total_ready, b + 1)
                v.reciprocal(share, total).then_inc(share_ready, 1)

            def shared_out(b, tiles):
                for t in tiles:
                    v.wait_ge(shared_ps, T * b + t + 1)
                    v.wait_ge(u_stored[t % 2], 16 * (2 * b + t // 2))
                    v.scalar_tensor_tensor(u[:, t % 2, :], TURN_PS[t % 2][:, 0:D], der[:, 3:4], sbb[:, :], ALU.mult, ALU.add).then_inc(u_ready, 1)
                    v.tensor_scalar(logit[:, t, :], TURN_PS[t % 2][:, D:D + E], der[:, 4:5], None,
                                    ALU.mult).then_inc(logits_ready, 1)

            def e_bounds(e, which):
                link = chain(v, expert_steps, EV * e + (0, EV1A)[which])
                v.wait_ge(expert_sums, 2 * e + which + 1)
                if which == 0:
                    link(v.scalar_tensor_tensor(ebnd[:, 1:2], etot[:, 0:1], float(D), etot[:, 1:2], ALU.mult, ALU.add))
                    link(v.tensor_scalar(ebnd[:, 0:1], etot[:, 0:1], 1e-24, None, ALU.max))
                    link(v.tensor_scalar(ebnd[:, 1:2], ebnd[:, 1:2], 2.0, 1e-24, ALU.mult, ALU.max))
                    link(v.reciprocal(ebnd[:, 0:2], ebnd[:, 0:2]))
                else:
                    link = chain(v, expert_steps, EV * e + EV1)
                    link(v.tensor_scalar(ebnd[:, 2:3], etot[:, 2:3], 1e-24, None, ALU.max))
                    link(v.reciprocal(ebnd[:, 2:3], ebnd[:, 2:3]))

            def e_tables(e, which):
                lo, hi = ((0, 2), (2, 3))[which]
                v.wait_ge(expert_roots, 2 * e + which + 1)
                v.tensor_scalar(escl[:, lo:hi].bitcast(I32), escl[:, lo:hi].bitcast(I32), EXP_MASK, None, ALU.bitwise_and).then_inc(expert_scales, 1)
                v.wait_ge(expert_scales, 2 * e + which + 1)
                link = chain(v, expert_steps, EV * e + (EV1A, EV2A)[which])
                link(v.tensor_scalar(einv[:, lo:hi].bitcast(I32), escl[:, lo:hi].bitcast(I32), -1.0, EXP_FLIP, ALU.mult, ALU.add))
                if which == 0:
                    link(v.tensor_scalar(tab[:, 0, bass.ds(e, 1)], einv[:, 0:1], 1.0 / SX, None, ALU.mult))
                    link(v.tensor_copy(tab[:, 1, bass.ds(e, 1)], escl[:, 1:2]))
                else:
                    link(v.tensor_tensor(tab[:, 2, bass.ds(e, 1)], einv[:, 2:3], einv[:, 1:2], ALU.mult))

            def e_low(e, which):
                v.wait_ge(w_high, 2 * e + which + 1)
                if which == 0:
                    v.scalar_tensor_tensor(w1_part(e, 1), staged(e, 0), escl[:, 0:1], w1_part(e, 0), ALU.mult, ALU.subtract).then_inc(w_low, 1)
                else:
                    v.scalar_tensor_tensor(w2_part(e, 1), staged(e, 1), escl[:, 2:3], w2_part(e, 0), ALU.mult, ALU.subtract).then_inc(w_low, 1)

            def release():
                v.wait_ge(shared_ps, T * B)
                v.wait_ge(z_ps, 2 * B)
                v.wait_ge(xf_high_ready, B)
                v.wait_ge(xf_low_ready, B)
                v.wait_ge(xf_stored, 16 * B)
                v.wait_ge(u_stored[0], 16 * B * T // 2)
                v.wait_ge(u_stored[1], 16 * B * T // 2)
                v.wait_ge(logits_ready, T * B)
                v.memset(zone[:, 0:8], 0.0).then_inc(attention_left, 1)

            def step(s):
                entering, mixing, leaving, e, placing = parts(s)
                if entering is not None:
                    enter_stats(entering)
                if mixing is not None:
                    cosines(mixing)
                if entering is not None:
                    enter(entering)
                if leaving is not None:
                    turned(leaving, xfT[:, 1, :, :].rearrange("p k c -> p (k c)"), TURN_PS[1], xf_turned, xfT_ready, [(shared_ps, T * leaving)])
                if mixing is not None:
                    cosines_low(mixing)
                    tailor(mixing)
                if leaving is not None:
                    shared_out(leaving, range(0, 2))
                if mixing is not None:
                    m_low(mixing)
                if entering is not None:
                    turned(entering, xTf(entering, 1), QK_PS[1], x_turned, xT_ready, [(z_ps, 2 * (entering - 1))])
                if e is not None:
                    e_bounds(e, 0)
                    e_tables(e, 0)
                if entering is not None:
                    q_out(entering, 0)
                    q_out(entering, 1)
                if leaving is not None:
                    shared_out(leaving, range(2, T))
                if entering is not None:
                    q_out(entering, 2)
                if leaving is not None:
                    pick_experts(leaving, (lambda: q_out(entering, 3)) if entering is not None else None)
                elif entering is not None:
                    q_out(entering, 3)
                if e is not None:
                    e_low(e, 0)
                if mixing is not None:
                    attended(mixing)
                if isinstance(s, int) and s == B + 1:
                    release()
                if leaving is not None:
                    shares(leaving)
                if mixing is not None:
                    residual(mixing)
                if e is not None:
                    e_bounds(e, 1)
                if entering is not None:
                    norms(entering)
                if e is not None:
                    e_tables(e, 1)
                if mixing is not None:
                    leave(mixing)
                if e is not None:
                    e_low(e, 1)
            run_steps(v, step)

            def late_bounds(e, which):
                lo, hi = ((0, 2), (2, 3))[which]
                v.wait_ge(expert_sums_ps, past(2 * (e - EARLY) + which + 1))
                v.tensor_copy(etot[:, lo:hi], MIX_PS[:, lo:hi]).then_inc(expert_sums, 1)
                e_bounds(e, which)
            for i, (e, which) in enumerate(late_pieces):
                late_bounds(e, which)
                e_tables(e, which)
                e_low(e, which)
                if i == 3:
                    vector_blocks(v)
            vector_rest(v)


_OUT = ((8, 512, 256), "float32")
_INS = ["L0_attn_x", "L0_attn_Wq", "L0_attn_bq", "L0_attn_Wk", "L0_attn_bk", "L0_attn_Wv", "L0_attn_bv", "L0_attn_gamma",
        "L0_ffn_W1", "L0_ffn_b1", "L0_ffn_W2", "L0_ffn_b2", "L0_ffn_gate_W", "L0_ffn_shared_W", "L0_ffn_shared_b",
        "L0_ffn_gamma", "L0_ffn_beta"]


def kernel(**inputs):
    import numpy as _np
    import concourse.bacc as _bacc
    from concourse import mybir as _mybir
    from concourse.bass_utils import run_bass_kernel_spmd as _run

    nc = _bacc.Bacc("TRN2", target_bir_lowering=False, num_devices=1)
    arrays, args = {}, []
    for name in _INS:
        a = _np.ascontiguousarray(inputs[name])
        arrays[f"in_{name}"] = a
        args.append(nc.dram_tensor(f"in_{name}", a.shape, _mybir.dt.from_np(a.dtype), kind="ExternalInput").ap())
    args.append(nc.dram_tensor("out_0", _OUT[0], _mybir.dt.from_np(_np.dtype(_OUT[1])), kind="ExternalOutput").ap())
    sandwich(nc, *args)
    r = _run(nc, [arrays], core_ids=[0])
    return r.results[0]["out_0"]
```
